# Optimizing a Trainium2 kernel written in Bass

```python
import numpy as np
import jax
import jax.numpy as jnp

def _softmax(x, axis=-1):
    return jax.nn.softmax(x, axis=axis)

def _gelu(x):
    return jax.nn.gelu(x, approximate=True)

def _silu(x):
    return jax.nn.silu(x)

def _sigmoid(x):
    return jax.nn.sigmoid(x)

def _layernorm(x, axis=-1, eps=1e-05):
    m = jnp.mean(x, axis=axis, keepdims=True)
    v = jnp.var(x, axis=axis, keepdims=True)
    return (x - m) / jnp.sqrt(v + eps)

def _scatter_add(tgt, idx, src, axis=0):
    return tgt.at[idx].add(src)

def _segment_sum(src, seg, n):
    return jax.ops.segment_sum(src, seg, n)
kernel_name = 'mk_audio_tower_d2_tok_audfeat512_r4_ba6bd4'

def setup_inputs(seed: int=0):
    np.random.seed(seed)
    _w = jnp.asarray

    def _rec_inputs():
        import jax
        import jax.numpy as jnp
        _rk = jax.random.key(seed)
        x = -0.000125008 + 0.999885 * jax.random.normal(jax.random.fold_in(_rk, 1), (16, 375, 128), jnp.float32)
        return x
    x = _rec_inputs()

    def _L0_tok_setup():
        import jax, jax.numpy as jnp
        import numpy as np
        KERNEL_SIZE = 5
        DILATION = 1

        def _tdnn(hidden_states, W, b):
            B, T, C = hidden_states.shape
            T_out = T - (KERNEL_SIZE - 1) * DILATION
            frames = [hidden_states[:, i * DILATION:i * DILATION + T_out, :] for i in range(KERNEL_SIZE)]
            windows = jnp.concatenate(frames, axis=-1)
            out = jnp.einsum('btk,ok->bto', windows, W) + b
            return jax.nn.relu(out)
        key = jax.random.key(seed)
        k1, k2, k3 = jax.random.split(key, 3)
        B, T, C, O = (16, 1024, 128, 128)
        hidden_states = jax.random.normal(k1, (B, T, C), dtype=jnp.float32)
        fan_in = C * KERNEL_SIZE
        W = jax.random.normal(k2, (O, fan_in), dtype=jnp.float32) / np.sqrt(fan_in)
        b = jax.random.normal(k3, (O,), dtype=jnp.float32) * 0.01
        return {'hidden_states': hidden_states, 'W': W, 'b': b}
    _L0_tok_all = _L0_tok_setup()
    _L0_tok_in = {k: v for k, v in _L0_tok_all.items() if k in ('W', 'b')}
    del _L0_tok_all

    def _L0_attn_setup():
        import jax, jax.numpy as jnp
        import numpy as np
        DIM = 128
        HEADS = 8
        DIM_HEAD = 64
        INNER = HEADS * DIM_HEAD
        key = jax.random.key(seed)
        kx, kq, kk, kv, ko = jax.random.split(key, 5)
        x = jax.random.normal(kx, (2, 1024, DIM), dtype=jnp.float32)
        lim = float(np.sqrt(6.0 / (DIM + INNER)))
        Wq = jax.random.uniform(kq, (INNER, DIM), minval=-lim, maxval=lim, dtype=jnp.float32)
        Wk = jax.random.uniform(kk, (INNER, DIM), minval=-lim, maxval=lim, dtype=jnp.float32)
        Wv = jax.random.uniform(kv, (INNER, DIM), minval=-lim, maxval=lim, dtype=jnp.float32) * 0.67
        lim_o = float(np.sqrt(6.0 / (INNER + DIM)))
        Wo = jax.random.uniform(ko, (DIM, INNER), minval=-lim_o, maxval=lim_o, dtype=jnp.float32) * 0.67
        return {'x': x, 'Wq': Wq, 'Wk': Wk, 'Wv': Wv, 'Wo': Wo}
    _L0_attn_all = _L0_attn_setup()
    _L0_attn_in = {k: v for k, v in _L0_attn_all.items() if k in ('Wq', 'Wk', 'Wv', 'Wo')}
    del _L0_attn_all

    def _L0_ffn_setup():
        import jax, jax.numpy as jnp
        import numpy as np
        B, S, D, F, E = (4, 512, 128, 512, 8)
        key = jax.random.key(seed)
        k = jax.random.split(key, 5)
        x = jax.random.normal(k[0], (B, S, D), dtype=jnp.float32)
        Ws = jax.random.normal(k[1], (D, E), dtype=jnp.float32) * 0.02
        bs = jnp.zeros((E,), dtype=jnp.float32)
        W1 = jax.random.normal(k[2], (E, D, F), dtype=jnp.float32) * 0.02
        b1 = jnp.zeros((E, F), dtype=jnp.float32)
        W2 = jax.random.normal(k[3], (E, F, D), dtype=jnp.float32) * 0.02
        b2 = jnp.zeros((E, D), dtype=jnp.float32)
        return {'x': x, 'Ws': Ws, 'bs': bs, 'W1': W1, 'b1': b1, 'W2': W2, 'b2': b2}
    _L0_ffn_all = _L0_ffn_setup()
    _L0_ffn_in = {k: v for k, v in _L0_ffn_all.items() if k in ('Ws', 'bs', 'W1', 'b1', 'W2', 'b2')}
    del _L0_ffn_all

    def _L1_attn_setup():
        import jax, jax.numpy as jnp
        import numpy as np
        DIM = 128
        HEADS = 8
        HD = DIM // HEADS
        WIN = 64
        HALF = WIN // 2

        def _sliding_window_attn(q, k, v):
            B, H, S, Dh = q.shape
            scale = Dh ** (-0.5)
            pos = jnp.arange(S)
            offsets = list(range(-HALF, HALF + 1))
            scores = []
            for o in offsets:
                k_sh = jnp.roll(k, -o, axis=2)
                s = jnp.einsum('bhsd,bhsd->bhs', q, k_sh) * scale
                valid = (pos + o >= 0) & (pos + o < S)
                s = jnp.where(valid[None, None, :], s, -jnp.inf)
                scores.append(s)
            scores = jnp.stack(scores, axis=-1)
            p = jax.nn.softmax(scores, axis=-1)
            out = jnp.zeros_like(q)
            for idx, o in enumerate(offsets):
                out = out + p[..., idx:idx + 1] * jnp.roll(v, -o, axis=2)
            return out
        key = jax.random.key(seed)
        k0, k1, k2 = jax.random.split(key, 3)
        x = jax.random.normal(k0, (4, 1024, DIM), dtype=jnp.float32)
        W_qkv = jax.random.normal(k1, (DIM, 3 * DIM), dtype=jnp.float32) * 0.02
        b_qkv = jnp.zeros((3 * DIM,), dtype=jnp.float32)
        W_proj = jax.random.normal(k2, (DIM, DIM), dtype=jnp.float32) * 0.02
        b_proj = jnp.zeros((DIM,), dtype=jnp.float32)
        return {'x': x, 'W_qkv': W_qkv, 'b_qkv': b_qkv, 'W_proj': W_proj, 'b_proj': b_proj}
    _L1_attn_all = _L1_attn_setup()
    _L1_attn_in = {k: v for k, v in _L1_attn_all.items() if k in ('W_qkv', 'b_qkv', 'W_proj', 'b_proj')}
    del _L1_attn_all

    def _L1_ffn_setup():
        import jax, jax.numpy as jnp
        import numpy as np
        B, N, DIM = (1, 512, 128)
        DH, H = (64, 8)
        E, FF = (8, 512)

        def _layernorm(x, g, b, eps=1e-05):
            mu = jnp.mean(x, axis=-1, keepdims=True)
            var = jnp.mean(jnp.square(x - mu), axis=-1, keepdims=True)
            return (x - mu) * jax.lax.rsqrt(var + eps) * g + b

        def _l2norm(x, eps=1e-12):
            return x / jnp.sqrt(jnp.sum(jnp.square(x), axis=-1, keepdims=True) + eps)
        key = jax.random.key(seed)
        ks = jax.random.split(key, 12)
        g = lambda k, shape: jax.random.normal(k, shape, jnp.float32) * 0.02
        return {'x': jax.random.normal(ks[0], (B, N, DIM), jnp.float32), 'ln_g': jnp.ones((DIM,), jnp.float32), 'ln_b': jnp.zeros((DIM,), jnp.float32), 'Wq': g(ks[1], (DIM, DIM)), 'Wk': g(ks[2], (DIM, DIM)), 'Wv': g(ks[3], (DIM, DIM)), 'Wo': g(ks[4], (DIM, DIM)), 'qn_g': jnp.ones((DH,), jnp.float32), 'kn_g': jnp.ones((DH,), jnp.float32), 'gate_W': g(ks[5], (DIM, E)), 'gate_b': jnp.zeros((E,), jnp.float32), 'W1': g(ks[6], (E, DIM, FF)), 'b1': jnp.zeros((E, FF), jnp.float32), 'W2': g(ks[7], (E, FF, DIM)), 'b2': jnp.zeros((E, DIM), jnp.float32)}
    _L1_ffn_all = _L1_ffn_setup()
    _L1_ffn_in = {k: v for k, v in _L1_ffn_all.items() if k in ('ln_g', 'ln_b', 'Wq', 'Wk', 'Wv', 'Wo', 'qn_g', 'kn_g', 'gate_W', 'gate_b', 'W1', 'b1', 'W2', 'b2')}
    del _L1_ffn_all
    return {'x': x, 'L0_tok_W': _L0_tok_in['W'], 'L0_tok_b': _L0_tok_in['b'], 'L0_attn_Wq': _L0_attn_in['Wq'], 'L0_attn_Wk': _L0_attn_in['Wk'], 'L0_attn_Wv': _L0_attn_in['Wv'], 'L0_attn_Wo': _L0_attn_in['Wo'], 'L0_ffn_Ws': _L0_ffn_in['Ws'], 'L0_ffn_bs': _L0_ffn_in['bs'], 'L0_ffn_W1': _L0_ffn_in['W1'], 'L0_ffn_b1': _L0_ffn_in['b1'], 'L0_ffn_W2': _L0_ffn_in['W2'], 'L0_ffn_b2': _L0_ffn_in['b2'], 'L1_attn_W_qkv': _L1_attn_in['W_qkv'], 'L1_attn_b_qkv': _L1_attn_in['b_qkv'], 'L1_attn_W_proj': _L1_attn_in['W_proj'], 'L1_attn_b_proj': _L1_attn_in['b_proj'], 'L1_ffn_ln_g': _L1_ffn_in['ln_g'], 'L1_ffn_ln_b': _L1_ffn_in['ln_b'], 'L1_ffn_Wq': _L1_ffn_in['Wq'], 'L1_ffn_Wk': _L1_ffn_in['Wk'], 'L1_ffn_Wv': _L1_ffn_in['Wv'], 'L1_ffn_Wo': _L1_ffn_in['Wo'], 'L1_ffn_qn_g': _L1_ffn_in['qn_g'], 'L1_ffn_kn_g': _L1_ffn_in['kn_g'], 'L1_ffn_gate_W': _L1_ffn_in['gate_W'], 'L1_ffn_gate_b': _L1_ffn_in['gate_b'], 'L1_ffn_W1': _L1_ffn_in['W1'], 'L1_ffn_b1': _L1_ffn_in['b1'], 'L1_ffn_W2': _L1_ffn_in['W2'], 'L1_ffn_b2': _L1_ffn_in['b2']}

def reference(x, L0_tok_W, L0_tok_b, L0_attn_Wq, L0_attn_Wk, L0_attn_Wv, L0_attn_Wo, L0_ffn_Ws, L0_ffn_bs, L0_ffn_W1, L0_ffn_b1, L0_ffn_W2, L0_ffn_b2, L1_attn_W_qkv, L1_attn_b_qkv, L1_attn_W_proj, L1_attn_b_proj, L1_ffn_ln_g, L1_ffn_ln_b, L1_ffn_Wq, L1_ffn_Wk, L1_ffn_Wv, L1_ffn_Wo, L1_ffn_qn_g, L1_ffn_kn_g, L1_ffn_gate_W, L1_ffn_gate_b, L1_ffn_W1, L1_ffn_b1, L1_ffn_W2, L1_ffn_b2):
    import jax
    import jax.numpy as jnp

    def _L0_tok_ref(hidden_states, W, b):
        import jax, jax.numpy as jnp
        import numpy as np
        KERNEL_SIZE = 5
        DILATION = 1

        def _tdnn(hidden_states, W, b):
            B, T, C = hidden_states.shape
            T_out = T - (KERNEL_SIZE - 1) * DILATION
            frames = [hidden_states[:, i * DILATION:i * DILATION + T_out, :] for i in range(KERNEL_SIZE)]
            windows = jnp.concatenate(frames, axis=-1)
            out = jnp.einsum('btk,ok->bto', windows, W) + b
            return jax.nn.relu(out)
        return _tdnn(hidden_states, W, b)

    def _L0_attn_ref(x, Wq, Wk, Wv, Wo):
        import jax, jax.numpy as jnp
        import numpy as np
        DIM = 128
        HEADS = 8
        DIM_HEAD = 64
        INNER = HEADS * DIM_HEAD
        scale = DIM_HEAD ** (-0.5)
        b, n, _ = x.shape

        def proj(W):
            t = jnp.einsum('bnc,ec->bne', x, W)
            return t.reshape(b, n, HEADS, DIM_HEAD).transpose(0, 2, 1, 3)
        q, k, v = (proj(Wq), proj(Wk), proj(Wv))
        dots = jnp.einsum('bhqd,bhkd->bhqk', q, k) * scale
        attn = jax.nn.softmax(dots, axis=-1)
        out = jnp.einsum('bhqk,bhkd->bhqd', attn, v)
        out = out.transpose(0, 2, 1, 3).reshape(b, n, INNER)
        out = jnp.einsum('bne,ce->bnc', out, Wo)
        return out + x

    def _L0_ffn_ref(x, Ws, bs, W1, b1, W2, b2):
        import jax, jax.numpy as jnp
        import numpy as np
        B, S, D, F, E = (4, 512, 128, 512, 8)
        Bb, Ss, Dd = x.shape
        xt = x.reshape(-1, Dd)
        logits = xt @ Ws + bs
        probs = jax.nn.softmax(logits, axis=-1)
        prob_max = jnp.max(probs, axis=-1)
        routes = jnp.argmax(probs, axis=-1)
        onehot = jax.nn.one_hot(routes, W1.shape[0], dtype=xt.dtype)

        def expert_ffn(w1, bb1, w2, bb2):
            h = jax.nn.gelu(xt @ w1 + bb1, approximate=False)
            return h @ w2 + bb2
        y = jax.vmap(expert_ffn)(W1, b1, W2, b2)
        out = jnp.einsum('te,etd->td', onehot, y)
        out = out * prob_max[:, None]
        return out.reshape(Bb, Ss, Dd)

    def _L1_attn_ref(x, W_qkv, b_qkv, W_proj, b_proj):
        import jax, jax.numpy as jnp
        import numpy as np
        DIM = 128
        HEADS = 8
        HD = DIM // HEADS
        WIN = 64
        HALF = WIN // 2

        def _sliding_window_attn(q, k, v):
            B, H, S, Dh = q.shape
            scale = Dh ** (-0.5)
            pos = jnp.arange(S)
            offsets = list(range(-HALF, HALF + 1))
            scores = []
            for o in offsets:
                k_sh = jnp.roll(k, -o, axis=2)
                s = jnp.einsum('bhsd,bhsd->bhs', q, k_sh) * scale
                valid = (pos + o >= 0) & (pos + o < S)
                s = jnp.where(valid[None, None, :], s, -jnp.inf)
                scores.append(s)
            scores = jnp.stack(scores, axis=-1)
            p = jax.nn.softmax(scores, axis=-1)
            out = jnp.zeros_like(q)
            for idx, o in enumerate(offsets):
                out = out + p[..., idx:idx + 1] * jnp.roll(v, -o, axis=2)
            return out
        B, S, _ = x.shape
        qkv = (x @ W_qkv + b_qkv).reshape(B, S, 3, HEADS, HD)
        qkv = jnp.transpose(qkv, (2, 0, 3, 1, 4))
        q, k, v = (qkv[0], qkv[1], qkv[2])
        attn = _sliding_window_attn(q, k, v)
        attn = jnp.transpose(attn, (0, 2, 1, 3)).reshape(B, S, DIM)
        return attn @ W_proj + b_proj

    def _L1_ffn_ref(x, ln_g, ln_b, Wq, Wk, Wv, Wo, qn_g, kn_g, gate_W, gate_b, W1, b1, W2, b2):
        import jax, jax.numpy as jnp
        import numpy as np
        B, N, DIM = (1, 512, 128)
        DH, H = (64, 8)
        E, FF = (8, 512)

        def _layernorm(x, g, b, eps=1e-05):
            mu = jnp.mean(x, axis=-1, keepdims=True)
            var = jnp.mean(jnp.square(x - mu), axis=-1, keepdims=True)
            return (x - mu) * jax.lax.rsqrt(var + eps) * g + b

        def _l2norm(x, eps=1e-12):
            return x / jnp.sqrt(jnp.sum(jnp.square(x), axis=-1, keepdims=True) + eps)
        b, n, d = x.shape
        dh = qn_g.shape[0]
        h = d // dh
        hx = _layernorm(x, ln_g, ln_b)
        q = (hx @ Wq).reshape(b, n, h, dh).transpose(0, 2, 1, 3)
        k = (hx @ Wk).reshape(b, n, h, dh).transpose(0, 2, 1, 3)
        v = (hx @ Wv).reshape(b, n, h, dh).transpose(0, 2, 1, 3)
        scale = jnp.sqrt(jnp.float32(dh))
        q = _l2norm(q) * scale * qn_g
        k = _l2norm(k) * scale * kn_g
        scores = jnp.einsum('bhqd,bhkd->bhqk', q, k) * dh ** (-0.5)
        causal = jnp.tril(jnp.ones((n, n), bool))
        scores = jnp.where(causal, scores, jnp.finfo(scores.dtype).min)
        attn = jax.nn.softmax(scores, axis=-1)
        o = jnp.einsum('bhqk,bhkd->bhqd', attn, v)
        y = o.transpose(0, 2, 1, 3).reshape(b, n, d) @ Wo
        gate = jax.nn.softmax(y @ gate_W + gate_b, axis=-1)
        hid = jax.nn.gelu(jnp.einsum('bnd,edf->bnef', y, W1) + b1)
        eo = jnp.einsum('bnef,efd->bned', hid, W2) + b2
        out = jnp.einsum('bned,bne->bnd', eo, gate)
        return out
    h = _L0_tok_ref(x, L0_tok_W, L0_tok_b)
    h = h + _L0_attn_ref(_layernorm(h, axis=-1), L0_attn_Wq, L0_attn_Wk, L0_attn_Wv, L0_attn_Wo)
    h = h + _L0_ffn_ref(_layernorm(h, axis=-1), L0_ffn_Ws, L0_ffn_bs, L0_ffn_W1, L0_ffn_b1, L0_ffn_W2, L0_ffn_b2)
    h = h + _L1_attn_ref(_layernorm(h, axis=-1), L1_attn_W_qkv, L1_attn_b_qkv, L1_attn_W_proj, L1_attn_b_proj)
    h = h + _L1_ffn_ref(_layernorm(h, axis=-1), L1_ffn_ln_g, L1_ffn_ln_b, L1_ffn_Wq, L1_ffn_Wk, L1_ffn_Wv, L1_ffn_Wo, L1_ffn_qn_g, L1_ffn_kn_g, L1_ffn_gate_W, L1_ffn_gate_b, L1_ffn_W1, L1_ffn_b1, L1_ffn_W2, L1_ffn_b2)
    return h

_drawn_inputs = setup_inputs


def setup_inputs(seed=0):
    import zlib

    import numpy as np

    out = dict(_drawn_inputs(seed))
    spreads = {'L0_ffn_bs': (0.0, 0.8),
     'L0_ffn_b1': (0.0, 0.8),
     'L0_ffn_b2': (0.0, 0.795),
     'L1_attn_b_qkv': (0.0, 0.557),
     'L1_attn_b_proj': (0.0, 0.1),
     'L1_ffn_ln_g': (1.0, 0.6),
     'L1_ffn_ln_b': (0.0, 0.8),
     'L1_ffn_qn_g': (1.0, 0.6),
     'L1_ffn_kn_g': (1.0, 0.6),
     'L1_ffn_gate_b': (0.0, 0.8),
     'L1_ffn_b1': (0.0, 0.8),
     'L1_ffn_b2': (0.0, 1.199)}
    factors = {'L0_tok_b': 4.892,
     'L0_attn_Wq': 6.03,
     'L0_attn_Wk': 6.051,
     'L0_attn_Wv': 3.749,
     'L0_attn_Wo': 3.722,
     'L0_ffn_Ws': 5.116,
     'L0_ffn_W1': 8.0,
     'L0_ffn_W2': 8.0,
     'L1_attn_W_qkv': 8.0,
     'L1_attn_W_proj': 3.906,
     'L1_ffn_Wq': 8.0,
     'L1_ffn_Wk': 8.0,
     'L1_ffn_Wv': 8.0,
     'L1_ffn_Wo': 8.0,
     'L1_ffn_gate_W': 8.0,
     'L1_ffn_W1': 8.0,
     'L1_ffn_W2': 8.0}
    for name, (base, spread) in spreads.items():
        noise = np.random.default_rng([zlib.crc32(name.encode()), seed]).standard_normal(out[name].shape)
        drawn = base * np.exp(spread * noise) if base else spread * noise
        out[name] = jnp.asarray(drawn.astype(out[name].dtype))
    for name, factor in factors.items():
        out[name] = (out[name] * factor).astype(out[name].dtype)
    return out
```

```python
from contextlib import ExitStack

import numpy as np

import concourse.bass as bass
from concourse import mybir

F32 = mybir.dt.float32
BF16 = mybir.dt.bfloat16
ALU = mybir.AluOpType
ACT = mybir.ActivationFunctionType
AX = mybir.AxisListType.X

P = 128
B, T_IN, C = 16, 375, 128
TAPS = 5
T = T_IN - TAPS + 1
NT = -(-T // P)
TP = NT * P
LAST = T - (NT - 1) * P
H0, D0 = 8, 64
H1, D1, HALF = 8, 16, 32
H2, D2 = 2, 64
E, FF = 8, 512
FC = FF // P
WIN = P + 2 * HALF
KC = WIN // 2
G1 = 2
J1 = H1 // G1
MASKED = -1e30


def constants():
    q = np.arange(P)
    ident = np.eye(P, dtype=np.float32)
    band_q = np.full((P, NT, WIN), MASKED, np.float32)
    band_k = np.full((KC, NT, 2, P), MASKED, np.float32)
    for t in range(NT):
        key = P * t - HALF + np.arange(WIN)
        seen = (abs(key[None, :] - (P * t + q)[:, None]) <= HALF) & (key >= 0) & (key < T)
        band_q[:, t][seen] = 0
        for c in range(2):
            band_k[:, t, c][seen.T[KC * c:KC * (c + 1)]] = 0
    later_q = np.where(q[None, :] > q[:, None], MASKED, 0).astype(np.float32)
    sel0 = np.zeros((H0, H0, TP), np.float32)
    sel2 = np.zeros((H2, H2, TP), np.float32)
    for h in range(H0):
        sel0[h, h] = 1
    for h in range(H2):
        sel2[h, h] = 1
    rank = np.tile(np.arange(E, 0, -1, dtype=np.float32), (P, NT)).reshape(P, NT, E)
    return {"c_ident": ident, "c_band_q": band_q, "c_band_k": band_k, "c_later_q": later_q,
            "c_later_k": np.ascontiguousarray(later_q.T), "c_sel0": sel0, "c_sel2": sel2, "c_rank": rank}


def tower(nc, w, out):
    with ExitStack() as ctx:
        def sb(name, shape, dt=F32):
            return ctx.enter_context(nc.sbuf_tensor("s_" + name, shape, dt))

        sems = []

        def sem(name):
            s = ctx.enter_context(nc.semaphore(name))
            sems.append(s)
            return s

        load = ctx.enter_context(nc.semaphore("weights_loaded"))
        prep = ctx.enter_context(nc.semaphore("constants_ready"))
        bank = ctx.enter_context(nc.psum_tensor("bank", [P, 8, 512], F32))

        res = {}
        for name, ap in w.items():
            if name not in ("x", "c_sel0", "c_sel2"):
                res[name] = sb(name, list(ap.shape))
        ident = res["c_ident"]
        identb = sb("identb", [P, P], BF16)
        bandq = sb("bandq", [P, NT, WIN], BF16)
        bandk = sb("bandk", [KC, NT, 2, P], BF16)
        laterq = sb("laterq", [P, P], BF16)
        laterk = sb("laterk", [P, P], BF16)
        ones = sb("ones", [1, P])

        xT = sb("xT", [P, TP + TAPS - 1])
        h = sb("h", [P, NT, C])
        hn = sb("hn", [P, NT, C])
        hnT = sb("hnT", [P, HALF + TP + HALF])
        stats = sb("stats", [P, NT, 6])
        mv = sb("mv", [P, NT, 2])
        ve = sb("ve", [P, NT])
        lnv = sb("lnv", [P, 12])
        y0 = sb("y0", [P, 12])
        nt1 = sb("nt1", [P, 12])
        nt2 = sb("nt2", [P, 12])
        rstd = sb("rstd", [P, 12])
        QA = sb("QA", [D0 + H0, H0, TP])
        KA = sb("KA", [D0 + H0, H0, TP])
        VA = sb("VA", [P, NT, H0, D0 + 1])
        Mx = sb("Mx", [P, NT, H0])
        PT = sb("PT", [P, 2, NT, TP])
        rec = sb("rec", [P, 2, NT])
        shared = sb("shared", [P, 2 * J1 * 2 * G1 * P])
        O = shared[:, 0:NT * H0 * D0].rearrange("p (t a d) -> p t a d", t=NT, a=H0)
        OT = shared[:, NT * H0 * D0:NT * H0 * D0 + 4 * TP].rearrange("p (c n) -> p c n", c=4)
        lm = sb("lm", [P, NT, E])
        gm = sb("gm", [P, NT])
        ge = sb("ge", [P, NT, E])
        gs = sb("gs", [P, NT])
        gr = sb("gr", [P, NT])
        ga = sb("ga", [P, NT, E])
        gb = sb("gb", [P, NT])
        gate = sb("gate", [P, NT, E])
        gT = sb("gT", [E, TP])
        HT = sb("HT", [P, 2, FC, TP])
        qT = sb("qT", [P, G1, TP])
        qTa = sb("qTa", [P, G1, TP])
        kT = sb("kT", [P, G1, HALF + TP + HALF])
        V1 = sb("V1", [KC, 2 * NT, H1, D1 + 1])
        Mexp = sb("Mexp", [P, NT, G1, P])
        P1 = shared[0:KC, :].rearrange("p (b j n) -> p b j n", b=2, j=J1)
        rec1 = sb("rec1", [P, H1])
        O1 = sb("O1", [P, NT, H1, D1])
        O1T = sb("O1T", [P, TP])
        sq = shared[:, 0:NT * 2 * C].rearrange("p (t c) -> p t c", t=NT)
        ss = sb("ss", [P, NT * 4])
        qk = sb("qk", [P, NT, 4, D2])
        VF = sb("VF", [P, NT, H2, D2 + 1])
        QF = sb("QF", [D2 + H2, H2, TP])
        KF = sb("KF", [D2 + H2, H2, TP])
        Mf = sb("Mf", [P, NT, H2])
        PF = PT
        rec2 = sb("rec2", [P, H2 * NT])
        OF = sb("OF", [P, NT, H2, D2])
        OFT = sb("OFT", [P, TP])
        yT = sb("yT", [P, TP])

        names = """x_loaded tdnn_done h_ready var_ready rsqrt_guess hn_ready hnT_psum hnT_ready
            q_psum k_psum q_ready k_ready v_psum v_ready smax_psum max_done maxT_psum negmax_ready
            st_psum exp_done pv_done o_norm oT_psum oT_act oT_dve attn_psum
            logits_psum logits_shift gate_exp gate_ready gateT_psum gateT_ready b2_psum
            hid_psum hid_ready w2_done acc_done
            lq_psum lv_psum lq_ready lv_ready lmax_psum lmax_done lmaxT_psum qTa_ready lst_psum
            lexp_done lpv_done lnorm_done lo_psum lo_ready lproj_psum
            fqkv_psum fsq fv_ready fss_ready frs_guess fqkn_ready fqT_psum fq_ready fk_ready
            fmax_psum fmax_done fmaxT_psum fneg_ready fst_psum fexp_done fpv_done fo_ready
            foT_psum foT_ready y_psum y_ready vector_step scalar_step out_stored""".split()
        s = {n: sem(n) for n in names}

        n_loads = len(res) + 2
        with nc.Block() as block:
            @block.sync
            def _(sp):
                for name, tile in res.items():
                    sp.dma_start(tile[:], w[name]).then_inc(load, 16)
                sp.dma_start(KA[D0:, :, :], w["c_sel0"]).then_inc(load, 16)
                sp.dma_start(KF[D2:, :, :], w["c_sel2"]).then_inc(load, 16)

            @block.vector
            def _(dve):
                nc.vector.memset(ones[:], 1.0)
                nc.vector.memset(xT[:, T_IN:], 0.0)
                nc.vector.memset(hnT[:, 0:HALF], 0.0)
                nc.vector.memset(hnT[:, HALF + TP:], 0.0)
                nc.vector.memset(kT[:, :, 0:HALF], 0.0)
                nc.vector.memset(kT[:, :, HALF + TP:], 0.0)
                nc.vector.memset(Mexp[:], 0.0)
                nc.vector.memset(VA[:, :, :, D0:], 1.0)
                nc.vector.memset(V1[:, :, :, D1:], 1.0)
                nc.vector.memset(VF[:, :, :, D2:], 1.0)
                dve.wait_ge(load, 16 * n_loads)
                nc.vector.tensor_copy(identb[:], ident[:])
                nc.vector.tensor_copy(bandq[:], res["c_band_q"][:])
                nc.vector.tensor_copy(bandk[:], res["c_band_k"][:])
                nc.vector.tensor_copy(laterq[:], res["c_later_q"][:])
                nc.vector.tensor_copy(laterk[:], res["c_later_k"][:])
        nc.all_engine_barrier()

        def tile(t):
            return slice(P * t, P * (t + 1))

        with nc.Fori(0, B) as seq:
            with nc.Block() as block:
                @block.sync
                def _(sp):
                    sp.dma_start(xT[:, 0:T_IN], w["x"][seq]).then_inc(s["x_loaded"], 16)
                    sp.wait_ge(s["acc_done"], 2 * E)
                    for t in range(NT):
                        n = P if t < NT - 1 else LAST
                        sp.dma_start(out[seq, P * t:P * t + n, :], h[0:n, t, :]).then_inc(s["out_stored"], 16)
                    sp.wait_ge(s["out_stored"], 16 * NT)

                @block.tensor
                def _(pe):
                    mm, tr = nc.tensor.matmul, nc.tensor.transpose

                    def normed_T(k):
                        pe.wait_ge(s["hn_ready"], k + 1)
                        for t in range(NT):
                            i = tr(bank[:, 1, tile(t)], hn[:, t, :], ident[:])
                        i.then_inc(s["hnT_psum"], 1)

                    def experts(f, inT, pre):
                        W1, W2 = res[pre + "W1"], res[pre + "W2"]

                        def up(e):
                            for c in range(FC):
                                if e or f:
                                    pe.wait_ge(s["hid_ready"], (E * f + e - 1) * FC + c + 1)
                                mm(bank[:, 2 + c, 0:TP], W1[:, e, tile(c)], inT, start=True,
                                   stop=True).then_inc(s["hid_psum"], 1)

                        def down(e):
                            n = E * f + e
                            pe.wait_ge(s["hid_ready"], (n + 1) * FC)
                            if n >= 2:
                                pe.wait_ge(s["acc_done"], n - 1)
                            for t in range(NT):
                                for c in range(FC):
                                    i = mm(bank[:, 6 + e % 2, tile(t)], HT[:, e % 2, c, tile(t)], W2[:, e, c, :],
                                           start=c == 0, stop=c == FC - 1)
                            i.then_inc(s["w2_done"], 1)

                        for t in range(NT):
                            mm(bank[:, 0, E * t:E * t + E], inT[:, tile(t)], res[pre + "Wg"][:], start=True, stop=False)
                            i = mm(bank[:, 0, E * t:E * t + E], ones[:], res[pre + "bg"][:], start=False, stop=True)
                        i.then_inc(s["logits_psum"], 1)
                        up(0)
                        pe.wait_ge(s["gate_ready"], f + 1)
                        for t in range(NT):
                            i = tr(bank[0:E, 0, tile(t)], gate[:, t, :], ident[:])
                        i.then_inc(s["gateT_psum"], 1)
                        pe.wait_ge(s["gateT_ready"], f + 1)
                        for t in range(NT):
                            i = mm(bank[:, 1, tile(t)], gT[:, tile(t)], res[pre + "b2"][:], start=True, stop=True)
                        i.then_inc(s["b2_psum"], 1)
                        for e in range(E):
                            if e + 1 < E:
                                up(e + 1)
                            down(e)

                    pe.wait_ge(s["x_loaded"], 16)
                    for t in range(NT):
                        for i in range(TAPS):
                            mm(bank[:, 0, tile(t)], xT[:, P * t + i:P * t + i + P], res["tokW"][:, i, :],
                               start=i == 0, stop=False)
                        i = mm(bank[:, 0, tile(t)], ones[:], res["tokb"][:], start=False, stop=True)
                    i.then_inc(s["tdnn_done"], 1)

                    normed_T(0)
                    inT = hnT[:, HALF:HALF + TP]
                    pe.wait_ge(s["hnT_ready"], 1)
                    for p in range(H0 // 2):
                        mm(bank[:, p, 0:TP], res["Wq"][:, tile(p)], inT, start=True, stop=True).then_inc(s["q_psum"], 1)
                        mm(bank[:, 4 + p, 0:TP], res["Wk"][:, tile(p)], inT, start=True, stop=True)\
                            .then_inc(s["k_psum"], 1)
                    for t in range(NT):
                        pe.wait_ge(s["q_ready"], 2 * t + 2)
                        mm(bank[:, t, :], inT[:, tile(t)], res["Wv"][:], start=True, stop=True).then_inc(s["v_psum"], 1)
                    pe.wait_ge(s["q_ready"], H0)
                    pe.wait_ge(s["k_ready"], H0)
                    pe.wait_ge(s["v_ready"], NT)
                    for hd in range(H0):
                        if hd >= 2:
                            pe.wait_ge(s["max_done"], hd - 1)
                        for t in range(NT):
                            i = mm(bank[:, NT * (hd % 2) + t, 0:T], QA[0:D0, hd, tile(t)], KA[0:D0, hd, 0:T],
                                   start=True, stop=True)
                        i.then_inc(s["smax_psum"], 1)
                    pe.wait_ge(s["max_done"], H0)
                    for t in range(NT):
                        i = tr(bank[0:H0, 6, tile(t)], Mx[:, t, :], ident[:])
                    i.then_inc(s["maxT_psum"], 1)
                    pe.wait_ge(s["negmax_ready"], 1)

                    def scores_T(hd):
                        if hd >= 2:
                            pe.wait_ge(s["exp_done"], hd - 1)
                        for t in range(NT):
                            i = mm(bank[:, NT * (hd % 2) + t, 0:TP], KA[:, hd, tile(t)], QA[:, hd, :],
                                   start=True, stop=True)
                        i.then_inc(s["st_psum"], 1)

                    def values(hd):
                        pe.wait_ge(s["exp_done"], hd + 1)
                        pair = hd // 2
                        if pair >= 2 and hd % 2 == 0:
                            pe.wait_ge(s["o_norm"], pair - 1)
                        for t in range(NT):
                            at = (hd % 2 * NT + t) * (D0 + 1)
                            for k in range(NT):
                                n = P if k < NT - 1 else LAST
                                i = mm(bank[:, 6 + pair % 2, at:at + D0 + 1], PT[0:n, hd % 2, k, tile(t)],
                                       VA[0:n, k, hd, :], start=k == 0, stop=k == NT - 1)
                        i.then_inc(s["pv_done"], 1)

                    scores_T(0)
                    for hd in range(H0):
                        if hd + 1 < H0:
                            scores_T(hd + 1)
                        values(hd)
                    pe.wait_ge(s["o_norm"], H0 // 2)
                    for c in range(4):
                        for t in range(NT):
                            i = tr(bank[:, c, tile(t)], O[:, t, 2 * c:2 * c + 2, :].rearrange("p a d -> p (a d)"), ident[:])
                        i.then_inc(s["oT_psum"], 1)
                    pe.wait_ge(s["oT_act"], 2)
                    pe.wait_ge(s["oT_dve"], 2)
                    for t in range(NT):
                        for c in range(4):
                            i = mm(bank[:, 4, tile(t)], OT[:, c, tile(t)], res["Wo"][:, c, :], start=c == 0, stop=c == 3)
                    i.then_inc(s["attn_psum"], 1)

                    normed_T(1)
                    pe.wait_ge(s["hnT_ready"], 2)
                    experts(0, inT, "m0_")

                    normed_T(2)
                    pe.wait_ge(s["hnT_ready"], 3)
                    for i, (m, g) in enumerate((("Wq1", 0), ("Wq1", 1), ("Wk1", 0), ("Wk1", 1))):
                        mm(bank[:, i, 0:TP], res[m][:, g, :], inT, start=True, stop=True).then_inc(s["lq_psum"], 1)
                    for u in range(2 * NT):
                        at = slice(P * (u % NT), P * (u % NT) + P)
                        first = P * (u // 2) + KC * (u % 2)
                        mm(bank[0:KC, 4 + u // NT, at], hnT[:, first:first + KC], res["Wv1"][:], start=True, stop=False)
                        i = mm(bank[0:KC, 4 + u // NT, at], ones[:, 0:KC], res["bv1"][:], start=False, stop=True)
                        if u % NT == NT - 1:
                            i.then_inc(s["lv_psum"], 1)
                    pe.wait_ge(s["lq_ready"], 4)
                    for t in range(NT):
                        if t == 1:
                            pe.wait_ge(s["lv_ready"], 2)
                        if t == 2:
                            pe.wait_ge(s["lmax_done"], 1)
                        for j in range(J1):
                            to = 4 * (t % 2) + j
                            mm(bank[:, to, 0:2 * WIN], identb[:], bandq[:, t, :].unsqueeze(1).to_broadcast([P, G1, WIN]),
                               start=True, stop=True)
                        for j in range(J1):
                            to, r = 4 * (t % 2) + j, slice(32 * j, 32 * j + 32)
                            for g in range(G1):
                                i = mm(bank[:, to, WIN * g:WIN * g + WIN], qT[r, g, tile(t)], kT[r, g, P * t:P * t + WIN],
                                       start=False, stop=True, skip_group_check=True, tile_position=(32 * j, 0))
                        i.then_inc(s["lmax_psum"], 1)
                    pe.wait_ge(s["lmax_done"], NT)
                    for g in range(G1):
                        for t in range(NT):
                            i = tr(bank[:, 4 + g, tile(t)], Mexp[:, t, g, :], ident[:])
                    i.then_inc(s["lmaxT_psum"], 1)
                    pe.wait_ge(s["qTa_ready"], 1)

                    def band_scores_T(t):
                        if t:
                            pe.wait_ge(s["lexp_done"], t)
                        for j in range(J1):
                            mm(bank[0:KC, j, :], identb[0:KC, 0:KC],
                               bandk[:, t, :, :].unsqueeze(2).to_broadcast([KC, 2, G1, P]), start=True, stop=True)
                        for j in range(J1):
                            r = slice(32 * j, 32 * j + 32)
                            for c in range(2):
                                for g in range(G1):
                                    i = mm(bank[0:KC, j, (c * G1 + g) * P:(c * G1 + g + 1) * P],
                                           kT[r, g, P * t + KC * c:P * t + KC * c + KC], qTa[r, g, tile(t)],
                                           start=False, stop=True, skip_group_check=True, tile_position=(32 * j, 0))
                        i.then_inc(s["lst_psum"], 1)

                    def band_values(t):
                        pe.wait_ge(s["lexp_done"], t + 1)
                        if t == 2:
                            pe.wait_ge(s["lnorm_done"], 1)
                        for hd in range(H1):
                            g, j = hd // J1, hd % J1
                            for c in range(2):
                                at = (c * G1 + g) * P
                                i = mm(bank[:, 6 + t % 2, (D1 + 1) * hd:(D1 + 1) * (hd + 1)], P1[:, t % 2, j, at:at + P],
                                       V1[:, 2 * t + c, hd, :], start=c == 0, stop=c == 1)
                        i.then_inc(s["lpv_done"], 1)

                    band_scores_T(0)
                    for t in range(NT):
                        if t + 1 < NT:
                            band_scores_T(t + 1)
                        band_values(t)
                    pe.wait_ge(s["lnorm_done"], NT)
                    for t in range(NT):
                        i = tr(bank[:, 4, tile(t)], O1[:, t, :, :].rearrange("p a d -> p (a d)"), ident[:])
                    i.then_inc(s["lo_psum"], 1)
                    pe.wait_ge(s["lo_ready"], 1)
                    for t in range(NT):
                        mm(bank[:, 5, tile(t)], O1T[:, tile(t)], res["Wp1"][:], start=True, stop=False)
                        i = mm(bank[:, 5, tile(t)], ones[:], res["bp1"][:], start=False, stop=True)
                    i.then_inc(s["lproj_psum"], 1)

                    normed_T(3)
                    pe.wait_ge(s["hnT_ready"], 4)
                    for t in range(NT):
                        mm(bank[:, t if t != 1 else 5, 0:3 * C], inT[:, tile(t)], res["Wqkv2"][:], start=True, stop=True)\
                            .then_inc(s["fqkv_psum"], 1)
                    pe.wait_ge(s["fqkn_ready"], 1)
                    for which in range(2):
                        for t in range(NT):
                            i = tr(bank[:, 3 + which, tile(t)],
                                   qk[:, t, 2 * which:2 * which + 2, :].rearrange("p a d -> p (a d)"), ident[:])
                        i.then_inc(s["fqT_psum"], 1)
                    pe.wait_ge(s["fq_ready"], 2)
                    pe.wait_ge(s["fk_ready"], 2)
                    pe.wait_ge(s["fv_ready"], NT)
                    for hd in range(H2):
                        for t in range(NT):
                            L = P * (t + 1)
                            mm(bank[:, NT * hd + t, 0:L], QF[0:D2, hd, tile(t)], KF[0:D2, hd, 0:L], start=True, stop=True)
                            i = mm(bank[:, NT * hd + t, tile(t)], identb[:], laterq[:], start=False, stop=True,
                                   skip_group_check=True)
                    i.then_inc(s["fmax_psum"], 1)
                    pe.wait_ge(s["fmax_done"], 1)
                    for t in range(NT):
                        i = tr(bank[0:H2, 6, tile(t)], Mf[:, t, :], ident[:])
                    i.then_inc(s["fmaxT_psum"], 1)
                    pe.wait_ge(s["fneg_ready"], 1)
                    for hd in range(H2):
                        for k in range(NT):
                            mm(bank[:, NT * hd + k, P * k:TP], KF[:, hd, tile(k)], QF[:, hd, P * k:TP], start=True, stop=True)
                            i = mm(bank[:, NT * hd + k, tile(k)], identb[:], laterk[:], start=False, stop=True,
                                   skip_group_check=True)
                            i.then_inc(s["fst_psum"], 1)
                    pe.wait_ge(s["fexp_done"], H2 * NT)
                    for hd in range(H2):
                        for t in range(NT):
                            at = (hd * NT + t) * (D2 + 1)
                            for k in range(t + 1):
                                i = mm(bank[:, 7, at:at + D2 + 1], PF[:, hd, k, tile(t)], VF[:, k, hd, :],
                                       start=k == 0, stop=k == t)
                    i.then_inc(s["fpv_done"], 1)
                    pe.wait_ge(s["fo_ready"], 1)
                    for t in range(NT):
                        i = tr(bank[:, 0, tile(t)], OF[:, t, :, :].rearrange("p a d -> p (a d)"), ident[:])
                    i.then_inc(s["foT_psum"], 1)
                    pe.wait_ge(s["foT_ready"], 1)
                    mm(bank[:, 1, 0:TP], res["Wo2"][:], OFT[:], start=True, stop=True).then_inc(s["y_psum"], 1)
                    pe.wait_ge(s["y_ready"], 1)
                    experts(1, yT[:], "m1_")

                @block.scalar
                def _(act):
                    fn = nc.scalar.activation
                    steps = [0]

                    def link(i):
                        steps[0] += 1
                        i.then_inc(s["scalar_step"], 1)
                        act.wait_ge(s["scalar_step"], steps[0])

                    def rsqrt(n):
                        link(fn(lnv[:, 0:n], ve[:] if n == NT else ss[:], ACT.Ln))
                        return fn(y0[:, 0:n], lnv[:, 0:n], ACT.Exp, scale=-0.5)

                    def norm(k):
                        act.wait_ge(s["var_ready"], k + 1)
                        rsqrt(NT).then_inc(s["rsqrt_guess"], 1)
                        act.wait_ge(s["hnT_psum"], k + 1)
                        fn(hnT[:, HALF:HALF + TP], bank[:, 1, 0:TP], ACT.Copy).then_inc(s["hnT_ready"], 1)

                    def experts(f, func, b1):
                        act.wait_ge(s["logits_shift"], f + 1)
                        fn(ge[:], lm[:], ACT.Exp).then_inc(s["gate_exp"], 1)
                        for e in range(E):
                            n = E * f + e
                            if e == 1:
                                act.wait_ge(s["gateT_psum"], f + 1)
                                fn(gT[:], bank[0:E, 0, 0:TP], ACT.Copy).then_inc(s["gateT_ready"], 1)
                            for c in range(FC):
                                act.wait_ge(s["hid_psum"], n * FC + c + 1)
                                if n >= 2:
                                    act.wait_ge(s["w2_done"], n - 1)
                                fn(HT[:, e % 2, c, :], bank[:, 2 + c, 0:TP], func, bias=b1[:, e, c:c + 1])\
                                    .then_inc(s["hid_ready"], 1)

                    act.wait_ge(s["tdnn_done"], 1)
                    fn(h[:], bank[:, 0, 0:TP].rearrange("p (t c) -> p t c", t=NT), ACT.Relu).then_inc(s["h_ready"], 1)
                    norm(0)
                    for p in range(H0 // 2):
                        act.wait_ge(s["q_psum"], p + 1)
                        for a in range(2):
                            fn(QA[0:D0, 2 * p + a, :], bank[D0 * a:D0 * a + D0, p, 0:TP], ACT.Copy)\
                                .then_inc(s["q_ready"], 1)
                    for t in range(NT):
                        act.wait_ge(s["v_psum"], t + 1)
                        fn(VA[:, t, :, 0:D0], bank[:, t, :].rearrange("p (a d) -> p a d", a=H0), ACT.Copy)\
                            .then_inc(s["v_ready"], 1)
                    act.wait_ge(s["maxT_psum"], 1)
                    fn(QA[D0:, :, :], bank[0:H0, 6, 0:TP].unsqueeze(1).to_broadcast([H0, H0, TP]), ACT.Copy,
                       scale=-1.0).then_inc(s["negmax_ready"], 1)
                    for hd in range(H0):
                        act.wait_ge(s["st_psum"], hd + 1)
                        if hd >= 2:
                            act.wait_ge(s["pv_done"], hd - 1)
                        b = NT * (hd % 2)
                        fn(PT[:, hd % 2, :, :], bank[:, b:b + NT, 0:TP], ACT.Exp, scale=D0 ** -0.5)\
                            .then_inc(s["exp_done"], 1)
                    for c in (0, 2):
                        act.wait_ge(s["oT_psum"], c + 1)
                        fn(OT[:, c, :], bank[:, c, 0:TP], ACT.Copy).then_inc(s["oT_act"], 1)
                    norm(1)
                    experts(0, ACT.Gelu, res["m0_b1"])
                    norm(2)
                    for i in range(4):
                        act.wait_ge(s["lq_psum"], i + 1)
                        to = qT[:, i, :] if i < 2 else kT[:, i - 2, HALF:HALF + TP]
                        fn(to, bank[:, i, 0:TP], ACT.Identity, bias=res["bqk1"][:, i:i + 1]).then_inc(s["lq_ready"], 1)
                    for t in range(NT):
                        act.wait_ge(s["lst_psum"], t + 1)
                        if t == 2:
                            act.wait_ge(s["lpv_done"], 1)
                        fn(P1[:, t % 2, :, :], bank[0:KC, 0:J1, :], ACT.Exp, scale=D1 ** -0.5).then_inc(s["lexp_done"], 1)
                    act.wait_ge(s["lo_psum"], 1)
                    fn(O1T[:], bank[:, 4, 0:TP], ACT.Copy).then_inc(s["lo_ready"], 1)
                    norm(3)
                    for t in range(NT):
                        b = t if t != 1 else 5
                        act.wait_ge(s["fqkv_psum"], t + 1)
                        fn(sq[:, t, :], bank[:, b, 0:2 * C], ACT.Square).then_inc(s["fsq"], 1)
                        fn(VF[:, t, :, 0:D2], bank[:, b, 2 * C:3 * C].rearrange("p (a d) -> p a d", a=H2), ACT.Copy)\
                            .then_inc(s["fv_ready"], 1)
                    act.wait_ge(s["fss_ready"], 1)
                    rsqrt(4 * NT).then_inc(s["frs_guess"], 1)
                    act.wait_ge(s["fqT_psum"], 1)
                    for a in range(H2):
                        fn(QF[0:D2, a, :], bank[D2 * a:D2 * a + D2, 3, 0:TP], ACT.Copy).then_inc(s["fq_ready"], 1)
                    act.wait_ge(s["fmaxT_psum"], 1)
                    fn(QF[D2:, :, :], bank[0:H2, 6, 0:TP].unsqueeze(1).to_broadcast([H2, H2, TP]), ACT.Copy,
                       scale=-1.0).then_inc(s["fneg_ready"], 1)
                    for hd in range(H2):
                        for k in range(NT):
                            act.wait_ge(s["fst_psum"], NT * hd + k + 1)
                            fn(PF[:, hd, k, P * k:TP], bank[:, NT * hd + k, P * k:TP], ACT.Exp, scale=float(D2) ** 0.5)\
                                .then_inc(s["fexp_done"], 1)
                    act.wait_ge(s["foT_psum"], 1)
                    fn(OFT[:], bank[:, 0, 0:TP], ACT.Copy).then_inc(s["foT_ready"], 1)
                    act.wait_ge(s["y_psum"], 1)
                    fn(yT[:], bank[:, 1, 0:TP], ACT.Copy).then_inc(s["y_ready"], 1)
                    experts(1, ACT.Gelu_apprx_tanh, res["m1_b1"])

                @block.vector
                def _(dve):
                    v = nc.vector
                    steps = [0]

                    def link(i):
                        steps[0] += 1
                        i.then_inc(s["vector_step"], 1)
                        dve.wait_ge(s["vector_step"], steps[0])

                    def newton(x, n):
                        y = y0[:, 0:n]
                        link(v.scalar_tensor_tensor(nt1[:, 0:n], y, -0.5, y, ALU.mult, ALU.mult))
                        link(v.tensor_tensor(nt2[:, 0:n], nt1[:, 0:n], x, ALU.mult))
                        link(v.scalar_tensor_tensor(rstd[:, 0:n], nt2[:, 0:n], 1.5, y, ALU.add, ALU.mult))

                    def norm(k):
                        for t in range(NT):
                            i = v.bn_stats(stats[:, t, :], h[:, t, :])
                        link(i)
                        for t in range(NT):
                            i = v.bn_aggr(mv[:, t, :], stats[:, t, :])
                        link(i)
                        v.tensor_scalar(ve[:], mv[:, :, 1], 1e-5, None, ALU.add).then_inc(s["var_ready"], 1)
                        dve.wait_ge(s["rsqrt_guess"], k + 1)
                        newton(ve[:], NT)
                        for t in range(NT):
                            i = v.tensor_scalar(hn[:, t, :], h[:, t, :], mv[:, t, 0:1], rstd[:, t:t + 1],
                                                ALU.subtract, ALU.mult)
                        if k == 3:
                            link(i)
                            link(v.tensor_tensor(hn[:], hn[:], res["lng"][:].unsqueeze(1).to_broadcast([P, NT, C]), ALU.mult))
                            i = v.tensor_tensor(hn[:], hn[:], res["lnb"][:].unsqueeze(1).to_broadcast([P, NT, C]), ALU.add)
                        i.then_inc(s["hn_ready"], 1)

                    def add_to_h(b):
                        link(v.tensor_tensor(h[:], bank[:, b, 0:TP].rearrange("p (t c) -> p t c", t=NT), h[:], ALU.add))

                    def experts(f):
                        dve.wait_ge(s["logits_psum"], f + 1)
                        lg = bank[:, 0, 0:NT * E].rearrange("p (t e) -> p t e", t=NT)

                        def per_tile(x):
                            return x[:].unsqueeze(2).to_broadcast([P, NT, E])

                        link(v.tensor_reduce(gm[:], lg, AX, ALU.max))
                        v.tensor_tensor(lm[:], lg, per_tile(gm), ALU.subtract).then_inc(s["logits_shift"], 1)
                        dve.wait_ge(s["gate_exp"], f + 1)
                        link(v.tensor_reduce(gs[:], ge[:], AX, ALU.add))
                        link(v.reciprocal(gr[:], gs[:]))
                        if f == 0:
                            link(v.scalar_tensor_tensor(ga[:], lm[:], 0.0, res["c_rank"][:], ALU.is_equal, ALU.mult))
                            link(v.tensor_reduce(gb[:], ga[:], AX, ALU.max))
                            link(v.tensor_tensor(ga[:], ga[:], per_tile(gb), ALU.is_equal))
                            v.tensor_tensor(gate[:], ga[:], per_tile(gr), ALU.mult).then_inc(s["gate_ready"], 1)
                        else:
                            v.tensor_tensor(gate[:], ge[:], per_tile(gr), ALU.mult).then_inc(s["gate_ready"], 1)
                        dve.wait_ge(s["b2_psum"], f + 1)
                        add_to_h(1)
                        for e in range(E):
                            dve.wait_ge(s["w2_done"], E * f + e + 1)
                            for t in range(NT):
                                i = v.scalar_tensor_tensor(h[:, t, :], bank[:, 6 + e % 2, tile(t)], gate[:, t, e:e + 1],
                                                           h[:, t, :], ALU.mult, ALU.add)
                            i.then_inc(s["acc_done"], 1)
                            dve.wait_ge(s["acc_done"], E * f + e + 1)

                    dve.wait_ge(s["h_ready"], 1)
                    norm(0)
                    for p in range(H0 // 2):
                        dve.wait_ge(s["k_psum"], p + 1)
                        for a in range(2):
                            v.tensor_copy(KA[0:D0, 2 * p + a, :], bank[D0 * a:D0 * a + D0, 4 + p, 0:TP])\
                                .then_inc(s["k_ready"], 1)
                    dve.wait_ge(s["hn_ready"], 1)
                    link(v.tensor_tensor(h[:], h[:], hn[:], ALU.add))
                    for hd in range(H0):
                        dve.wait_ge(s["smax_psum"], hd + 1)
                        b = NT * (hd % 2)
                        v.tensor_reduce(Mx[:, :, hd], bank[:, b:b + NT, 0:T], AX, ALU.max).then_inc(s["max_done"], 1)
                    for pair in range(H0 // 2):
                        dve.wait_ge(s["pv_done"], 2 * pair + 2)
                        ov = bank[:, 6 + pair % 2, 0:2 * NT * (D0 + 1)].rearrange("p (a t d) -> p a t d", a=2, t=NT)
                        link(v.reciprocal(rec[:], ov[:, :, :, D0]))
                        for a in range(2):
                            i = v.tensor_tensor(O[:, :, 2 * pair + a, :], ov[:, a, :, 0:D0],
                                                rec[:, a, :].unsqueeze(2).to_broadcast([P, NT, D0]), ALU.mult)
                        i.then_inc(s["o_norm"], 1)
                        dve.wait_ge(s["o_norm"], pair + 1)
                    for c in (1, 3):
                        dve.wait_ge(s["oT_psum"], c + 1)
                        v.tensor_copy(OT[:, c, :], bank[:, c, 0:TP]).then_inc(s["oT_dve"], 1)
                    dve.wait_ge(s["attn_psum"], 1)
                    add_to_h(4)
                    norm(1)
                    experts(0)
                    norm(2)
                    for i in range(2):
                        dve.wait_ge(s["lv_psum"], i + 1)
                        for u in range(NT):
                            n = v.tensor_copy(V1[:, NT * i + u, :, 0:D1],
                                              bank[0:KC, 4 + i, tile(u)].rearrange("p (a d) -> p a d", a=H1))
                        n.then_inc(s["lv_ready"], 1)
                    for t in range(NT):
                        dve.wait_ge(s["lmax_psum"], t + 1)
                        b = 4 * (t % 2)
                        for g in range(G1):
                            i = v.tensor_reduce(Mexp[:, t, g, 0:P:32], bank[:, b:b + J1, WIN * g:WIN * g + WIN], AX, ALU.max)
                        i.then_inc(s["lmax_done"], 1)
                    dve.wait_ge(s["lmaxT_psum"], 1)
                    v.tensor_tensor(qTa[:], qT[:], bank[:, 4:6, 0:TP], ALU.subtract).then_inc(s["qTa_ready"], 1)
                    for t in range(NT):
                        dve.wait_ge(s["lpv_done"], t + 1)
                        ov = bank[:, 6 + t % 2, 0:H1 * (D1 + 1)].rearrange("p (a d) -> p a d", a=H1)
                        link(v.reciprocal(rec1[:], ov[:, :, D1]))
                        v.tensor_tensor(O1[:, t, :, :], ov[:, :, 0:D1], rec1[:].unsqueeze(2).to_broadcast([P, H1, D1]),
                                        ALU.mult).then_inc(s["lnorm_done"], 1)
                        dve.wait_ge(s["lnorm_done"], t + 1)
                    dve.wait_ge(s["lproj_psum"], 1)
                    add_to_h(5)
                    norm(3)
                    dve.wait_ge(s["fsq"], NT)
                    link(v.tensor_reduce(ss[:], sq.rearrange("p t (a d) -> p (t a) d", a=4), AX, ALU.add))
                    v.tensor_scalar(ss[:], ss[:], 1e-12, None, ALU.add).then_inc(s["fss_ready"], 1)
                    dve.wait_ge(s["frs_guess"], 1)
                    newton(ss[:], 4 * NT)
                    for t in range(NT):
                        b = t if t != 1 else 5
                        i = v.tensor_tensor(qk[:, t, :, :], bank[:, b, 0:2 * C].rearrange("p (a d) -> p a d", a=4),
                                            rstd[:, 4 * t:4 * t + 4].unsqueeze(2).to_broadcast([P, 4, D2]), ALU.mult)
                    link(i)
                    for t in range(NT):
                        i = v.tensor_tensor(qk[:, t, :, :], qk[:, t, :, :], res["qkg"][:], ALU.mult)
                    i.then_inc(s["fqkn_ready"], 1)
                    dve.wait_ge(s["fqT_psum"], 2)
                    for a in range(H2):
                        v.tensor_copy(KF[0:D2, a, :], bank[D2 * a:D2 * a + D2, 4, 0:TP]).then_inc(s["fk_ready"], 1)
                    dve.wait_ge(s["fmax_psum"], 1)
                    for t in range(NT):
                        for hd in range(H2):
                            i = v.tensor_reduce(Mf[:, t, hd:hd + 1], bank[:, NT * hd + t, 0:P * (t + 1)], AX, ALU.max)
                    i.then_inc(s["fmax_done"], 1)
                    dve.wait_ge(s["fpv_done"], 1)
                    ov = bank[:, 7, 0:H2 * NT * (D2 + 1)].rearrange("p (a t d) -> p a t d", a=H2, t=NT)
                    link(v.reciprocal(rec2[:], bank[:, 7, 0:H2 * NT * (D2 + 1)].rearrange("p (a d) -> p a d", d=D2 + 1)[:, :, D2]))
                    for a in range(H2):
                        i = v.tensor_tensor(OF[:, :, a, :], ov[:, a, :, 0:D2],
                                            rec2[:, NT * a:NT * a + NT].unsqueeze(2).to_broadcast([P, NT, D2]), ALU.mult)
                    i.then_inc(s["fo_ready"], 1)
                    experts(1)

            nc.all_engine_barrier()
            for one in sems:
                nc.gpsimd.sem_clear(one)
            nc.all_engine_barrier()


def layout(i):
    f = {k: np.asarray(v) for k, v in i.items()}
    a = np.ascontiguousarray

    def chunks(m, n):
        return a(m.reshape(n, P, m.shape[-1]).transpose(1, 0, 2))

    w = {"x": a(f["x"].transpose(0, 2, 1)),
         "tokW": chunks(f["L0_tok_W"].T, TAPS), "tokb": a(f["L0_tok_b"].reshape(1, C)),
         "Wq": a(f["L0_attn_Wq"].T), "Wk": a(f["L0_attn_Wk"].T), "Wv": a(f["L0_attn_Wv"].T),
         "Wo": chunks(f["L0_attn_Wo"].T, 4)}
    for pre, src, wg, bg in (("m0_", "L0_ffn_", "Ws", "bs"), ("m1_", "L1_ffn_", "gate_W", "gate_b")):
        w[pre + "Wg"] = a(f[src + wg])
        w[pre + "bg"] = a(f[src + bg].reshape(1, E))
        w[pre + "W1"] = a(f[src + "W1"].transpose(1, 0, 2))
        w[pre + "b1"] = a(f[src + "b1"].reshape(E, FC, P).transpose(2, 0, 1))
        w[pre + "W2"] = a(f[src + "W2"].reshape(E, FC, P, C).transpose(2, 0, 1, 3))
        w[pre + "b2"] = a(f[src + "b2"])
    wqkv, bqkv = f["L1_attn_W_qkv"], f["L1_attn_b_qkv"]
    bias = np.zeros((G1 * 2, J1, 32), np.float32)
    for k, name in enumerate(("Wq1", "Wk1")):
        m = np.zeros((P, G1, J1, 32), np.float32)
        m[:, :, :, 1:D1 + 1] = wqkv[:, C * k:C * k + C].reshape(P, G1, J1, D1)
        w[name] = m.reshape(P, G1, P)
        bias[G1 * k:G1 * k + G1, :, 1:D1 + 1] = bqkv[C * k:C * k + C].reshape(G1, J1, D1)
    bias[G1:, :, 0] = 1
    w["bqk1"] = a(bias.reshape(2 * G1, P).T)
    w["Wv1"] = a(wqkv[:, 2 * C:])
    w["bv1"] = a(bqkv[2 * C:].reshape(1, C))
    w["Wp1"] = a(f["L1_attn_W_proj"])
    w["bp1"] = a(f["L1_attn_b_proj"].reshape(1, C))
    w["lng"] = a(np.broadcast_to(f["L1_ffn_ln_g"], (P, C)))
    w["lnb"] = a(np.broadcast_to(f["L1_ffn_ln_b"], (P, C)))
    w["Wqkv2"] = a(np.concatenate([f["L1_ffn_Wq"], f["L1_ffn_Wk"], f["L1_ffn_Wv"]], 1))
    w["Wo2"] = a(f["L1_ffn_Wo"])
    g = np.stack([f["L1_ffn_qn_g"]] * H2 + [f["L1_ffn_kn_g"]] * H2)
    w["qkg"] = a(np.broadcast_to(g, (P, 2 * H2, D2)))
    return w


def kernel(**inputs):
    import concourse.bacc as _bacc
    from concourse.bass_utils import run_bass_kernel_spmd as _run

    nc = _bacc.Bacc("TRN2", target_bir_lowering=False, num_devices=1)
    arrays = {**layout(inputs), **constants()}
    aps = {n: nc.dram_tensor(f"in_{n}", a.shape, mybir.dt.from_np(a.dtype), kind="ExternalInput").ap()
           for n, a in arrays.items()}
    out = nc.dram_tensor("out_0", (B, T, C), F32, kind="ExternalOutput").ap()
    tower(nc, aps, out)
    r = _run(nc, [{f"in_{n}": a for n, a in arrays.items()}], core_ids=[0])
    return r.results[0]["out_0"]
```

```python
from contextlib import ExitStack

import numpy as np

import concourse.bass as bass
from concourse import mybir

F32 = mybir.dt.float32
BF16 = mybir.dt.bfloat16
F16 = mybir.dt.float16
I32 = mybir.dt.int32
ALU = mybir.AluOpType
ACT = mybir.ActivationFunctionType
AX = mybir.AxisListType.X

P = 128
B, T_IN, C = 16, 375, 128
TAPS = 5
T = T_IN - TAPS + 1
NT = -(-T // P)
TP = NT * P
LAST = T - (NT - 1) * P
H0, D0 = 8, 64
H1, D1, HALF = 8, 16, 32
H2, D2 = 2, 64
E, FF = 8, 512
FC = FF // P
WIN = P + 2 * HALF
KC = WIN // 2
G1 = 2
J1 = H1 // G1
MASKED = -1e30


def constants():
    q = np.arange(P)
    ident = np.eye(P, dtype=np.float32)
    band_q = np.full((P, NT, WIN), MASKED, np.float32)
    band_k = np.full((KC, NT, 2, P), MASKED, np.float32)
    for t in range(NT):
        key = P * t - HALF + np.arange(WIN)
        seen = (abs(key[None, :] - (P * t + q)[:, None]) <= HALF) & (key >= 0) & (key < T)
        band_q[:, t][seen] = 0
        for c in range(2):
            band_k[:, t, c][seen.T[KC * c:KC * (c + 1)]] = 0
    later_q = np.where(q[None, :] > q[:, None], MASKED, 0).astype(np.float32)
    sel0 = np.zeros((H0 + 1, 2 * H0), np.float32)
    sel0[:H0] = np.tile(np.eye(H0), 2)
    sel0[H0, H0:] = -30000
    part = np.array([[0], [-1]], np.float32)
    rank = np.tile(np.arange(E, 0, -1, dtype=np.float32), (P, NT)).reshape(P, NT, E)
    row = np.arange(P)
    rows = np.stack([-((row % 32 >= D1).astype(np.float32)), row % 32 < D1, row % 32 == D1], 1).astype(np.float32)
    heads = (row[:, None] // 32 == np.arange(J1)).astype(np.float32)
    return {"c_rows": rows, "c_heads": heads, "c_ident": ident, "c_band_q": band_q, "c_band_k": band_k, "c_later_q": later_q,
            "c_later_k": np.ascontiguousarray(later_q.T), "c_sel0": sel0, "c_part": part, "c_rank": rank}


FULL = dict(qk_psum=H0, qk_hi=2 * H0, qk_lo=2 * H0, q_copied=H0, k_copied=16 * H0 // 2, v_psum=NT, v_hi=NT, v_lo=NT,
            smax_psum=H0 * NT // 2, max_done=H0 * NT // 2, maxT_psum=1, negmax_ready=1, st_psum=H0, exp_done=H0,
            p_hi=H0, p_lo=H0, p_lo_pool=H0, pv_psum=H0, o_norm=H0, oT_psum=4, oT_hi=4, oT_lo=4, attn_psum=1)
SLID = {n: FULL[n] + k for n, k in dict(
    qk_psum=4, qk_hi=4, qk_lo=4, q_copied=0, k_copied=0, v_psum=2, v_hi=2, v_lo=2, smax_psum=4 * NT, max_done=4 * NT,
    maxT_psum=1, negmax_ready=0, st_psum=4 * NT, exp_done=4 * NT, p_hi=4 * NT, p_lo=3 * NT, p_lo_pool=NT,
    pv_psum=NT, o_norm=NT, oT_psum=1, oT_hi=1, oT_lo=1, attn_psum=1).items()}


PIECES = {"tdnn": 1, "norm0": 1, "norm1": 1, "norm2": 1, "norm3": 1, "qkv": 11, "maxima": 13, "heads": 9, "out0": 5,
          "experts0": 9, "bproj": 6, "bmax": 4, "bheads": 4, "bout": 2, "cproj": 2, "cmax": 2, "cheads": 3,
          "cout": 2, "experts1": 9}
GROUPS = [["tdnn", "norm0", "qkv"], ["maxima"], ["heads"], ["out0", "norm1"], ["experts0"],
          ["norm2", "bproj", "bmax"], ["bheads"], ["bout", "norm3", "cproj"], ["cmax", "cheads", "cout"],
          ["experts1"]]


def side_by_side(stages, slots):
    def through(group, slot):
        for name in group:
            n = 0
            for _ in stages[name](slot):
                n += 1
                yield
            assert n == PIECES[name], (name, n)

    for g in range(len(GROUPS) + 1):
        runs = [(through(GROUPS[g - q], slots[q]), sum(PIECES[n] for n in GROUPS[g - q]))
                for q in range(2) if 0 <= g - q < len(GROUPS)]
        turns = sorted(((i + 0.5) / n, q) for q, (_, n) in enumerate(runs) for i in range(n))
        for _, q in turns:
            next(runs[q][0])
        for run, _ in runs:
            assert next(run, "done") == "done"


def tower(nc, w, out):
    with ExitStack() as ctx:
        def sb(name, shape, dt=F32):
            return ctx.enter_context(nc.sbuf_tensor("s_" + name, shape, dt))

        load = ctx.enter_context(nc.semaphore("weights_loaded"))
        round_split = ctx.enter_context(nc.semaphore("round_split"))
        out_stored = ctx.enter_context(nc.semaphore("out_stored"))
        step = ctx.enter_context(nc.semaphore("startup_step"))
        bank = ctx.enter_context(nc.psum_tensor("bank", [P, 8, 512], F32))
        SLOTS = range(2)

        PLAIN = ["c_rows", "c_heads", "c_sel0", "c_part", "c_ident", "c_rank", "lng", "lnb", "qkg",
                 "m0_b1", "m1_b1", "m0_b2", "m1_b2"]
        MASKS = {"c_band_q": "bandq", "c_band_k": "bandk", "c_later_q": "laterq", "c_later_k": "laterk"}
        res = {n: sb(n, list(w[n].shape)) for n in PLAIN}
        mask = {n: sb(MASKS[n], list(w[n].shape), BF16) for n in MASKS}
        SPLIT = ["tokW", "Wq", "Wk", "Wv", "Wo", "m0_Wg", "m1_Wg", "Wq1", "Wk1", "Wv1", "Wp1", "Wqkv2", "Wo2",
                 "m0_W1", "m0_W2", "m1_W1", "m1_W2"]
        hi = {n: sb(n + "_hi", list(w[n].shape), F16) for n in SPLIT}
        lo = {n: sb(n + "_lo", list(w[n].shape), F16) for n in SPLIT}
        BIAS = ["tokb", "m0_bg", "m1_bg", "bqk1", "bv1", "bp1"]
        bias = {n: sb(n, [2, w[n].shape[1]], F16) for n in BIAS}
        bias_hi = {n: sb(n + "_hi", [2, w[n].shape[1]], F16) for n in BIAS}
        ident = res["c_ident"]
        identb = sb("identb", [P, P], BF16)
        ones = sb("ones", [2, TP], F16)

        class Slot:
            pass

        slots = []
        RING = 6
        ARENA = 9776
        sems = [out_stored]
        names = """margins_set x_loaded x_hi x_lo tdnn_psum h_ready hn_ready hnT_psum hnT_hi hnT_lo qk_psum qk_hi qk_lo q_copied k_copied
            v_psum v_hi v_lo smax_psum max_done maxT_psum negmax_ready st_psum exp_done p_hi p_lo p_lo_pool
            pv_psum o_norm oT_psum oT_hi oT_lo attn_psum logits_psum logits_shift gate_exp gate_ready gateT_psum
            gateT_ready b2_psum hid_psum gelu_done hid_hi hid_lo hid_lo_pool down_psum acc_done bqz_ready
            bq2_ready csq cqk_ready cqkT_psum y_psum y_hi y_lo vector_step""".split()
        for q in SLOTS:
            z = Slot()
            slots.append(z)

            def own(name, shape, dt=F32):
                return sb(f"{name}{q}", shape, dt)

            z.q, z.b = q, 4 * q
            z.s = {}
            for n in names:
                z.s[n] = ctx.enter_context(nc.semaphore(f"{n}{q}"))
                sems.append(z.s[n])
            z.xT_hi, z.xT_lo = own("xT_hi", [P, TP + TAPS - 1], F16), own("xT_lo", [P, TP + TAPS - 1], F16)
            z.h, z.hn = own("h", [P, NT, C]), own("hn", [P, NT, C])
            z.hT_hi, z.hT_lo = (own("hT_hi", [P, HALF + TP + HALF], F16), own("hT_lo", [P, HALF + TP + HALF], F16))
            z.stats, z.mv = own("stats", [P, NT, 6]), own("mv", [P, NT, 2])
            z.ve, z.guess, z.n1, z.n2, z.rstd = (own(n, [P, 12]) for n in ("ve", "guess", "n1", "n2", "rstd"))
            z.KB = own("KB", [D0 + H0 + 1, H0, TP], F16)
            z.V_hi, z.V_lo = (own("V_hi", [P, NT, H0, D0 + 1], F16), own("V_lo", [P, NT, H0, D0 + 1], F16))
            z.Mx, z.rec = own("Mx", [P, (H0 + 1) * NT]), own("rec", [P, 8])
            z.lm, z.ge, z.ga, z.gate = (own(n, [P, NT, E]) for n in ("lm", "ge", "ga", "gate"))
            z.gm, z.gs, z.gr, z.gb = (own(n, [P, NT]) for n in ("gm", "gs", "gr", "gb"))
            arena = own("arena", [P, ARENA])
            z.arena = arena

            class Carver:
                at = 0

            def carve(words, dt, pattern, parts=P, **sizes):
                v = arena[0:parts, Carver.at:Carver.at + words]
                Carver.at += words
                assert Carver.at <= ARENA, Carver.at
                return (v if dt == F32 else v.bitcast(dt)).rearrange(pattern, **sizes)

            hw = H0 * TP // 2
            z.QS = carve(hw, F16, "p (a n) -> p a n", a=H0)
            z.QB = carve(hw, F16, "p (a n) -> p a n", a=H0)
            z.KS = carve(hw, F16, "p (a n) -> p a n", a=H0)
            z.Pf = carve(NT * TP, F32, "p (t n) -> p t n", t=NT)
            z.P_hi = carve(NT * TP, F16, "p (b t n) -> p b t n", b=2, t=NT)
            z.P_lo = carve(NT * TP, F16, "p (b t n) -> p b t n", b=2, t=NT)
            z.O = carve(NT * C * 4, F32, "p (t a d) -> p t a d", t=NT, a=H0)
            z.OT_hi = z.P_hi.rearrange("p b t n -> p (b t n)")[:, 0:4 * TP].rearrange("p (c n) -> p c n", c=4)
            z.OT_lo = z.P_lo.rearrange("p b t n -> p (b t n)")[:, 0:4 * TP].rearrange("p (c n) -> p c n", c=4)
            z.xf = z.Pf[:, 0, :]
            Carver.at = 0
            z.Hf = carve(FC * TP, F32, "p (c n) -> p c n", c=FC)
            z.H_hi = carve(FC * TP, F16, "p (b c n) -> p b c n", b=2, c=FC)
            z.H_lo = carve(FC * TP, F16, "p (b c n) -> p b c n", b=2, c=FC)
            z.gT = carve(TP, F32, "p n -> p n", parts=E)
            Carver.at = 0
            z.q1_hi = carve(TP * G1 // 2, F16, "p (g n) -> p g n", g=G1)
            z.q1_st = carve(TP * G1 // 2, F16, "p (g n) -> p g n", g=G1)
            z.q1_m = z.q1_st
            z.qz_hi = carve(TP * G1 * J1 // 2, F16, "p (g j n) -> p g j n", g=G1, j=J1)
            z.qz_st = carve(TP * G1 * J1 // 2, F16, "p (g j n) -> p g j n", g=G1, j=J1)
            z.qz_m = z.qz_hi
            z.P1f_whole = carve(2 * 512, F32, "p n -> p n")
            z.P1f = z.P1f_whole[0:KC, :].rearrange("p (b n) -> p b n", b=2)
            mexp_at = Carver.at
            z.P1_hi, z.P1_lo = (carve(RING * 256, F16, "p (u n) -> p u n", parts=KC, u=RING) for _ in range(2))
            z.k1_d = z.P1f_whole[:, 0:G1 * TP].rearrange("p (g n) -> p g n", g=G1)
            z.V1_hi, z.V1_lo = (carve(NT * H1 * (D1 + 1), F16, "p (t a d) -> p t a d", parts=KC, t=2 * NT, a=H1)
                                for _ in range(2))
            z.k1_hi, z.k1_lo = (carve(G1 * (HALF + TP + HALF) // 2, F16, "p (g n) -> p g n", g=G1) for _ in range(2))
            z.Mexp = arena[:, mexp_at:mexp_at + NT * G1 * P].rearrange("p (t g n) -> p t g n", t=NT, g=G1)
            z.O1 = z.hn[:].rearrange("p t (a d) -> p t a d", a=H1)
            z.O1T_hi, z.O1T_lo = z.q1_hi[:, 0, :], z.q1_hi[:, 1, :]
            Carver.at = 3 * hw
            z.sq = carve(NT * 2 * C, F32, "p (t c) -> p t c", t=NT)
            z.qk = carve(NT * 2 * C, F32, "p (t a d) -> p t a d", t=NT, a=4)

        def flat(x):
            k = len(x.shape)
            return x if k == 2 else x.rearrange({3: "p a b -> p (a b)", 4: "p a b c -> p (a b c)"}[k])

        rounds, room = [[]], [ARENA, ARENA]
        for n in list(MASKS) + BIAS + SPLIT:
            words = int(np.prod(w[n].shape[1:]))
            q = 0 if words <= room[0] else 1
            if words > room[q]:
                rounds.append([])
                room, q = [ARENA, ARENA], 0
            at = ARENA - room[q]
            rounds[-1].append((n, slots[q].arena[0:w[n].shape[0], at:at + words]))
            room[q] -= words
        with nc.Block() as block:
            @block.sync
            def _(sp):
                for n in PLAIN:
                    sp.dma_start(res[n][:], w[n]).then_inc(load, 16)
                for r, what in enumerate(rounds):
                    if r:
                        sp.wait_ge(round_split, r)
                    for n, land in what:
                        sp.dma_start(land, flat(w[n])).then_inc(load, 16)

            @block.vector
            def _(dve):
                v = nc.vector
                v.memset(ones[:], 1.0)
                for z in slots:
                    for x in (z.xT_hi[:, T_IN:], z.xT_lo[:, T_IN:], z.hT_hi[:, 0:HALF], z.hT_hi[:, HALF + TP:],
                              z.hT_lo[:, 0:HALF], z.hT_lo[:, HALF + TP:], z.V_lo[:, :, :, D0:]):
                        v.memset(x, 0.0)
                    v.memset(z.V_hi[:, :, :, D0:], 1.0)
                    v.memset(z.Mx[:, H0 * NT:], -1.0)
                n_loads, n_steps = len(PLAIN), 0
                for r, what in enumerate(rounds):
                    n_loads += len(what)
                    dve.wait_ge(load, 16 * n_loads)
                    if r == 0:
                        v.tensor_copy(identb[:], ident[:])
                        for z in slots:
                            for at, n, rows in ((0, T, res["c_sel0"][:, 0:H0]), (T, TP - T, res["c_sel0"][:, H0:])):
                                v.tensor_copy(z.KB[D0:, :, at:at + n], rows.unsqueeze(2).to_broadcast([H0 + 1, H0, n]))
                    for n, land in what:
                        if n in SPLIT:
                            v.tensor_copy(flat(hi[n][:]), land).then_inc(step, 1)
                        elif n in BIAS:
                            v.tensor_copy(bias_hi[n][:], land).then_inc(step, 1)
                        else:
                            v.tensor_copy(flat(mask[n][:]), land).then_inc(step, 1)
                    n_steps += len(what)
                    dve.wait_ge(step, n_steps)
                    for n, land in what:
                        if n in SPLIT:
                            i = v.tensor_tensor(flat(lo[n][:]), land, flat(hi[n][:]), ALU.subtract)
                        elif n in BIAS:
                            i = v.scalar_tensor_tensor(bias[n][:], bias_hi[n][:], res["c_part"][:, 0:1], land,
                                                       ALU.mult, ALU.add)
                    i.then_inc(round_split, 1)
        nc.all_engine_barrier()

        def tile(t):
            return slice(P * t, P * (t + 1))

        def tiles(x):
            return x.rearrange("p (t c) -> p t c", t=NT)

        INNER = slice(HALF, HALF + TP)
        ROOT = D0 ** -0.5
        M_ROW = 16

        with nc.Fori(0, B - 1, 2) as seq:
            with nc.Block() as block:
                @block.sync
                def _(sp):
                    for z in slots:
                        sp.dma_start(z.xf[:, 0:T_IN], w["x"][seq + z.q]).then_inc(z.s["x_loaded"], 16)
                    for z in slots:
                        for i in range(1, H0, 2):
                            sp.wait_ge(z.s["qk_hi"], 2 * i + 2)
                            sp.dma_start(z.KS[D0:, i - 1:i + 1, :], z.KS[0:D0, i - 1:i + 1, :]).then_inc(z.s["k_copied"], 16)
                    for z in slots:
                        sp.wait_ge(z.s["qk_hi"], SLID["qk_hi"] + 2 * H2)
                        sp.dma_start(z.KS[D2:, 0:H2, :], z.KS[0:D2, 0:H2, :]).then_inc(z.s["k_copied"], 16)
                    for z in slots:
                        sp.wait_ge(z.s["acc_done"], 2 * (E + 1))
                        for t in range(NT):
                            n = P if t < NT - 1 else LAST
                            sp.dma_start(out[seq + z.q, P * t:P * t + n, :], z.h[0:n, t, :]).then_inc(out_stored, 16)
                    sp.wait_ge(out_stored, 2 * 16 * NT)

                @block.tensor
                def _(pe):
                    mm, tr = nc.tensor.matmul, nc.tensor.transpose

                    def mm3(to, a, b, start=True, stop=True):
                        mm(to, a[0], b[0], start=start, stop=False)
                        mm(to, a[0], b[1], start=False, stop=False)
                        return mm(to, a[1], b[0], start=False, stop=stop)

                    def weights(n, at):
                        return hi[n][at], lo[n][at]

                    def tdnn(z):
                        s = z.s
                        pe.wait_ge(s["x_hi"], 1)
                        pe.wait_ge(s["x_lo"], 1)
                        for t in range(NT):
                            to = bank[:, z.b, tile(t)]
                            mm(to, ones[:, 0:P], bias["tokb"][:], start=True, stop=False)
                            for k in range(TAPS):
                                at = slice(P * t + k, P * t + k + P)
                                i = mm3(to, (z.xT_hi[:, at], z.xT_lo[:, at]), weights("tokW", np.s_[:, k, :]),
                                        start=False, stop=k == TAPS - 1)
                        i.then_inc(s["tdnn_psum"], 1)
                        yield

                    def norm(k):
                        def stage(z):
                            pe.wait_ge(z.s["hn_ready"], k + 1)
                            for t in range(NT):
                                i = tr(bank[:, z.b + 1, tile(t)], z.hn[:, t, :], ident[:])
                            i.then_inc(z.s["hnT_psum"], 1)
                            yield
                        return stage

                    def await_hnT(z, k):
                        pe.wait_ge(z.s["hnT_hi"], k + 1)
                        pe.wait_ge(z.s["hnT_lo"], k + 1)
                        return z.hT_hi[:, INNER], z.hT_lo[:, INNER]

                    def qkv(z):
                        s = z.s
                        x = await_hnT(z, 0)
                        for i in range(H0):
                            if i >= 4:
                                pe.wait_ge(s["qk_hi"], 2 * (i - 3))
                                pe.wait_ge(s["qk_lo"], 2 * (i - 3))
                            mm3(bank[:, z.b + i % 4, 0:TP], weights("Wk" if i % 2 else "Wq", np.s_[:, tile(i // 2)]), x)\
                                .then_inc(s["qk_psum"], 1)
                            yield
                        for t in range(NT):
                            pe.wait_ge(s["qk_hi"], 2 * t + 10)
                            pe.wait_ge(s["qk_lo"], 2 * t + 10)
                            mm3(bank[:, z.b + t, :], (x[0][:, tile(t)], x[1][:, tile(t)]), weights("Wv", np.s_[:, :]))\
                                .then_inc(s["v_psum"], 1)
                            yield

                    def maxima(z):
                        s = z.s
                        pe.wait_ge(s["qk_hi"], 2 * H0)
                        pe.wait_ge(s["qk_lo"], 2 * H0)
                        pe.wait_ge(s["v_hi"], NT)
                        pe.wait_ge(s["v_lo"], NT)
                        for i in range(H0 * NT // 2):
                            if i >= 2:
                                pe.wait_ge(s["max_done"], i - 1)
                            for a in range(2):
                                hd, t = divmod(2 * i + a, NT)
                                n = mm(bank[:, z.b + 2 * (i % 2) + a, 0:T], z.QS[0:D0, hd, tile(t)], z.KS[0:D0, hd, 0:T],
                                       start=True, stop=True)
                            n.then_inc(s["smax_psum"], 1)
                            yield
                        pe.wait_ge(s["max_done"], H0 * NT // 2)
                        for t in range(NT):
                            i = tr(bank[0:H0 + 1, z.b, tile(t)], z.Mx[:, t::NT], ident[:])
                        i.then_inc(s["maxT_psum"], 1)
                        yield

                    def heads(z):
                        s = z.s
                        for i in range(H0 + 1):
                            if i < H0:
                                if i == 0:
                                    pe.wait_ge(s["negmax_ready"], 1)
                                    pe.wait_ge(s["q_copied"], H0)
                                    pe.wait_ge(s["k_copied"], 16 * H0 // 2)
                                else:
                                    pe.wait_ge(s["exp_done"], i)
                                for t in range(NT):
                                    mm(bank[:, z.b + t, 0:TP], z.KS[:, i, tile(t)], z.QS[:, i, :], start=True, stop=False)
                                    n = mm(bank[:, z.b + t, 0:TP], z.KB[:, i, tile(t)], z.QB[0:D0 + H0 + 1, i, :],
                                           start=False, stop=True)
                                n.then_inc(s["st_psum"], 1)
                            if i:
                                hd = i - 1
                                pe.wait_ge(s["p_hi"], i)
                                pe.wait_ge(s["p_lo"], i)
                                pe.wait_ge(s["p_lo_pool"], i)
                                if hd:
                                    pe.wait_ge(s["o_norm"], hd)
                                for t in range(NT):
                                    to = bank[:, z.b + 3, (D0 + 1) * t:(D0 + 1) * (t + 1)]
                                    for k in range(NT):
                                        m = P if k < NT - 1 else LAST
                                        n = mm3(to, (z.P_hi[0:m, hd % 2, k, tile(t)], z.P_lo[0:m, hd % 2, k, tile(t)]),
                                                (z.V_hi[0:m, k, hd, :], z.V_lo[0:m, k, hd, :]), start=k == 0, stop=k == NT - 1)
                                n.then_inc(s["pv_psum"], 1)
                            yield

                    def out0(z):
                        s = z.s
                        pe.wait_ge(s["o_norm"], H0)
                        for c in range(4):
                            for t in range(NT):
                                i = tr(bank[:, z.b + c, tile(t)],
                                       z.O[:, t, 2 * c:2 * c + 2, :].rearrange("p a d -> p (a d)"), ident[:])
                            i.then_inc(s["oT_psum"], 1)
                            yield
                        pe.wait_ge(s["oT_hi"], 4)
                        pe.wait_ge(s["oT_lo"], 4)
                        for t in range(NT):
                            for c in range(4):
                                i = mm3(bank[:, z.b, tile(t)], (z.OT_hi[:, c, tile(t)], z.OT_lo[:, c, tile(t)]),
                                        weights("Wo", np.s_[:, c, :]), start=c == 0, stop=c == 3)
                        i.then_inc(s["attn_psum"], 1)
                        yield

                    def experts(f):
                        def up(z, e, x):
                            for c in range(FC):
                                n = (E * f + e) * FC + c
                                if n - E * f * FC >= 3:
                                    pe.wait_ge(z.s["gelu_done"], n - 2)
                                mm3(bank[:, z.b + (e * FC + c) % 3, 0:TP], weights(f"m{f}_W1", np.s_[:, e, tile(c)]), x)\
                                    .then_inc(z.s["hid_psum"], 1)

                        def down(z, e):
                            n = E * f + e
                            pe.wait_ge(z.s["hid_hi"], FC * (n + 1))
                            pe.wait_ge(z.s["hid_lo"], (FC - 1) * (n + 1))
                            pe.wait_ge(z.s["hid_lo_pool"], n + 1)
                            pe.wait_ge(z.s["acc_done"], (E + 1) * f + e + 1)
                            for t in range(NT):
                                for c in range(FC):
                                    i = mm3(bank[:, z.b + 3, tile(t)],
                                            (z.H_hi[:, e % 2, c, tile(t)], z.H_lo[:, e % 2, c, tile(t)]),
                                            weights(f"m{f}_W2", np.s_[:, e, c, :]), start=c == 0, stop=c == FC - 1)
                            i.then_inc(z.s["down_psum"], 1)

                        def stage(z):
                            s = z.s
                            if f == 0:
                                x = await_hnT(z, 1)
                            else:
                                pe.wait_ge(s["y_hi"], 1)
                                pe.wait_ge(s["y_lo"], 1)
                                x = z.hT_hi[:, INNER], z.hT_lo[:, INNER]
                            for t in range(NT):
                                to = bank[:, z.b + 3, E * t:E * t + E]
                                mm(to, ones[:, 0:P], bias[f"m{f}_bg"][:], start=True, stop=False)
                                i = mm3(to, (x[0][:, tile(t)], x[1][:, tile(t)]), weights(f"m{f}_Wg", np.s_[:, :]), start=False)
                            i.then_inc(s["logits_psum"], 1)
                            up(z, 0, x)
                            yield
                            for e in range(E):
                                if e == 0:
                                    pe.wait_ge(s["gate_ready"], f + 1)
                                    for t in range(NT):
                                        i = tr(bank[0:E, z.b + 3, tile(t)], z.gate[:, t, :], ident[:])
                                    i.then_inc(s["gateT_psum"], 1)
                                if e + 1 < E:
                                    up(z, e + 1, x)
                                if e == 0:
                                    pe.wait_ge(s["gateT_ready"], f + 1)
                                    for t in range(NT):
                                        i = mm(bank[:, z.b + 3, tile(t)], z.gT[:, tile(t)], res[f"m{f}_b2"][:],
                                               start=True, stop=True)
                                    i.then_inc(s["b2_psum"], 1)
                                down(z, e)
                                yield
                        return stage

                    def bproj(z):
                        s = z.s
                        x = await_hnT(z, 2)
                        for i in range(4):
                            g = i % G1
                            mm(bank[:, z.b + i, 0:TP], bias["bqk1"][:, P * i:P * i + P], ones[:], start=True, stop=False)
                            mm3(bank[:, z.b + i, 0:TP], weights("Wq1" if i < G1 else "Wk1", np.s_[:, g, :]), x, start=False)\
                                .then_inc(s["qk_psum"], 1)
                            yield
                        for i in range(2):
                            pe.wait_ge(s["qk_hi"], FULL["qk_hi"] + i + 1)
                            pe.wait_ge(s["qk_lo"], FULL["qk_lo"] + i + 1)
                            for u in range(NT):
                                t, c = divmod(NT * i + u, 2)
                                at = slice(P * t + KC * c, P * t + KC * c + KC)
                                to = bank[0:KC, z.b + i, tile(u)]
                                mm(to, ones[:, 0:KC], bias["bv1"][:], start=True, stop=False)
                                n = mm3(to, (z.hT_hi[:, at], z.hT_lo[:, at]), weights("Wv1", np.s_[:, :]), start=False)
                            n.then_inc(s["v_psum"], 1)
                            yield

                    def bmax(z):
                        s = z.s
                        pe.wait_ge(s["qk_hi"], FULL["qk_hi"] + 4)
                        pe.wait_ge(s["qk_lo"], FULL["qk_lo"] + 4)
                        pe.wait_ge(s["bqz_ready"], 1)
                        pe.wait_ge(s["margins_set"], 1)
                        for t in range(NT):
                            for pair in range(4):
                                u = 4 * t + pair
                                if u == 2:
                                    pe.wait_ge(s["v_hi"], FULL["v_hi"] + 2)
                                    pe.wait_ge(s["v_lo"], FULL["v_lo"] + 2)
                                if u >= 4:
                                    pe.wait_ge(s["max_done"], FULL["max_done"] + u - 3)
                                to = bank[:, z.b + (u + 2) % 4, 0:2 * WIN]
                                mm(to, identb[:], mask["c_band_q"][:, t, :].unsqueeze(1).to_broadcast([P, 2, WIN]),
                                   start=True, stop=True)
                                for a in range(2):
                                    g, j = divmod(2 * pair + a, J1)
                                    n = mm(bank[:, z.b + (u + 2) % 4, WIN * a:WIN * a + WIN], z.qz_hi[:, g, j, tile(t)],
                                           z.k1_hi[:, g, P * t:P * t + WIN], start=False, stop=True, skip_group_check=True)
                                n.then_inc(s["smax_psum"], 1)
                            yield
                        pe.wait_ge(s["max_done"], FULL["max_done"] + 4 * NT)
                        for g in range(G1):
                            for t in range(NT):
                                i = tr(bank[:, z.b + g, tile(t)], z.Mexp[:, t, g, :], ident[:])
                        i.then_inc(s["maxT_psum"], 1)
                        yield

                    def bheads(z):
                        s = z.s
                        pe.wait_ge(s["bq2_ready"], 1)
                        for t in range(NT + 1):
                            if t < NT:
                                for c in range(2):
                                    for g in range(G1):
                                        u = 4 * t + 2 * c + g
                                        if u >= 3:
                                            pe.wait_ge(s["exp_done"], FULL["exp_done"] + u - 2)
                                        to = bank[0:KC, z.b + u % 3, :]
                                        keys = slice(P * t + KC * c, P * t + KC * c + KC)
                                        mm(to, identb[0:KC, 0:KC],
                                           mask["c_band_k"][:, t, c, :].unsqueeze(1).to_broadcast([KC, J1, P]),
                                           start=True, stop=False)
                                        mm(to, z.k1_hi[:, g, keys], z.qz_st[:, g, :, tile(t)], start=False, stop=False)
                                        mm(to, z.k1_lo[:, g, keys], z.qz_m[:, g, :, tile(t)], start=False, stop=True)\
                                            .then_inc(s["st_psum"], 1)
                            if t:
                                pe.wait_ge(s["p_hi"], FULL["p_hi"] + 4 * t)
                                pe.wait_ge(s["p_lo"], FULL["p_lo"] + 3 * t)
                                pe.wait_ge(s["p_lo_pool"], FULL["p_lo_pool"] + t)
                                if t > 1:
                                    pe.wait_ge(s["o_norm"], FULL["o_norm"] + t - 1)
                                for hd in range(H1):
                                    g, j = divmod(hd, J1)
                                    for c in range(2):
                                        u = 4 * (t - 1) + 2 * c + g
                                        i = mm3(bank[:, z.b + 3, (D1 + 1) * hd:(D1 + 1) * (hd + 1)],
                                                (z.P1_hi[:, u % RING, tile(j)], z.P1_lo[:, u % RING, tile(j)]),
                                                (z.V1_hi[:, 2 * (t - 1) + c, hd, :], z.V1_lo[:, 2 * (t - 1) + c, hd, :]),
                                                start=c == 0, stop=c == 1)
                                i.then_inc(s["pv_psum"], 1)
                            yield

                    def bout(z):
                        s = z.s
                        pe.wait_ge(s["o_norm"], FULL["o_norm"] + NT)
                        for t in range(NT):
                            i = tr(bank[:, z.b, tile(t)], z.O1[:, t, :, :].rearrange("p a d -> p (a d)"), ident[:])
                        i.then_inc(s["oT_psum"], 1)
                        yield
                        pe.wait_ge(s["oT_hi"], FULL["oT_hi"] + 1)
                        pe.wait_ge(s["oT_lo"], FULL["oT_lo"] + 1)
                        for t in range(NT):
                            mm(bank[:, z.b + 1, tile(t)], ones[:, 0:P], bias["bp1"][:], start=True, stop=False)
                            i = mm3(bank[:, z.b + 1, tile(t)], (z.O1T_hi[:, tile(t)], z.O1T_lo[:, tile(t)]),
                                    weights("Wp1", np.s_[:, :]), start=False)
                        i.then_inc(s["attn_psum"], 1)
                        yield

                    def cproj(z):
                        s = z.s
                        x = await_hnT(z, 3)
                        for t in range(NT):
                            mm3(bank[:, z.b + t, 0:3 * C], (x[0][:, tile(t)], x[1][:, tile(t)]),
                                weights("Wqkv2", np.s_[:, :])).then_inc(s["v_psum"], 1)
                        yield
                        pe.wait_ge(s["cqk_ready"], 1)
                        pe.wait_ge(s["v_hi"], SLID["v_hi"] + NT)
                        for which in range(2):
                            for t in range(NT):
                                i = tr(bank[:, z.b + (0 if which else 3), tile(t)],
                                       z.qk[:, t, 2 * which:2 * which + 2, :].rearrange("p a d -> p (a d)"), ident[:])
                            i.then_inc(s["cqkT_psum"], 1)
                        yield

                    def cmax(z):
                        s = z.s
                        pe.wait_ge(s["qk_hi"], SLID["qk_hi"] + 4)
                        pe.wait_ge(s["qk_lo"], SLID["qk_lo"] + 4)
                        for u in range(H2 * NT):
                            hd, t = divmod(u, NT)
                            if u >= 4:
                                pe.wait_ge(s["max_done"], SLID["max_done"] + u - 3)
                            L, b = P * (t + 1), z.b + (u + 1) % 4
                            mm(bank[:, b, 0:L], z.QS[0:D2, hd, tile(t)], z.KS[0:D2, hd, 0:L], start=True, stop=True)
                            mm(bank[:, b, tile(t)], identb[:], mask["c_later_q"][:], start=False, stop=True,
                               skip_group_check=True).then_inc(s["smax_psum"], 1)
                        yield
                        pe.wait_ge(s["max_done"], SLID["max_done"] + H2 * NT)
                        for t in range(NT):
                            i = tr(bank[0:H2, z.b, tile(t)], z.Mx[:, t:H2 * NT:NT], ident[:])
                        i.then_inc(s["maxT_psum"], 1)
                        yield

                    def cheads(z):
                        s = z.s
                        for i in range(H2 + 1):
                            if i < H2:
                                if i == 0:
                                    pe.wait_ge(s["negmax_ready"], SLID["negmax_ready"] + 1)
                                    pe.wait_ge(s["q_copied"], SLID["q_copied"] + H2)
                                    pe.wait_ge(s["k_copied"], SLID["k_copied"] + 16)
                                else:
                                    pe.wait_ge(s["exp_done"], SLID["exp_done"] + NT)
                                for k in range(NT):
                                    to = bank[:, z.b + k, P * k:TP]
                                    mm(to, z.KS[:, i, tile(k)], z.QS[:, i, P * k:TP], start=True, stop=True)
                                    mm(to, z.KB[0:D2 + H2, i, tile(k)], z.QB[0:D2 + H2, i, P * k:TP], start=False,
                                       stop=True, skip_group_check=True)
                                    mm(bank[:, z.b + k, tile(k)], identb[:], mask["c_later_k"][:], start=False, stop=True,
                                       skip_group_check=True).then_inc(s["st_psum"], 1)
                            if i:
                                hd = i - 1
                                pe.wait_ge(s["p_lo"], SLID["p_lo"] + NT * i)
                                if hd:
                                    pe.wait_ge(s["o_norm"], SLID["o_norm"] + hd)
                                for t in range(NT):
                                    for k in range(t + 1):
                                        n = mm3(bank[:, z.b + 3, (D2 + 1) * t:(D2 + 1) * (t + 1)],
                                                (z.P_hi[:, hd, k, tile(t)], z.P_lo[:, hd, k, tile(t)]),
                                                (z.V_hi[:, k, hd, :], z.V_lo[:, k, hd, :]), start=k == 0, stop=k == t)
                                n.then_inc(s["pv_psum"], 1)
                            yield

                    def cout(z):
                        s = z.s
                        pe.wait_ge(s["o_norm"], SLID["o_norm"] + H2)
                        for t in range(NT):
                            i = tr(bank[:, z.b, tile(t)], z.O[:, t, 0:H2, :].rearrange("p a d -> p (a d)"), ident[:])
                        i.then_inc(s["oT_psum"], 1)
                        yield
                        pe.wait_ge(s["oT_hi"], SLID["oT_hi"] + 1)
                        pe.wait_ge(s["oT_lo"], SLID["oT_lo"] + 1)
                        mm3(bank[:, z.b + 1, 0:TP], weights("Wo2", np.s_[:, :]), (z.OT_hi[:, 0, :], z.OT_lo[:, 0, :]))\
                            .then_inc(s["y_psum"], 1)
                        yield

                    side_by_side({"tdnn": tdnn, "norm0": norm(0), "norm1": norm(1), "norm2": norm(2), "norm3": norm(3),
                                  "qkv": qkv, "maxima": maxima, "heads": heads, "out0": out0, "experts0": experts(0),
                                  "bproj": bproj, "bmax": bmax, "bheads": bheads, "bout": bout, "cproj": cproj,
                                  "cmax": cmax, "cheads": cheads, "cout": cout, "experts1": experts(1)}, slots)

                @block.scalar
                def _(act):
                    fn = nc.scalar.activation

                    def tdnn(z):
                        act.wait_ge(z.s["x_loaded"], 16)
                        fn(z.xT_hi[:, 0:T_IN], z.xf[:, 0:T_IN], ACT.Copy).then_inc(z.s["x_hi"], 1)
                        act.wait_ge(z.s["tdnn_psum"], 1)
                        fn(z.h[:], tiles(bank[:, z.b, 0:TP]), ACT.Relu).then_inc(z.s["h_ready"], 1)
                        yield

                    def norm(k):
                        def stage(z):
                            act.wait_ge(z.s["hnT_psum"], k + 1)
                            fn(z.hT_hi[:, INNER], bank[:, z.b + 1, 0:TP], ACT.Copy).then_inc(z.s["hnT_hi"], 1)
                            yield
                        return stage

                    def qkv(z):
                        for i in range(H0):
                            act.wait_ge(z.s["qk_psum"], i + 1)
                            for a in range(2):
                                fn((z.KS if i % 2 else z.QS)[0:D0, 2 * (i // 2) + a, :],
                                   bank[D0 * a:D0 * a + D0, z.b + i % 4, 0:TP], ACT.Copy).then_inc(z.s["qk_hi"], 1)
                            yield
                        for t in range(NT):
                            act.wait_ge(z.s["v_psum"], t + 1)
                            fn(z.V_hi[:, t, :, 0:D0], bank[:, z.b + t, :].rearrange("p (a d) -> p a d", a=H0), ACT.Copy)\
                                .then_inc(z.s["v_hi"], 1)
                            yield

                    def maxima(z):
                        for i in range(H0 * NT // 2):
                            yield
                        act.wait_ge(z.s["maxT_psum"], 1)
                        fn(z.QB[D0:D0 + H0 + 1, :, :],
                           bank[0:H0 + 1, z.b, 0:TP].unsqueeze(1).to_broadcast([H0 + 1, H0, TP]),
                           ACT.Copy, scale=-1.0).then_inc(z.s["negmax_ready"], 1)
                        yield

                    def heads(z):
                        for i in range(H0):
                            act.wait_ge(z.s["st_psum"], i + 1)
                            if i:
                                act.wait_ge(z.s["p_lo"], i)
                                act.wait_ge(z.s["p_lo_pool"], i)
                            fn(z.Pf[:], bank[:, z.b:z.b + NT, 0:TP], ACT.Exp, scale=ROOT).then_inc(z.s["exp_done"], 1)
                            yield
                        yield

                    def out0(z):
                        for c in range(4):
                            act.wait_ge(z.s["oT_psum"], c + 1)
                            fn(z.OT_hi[:, c, :], bank[:, z.b + c, 0:TP], ACT.Copy).then_inc(z.s["oT_hi"], 1)
                            yield
                        yield

                    def experts(f):
                        def gelus(z, e):
                            n = E * f + e
                            for c in range(FC):
                                act.wait_ge(z.s["hid_psum"], FC * n + c + 1)
                                if n:
                                    if c < FC - 1:
                                        act.wait_ge(z.s["hid_lo"], (FC - 1) * (n - 1) + c + 1)
                                    else:
                                        act.wait_ge(z.s["hid_lo_pool"], n)
                                fn(z.Hf[:, c, :], bank[:, z.b + (FC * e + c) % 3, 0:TP],
                                   ACT.Gelu_apprx_tanh if f else ACT.Gelu, bias=res[f"m{f}_b1"][:, e, c:c + 1])\
                                    .then_inc(z.s["gelu_done"], 1)

                        def stage(z):
                            s = z.s
                            act.wait_ge(s["logits_shift"], f + 1)
                            fn(z.ge[:], z.lm[:], ACT.Exp).then_inc(s["gate_exp"], 1)
                            gelus(z, 0)
                            yield
                            act.wait_ge(s["gateT_psum"], f + 1)
                            fn(z.gT, bank[0:E, z.b + 3, 0:TP], ACT.Copy).then_inc(s["gateT_ready"], 1)
                            for e in range(1, E):
                                gelus(z, e)
                                yield
                            yield
                        return stage

                    def bproj(z):
                        for i in range(4):
                            act.wait_ge(z.s["qk_psum"], FULL["qk_psum"] + i + 1)
                            to = z.q1_hi[:, i, :] if i < G1 else z.k1_hi[:, i - G1, INNER]
                            fn(to, bank[:, z.b + i, 0:TP], ACT.Copy).then_inc(z.s["qk_hi"], 1)
                            yield
                        for i in range(2):
                            act.wait_ge(z.s["v_psum"], FULL["v_psum"] + i + 1)
                            for u in range(NT):
                                n = fn(z.V1_hi[:, NT * i + u, :, 0:D1],
                                       bank[0:KC, z.b + i, tile(u)].rearrange("p (a d) -> p a d", a=H1), ACT.Copy)
                            n.then_inc(z.s["v_hi"], 1)
                            yield

                    def bmax(z):
                        for t in range(NT + 1):
                            yield

                    def bheads(z):
                        for t in range(NT):
                            for u in range(4 * t, 4 * t + 4):
                                act.wait_ge(z.s["st_psum"], FULL["st_psum"] + u + 1)
                                if u >= 2:
                                    act.wait_ge(z.s["p_lo"], FULL["p_lo"] + sum(x % 4 != 3 for x in range(u - 1)))
                                    if u >= 5:
                                        act.wait_ge(z.s["p_lo_pool"], FULL["p_lo_pool"] + sum(x % 4 == 3 for x in range(u - 1)))
                                fn(z.P1f[:, u % 2, :], bank[0:KC, z.b + u % 3, :], ACT.Exp, scale=D1 ** -0.5)\
                                    .then_inc(z.s["exp_done"], 1)
                            yield
                        yield

                    def bout(z):
                        act.wait_ge(z.s["oT_psum"], FULL["oT_psum"] + 1)
                        fn(z.O1T_hi, bank[:, z.b, 0:TP], ACT.Copy).then_inc(z.s["oT_hi"], 1)
                        yield
                        yield

                    def cproj(z):
                        for t in range(NT):
                            act.wait_ge(z.s["v_psum"], SLID["v_psum"] + t + 1)
                            fn(z.sq[:, t, :], bank[:, z.b + t, 0:2 * C], ACT.Square).then_inc(z.s["csq"], 1)
                            fn(z.V_hi[:, t, 0:H2, 0:D2], bank[:, z.b + t, 2 * C:3 * C].rearrange("p (a d) -> p a d", a=H2),
                               ACT.Copy).then_inc(z.s["v_hi"], 1)
                        yield
                        for which in range(2):
                            act.wait_ge(z.s["cqkT_psum"], which + 1)
                            for a in range(H2):
                                fn((z.KS if which else z.QS)[0:D2, a, :],
                                   bank[D2 * a:D2 * a + D2, z.b + (0 if which else 3), 0:TP], ACT.Copy)\
                                    .then_inc(z.s["qk_hi"], 1)
                        yield

                    def cmax(z):
                        yield
                        act.wait_ge(z.s["maxT_psum"], SLID["maxT_psum"] + 1)
                        fn(z.QB[D2:D2 + H2, 0:H2, :], bank[0:H2, z.b, 0:TP].unsqueeze(1).to_broadcast([H2, H2, TP]),
                           ACT.Copy, scale=-1.0).then_inc(z.s["negmax_ready"], 1)
                        yield

                    def cheads(z):
                        for i in range(H2):
                            for k in range(NT):
                                act.wait_ge(z.s["st_psum"], SLID["st_psum"] + NT * i + k + 1)
                                if i:
                                    act.wait_ge(z.s["p_lo"], SLID["p_lo"] + k + 1)
                                fn(z.Pf[:, k, P * k:TP], bank[:, z.b + k, P * k:TP], ACT.Exp, scale=float(D2) ** 0.5)\
                                    .then_inc(z.s["exp_done"], 1)
                            yield
                        yield

                    def cout(z):
                        act.wait_ge(z.s["oT_psum"], SLID["oT_psum"] + 1)
                        fn(z.OT_hi[:, 0, :], bank[:, z.b, 0:TP], ACT.Copy).then_inc(z.s["oT_hi"], 1)
                        yield
                        act.wait_ge(z.s["y_psum"], 1)
                        fn(z.hT_hi[:, INNER], bank[:, z.b + 1, 0:TP], ACT.Copy).then_inc(z.s["y_hi"], 1)
                        yield

                    side_by_side({"tdnn": tdnn, "norm0": norm(0), "norm1": norm(1), "norm2": norm(2), "norm3": norm(3),
                                  "qkv": qkv, "maxima": maxima, "heads": heads, "out0": out0, "experts0": experts(0),
                                  "bproj": bproj, "bmax": bmax, "bheads": bheads, "bout": bout, "cproj": cproj,
                                  "cmax": cmax, "cheads": cheads, "cout": cout, "experts1": experts(1)}, slots)

                @block.vector
                def _(dve):
                    v = nc.vector
                    steps = [0, 0]

                    def link(z, i):
                        steps[z.q] += 1
                        i.then_inc(z.s["vector_step"], 1)
                        dve.wait_ge(z.s["vector_step"], steps[z.q])

                    def lower(to, x, high):
                        return v.tensor_tensor(to, x, high, ALU.subtract)

                    def rsqrt(z, x, n):
                        y, other = z.guess[:, 0:n], z.rstd[:, 0:n]
                        link(z, v.tensor_scalar(y.bitcast(I32), x.bitcast(I32), -0.5, 1597463007.0, ALU.mult, ALU.add))
                        for _ in range(3):
                            link(z, v.scalar_tensor_tensor(z.n1[:, 0:n], y, -0.5, y, ALU.mult, ALU.mult))
                            link(z, v.tensor_tensor(z.n2[:, 0:n], z.n1[:, 0:n], x, ALU.mult))
                            link(z, v.scalar_tensor_tensor(other, z.n2[:, 0:n], 1.5, y, ALU.add, ALU.mult))
                            y, other = other, y

                    def tdnn(z):
                        dve.wait_ge(z.s["x_loaded"], 16)
                        dve.wait_ge(z.s["x_hi"], 1)
                        lower(z.xT_lo[:, 0:T_IN], z.xf[:, 0:T_IN], z.xT_hi[:, 0:T_IN]).then_inc(z.s["x_lo"], 1)
                        yield

                    def norm(k):
                        def stage(z):
                            if k == 0:
                                dve.wait_ge(z.s["h_ready"], 1)
                            for t in range(NT):
                                i = v.bn_stats(z.stats[:, t, :], z.h[:, t, :])
                            link(z, i)
                            for t in range(NT):
                                i = v.bn_aggr(z.mv[:, t, :], z.stats[:, t, :])
                            link(z, i)
                            link(z, v.tensor_scalar(z.ve[:, 0:NT], z.mv[:, :, 1], 1e-5, None, ALU.add))
                            rsqrt(z, z.ve[:, 0:NT], NT)
                            for t in range(NT):
                                i = v.tensor_scalar(z.hn[:, t, :], z.h[:, t, :], z.mv[:, t, 0:1], z.rstd[:, t:t + 1],
                                                    ALU.subtract, ALU.mult)
                            if k == 3:
                                link(z, i)
                                link(z, v.tensor_tensor(z.hn[:], z.hn[:], res["lng"][:].unsqueeze(1)
                                                        .to_broadcast([P, NT, C]), ALU.mult))
                                i = v.tensor_tensor(z.hn[:], z.hn[:], res["lnb"][:].unsqueeze(1)
                                                    .to_broadcast([P, NT, C]), ALU.add)
                            i.then_inc(z.s["hn_ready"], 1)
                            if k == 0:
                                dve.wait_ge(z.s["hn_ready"], 1)
                                link(z, v.tensor_tensor(z.h[:], z.h[:], z.hn[:], ALU.add))
                            dve.wait_ge(z.s["hnT_psum"], k + 1)
                            dve.wait_ge(z.s["hnT_hi"], k + 1)
                            lower(z.hT_lo[:, INNER], bank[:, z.b + 1, 0:TP], z.hT_hi[:, INNER]).then_inc(z.s["hnT_lo"], 1)
                            yield
                        return stage

                    def add_to_h(z, b):
                        link(z, v.tensor_tensor(z.h[:], tiles(bank[:, z.b + b, 0:TP]), z.h[:], ALU.add))

                    def qkv(z):
                        s = z.s
                        for i in range(H0):
                            for a in range(2):
                                hd = 2 * (i // 2) + a
                                dve.wait_ge(s["qk_hi"], 2 * i + a + 1)
                                to = z.KB[0:D0, hd, :] if i % 2 else z.QS[D0:, hd, :]
                                lower(to, bank[D0 * a:D0 * a + D0, z.b + i % 4, 0:TP], (z.KS if i % 2 else z.QS)[0:D0, hd, :])\
                                    .then_inc(s["qk_lo"], 1)
                            yield
                        for t in range(NT):
                            dve.wait_ge(s["v_hi"], t + 1)
                            lower(z.V_lo[:, t, :, 0:D0], bank[:, z.b + t, :].rearrange("p (a d) -> p a d", a=H0),
                                  z.V_hi[:, t, :, 0:D0]).then_inc(s["v_lo"], 1)
                            yield

                    def maxima(z):
                        for i in range(H0 * NT // 2):
                            dve.wait_ge(z.s["smax_psum"], i + 1)
                            b = z.b + 2 * (i % 2)
                            v.tensor_reduce(z.Mx[:, 2 * i:2 * i + 2], bank[:, b:b + 2, 0:T], AX, ALU.max)\
                                .then_inc(z.s["max_done"], 1)
                            yield
                        yield

                    def normalise(z, to, b, n, d, sem):
                        x = bank[:, b, 0:n * (d + 1)].rearrange("p (a d) -> p a d", a=n)
                        link(z, v.reciprocal(z.rec[:, 0:n], x[:, :, d]))
                        v.tensor_tensor(to, x[:, :, 0:d], z.rec[:, 0:n].unsqueeze(2).to_broadcast([P, n, d]), ALU.mult)\
                            .then_inc(sem, 1)

                    def heads(z):
                        s = z.s
                        yield
                        for hd in range(H0):
                            dve.wait_ge(s["exp_done"], hd + 1)
                            if hd >= 2:
                                dve.wait_ge(s["pv_psum"], hd - 1)
                            v.tensor_copy(z.P_hi[:, hd % 2, :, :], z.Pf[:]).then_inc(s["p_hi"], 1)
                            if hd:
                                dve.wait_ge(s["pv_psum"], hd)
                                if hd > 1:
                                    dve.wait_ge(s["o_norm"], hd - 1)
                                normalise(z, z.O[:, :, hd - 1, :], z.b + 3, NT, D0, s["o_norm"])
                            dve.wait_ge(s["p_hi"], hd + 1)
                            lower(z.P_lo[:, hd % 2, 0:2, :], z.Pf[:, 0:2, :], z.P_hi[:, hd % 2, 0:2, :]).then_inc(s["p_lo"], 1)
                            yield

                    def out0(z):
                        s = z.s
                        dve.wait_ge(s["pv_psum"], H0)
                        dve.wait_ge(s["o_norm"], H0 - 1)
                        normalise(z, z.O[:, :, H0 - 1, :], z.b + 3, NT, D0, s["o_norm"])
                        for c in range(4):
                            dve.wait_ge(s["oT_hi"], c + 1)
                            lower(z.OT_lo[:, c, :], bank[:, z.b + c, 0:TP], z.OT_hi[:, c, :]).then_inc(s["oT_lo"], 1)
                            yield
                        dve.wait_ge(s["attn_psum"], 1)
                        add_to_h(z, 0)
                        yield

                    def experts(f):
                        def per_tile(x):
                            return x[:].unsqueeze(2).to_broadcast([P, NT, E])

                        def split(z, e):
                            n = E * f + e
                            if e >= 2:
                                dve.wait_ge(z.s["down_psum"], n - 1)
                            for c in range(FC):
                                dve.wait_ge(z.s["gelu_done"], FC * n + c + 1)
                                v.tensor_copy(z.H_hi[:, e % 2, c, :], z.Hf[:, c, :]).then_inc(z.s["hid_hi"], 1)
                                if c:
                                    dve.wait_ge(z.s["hid_hi"], FC * n + c)
                                    lower(z.H_lo[:, e % 2, c - 1, :], z.Hf[:, c - 1, :], z.H_hi[:, e % 2, c - 1, :])\
                                        .then_inc(z.s["hid_lo"], 1)

                        def gates(z):
                            s = z.s
                            dve.wait_ge(s["logits_psum"], f + 1)
                            lg = bank[:, z.b + 3, 0:NT * E].rearrange("p (t e) -> p t e", t=NT)
                            link(z, v.tensor_reduce(z.gm[:], lg, AX, ALU.max))
                            v.tensor_tensor(z.lm[:], lg, per_tile(z.gm), ALU.subtract).then_inc(s["logits_shift"], 1)
                            dve.wait_ge(s["gate_exp"], f + 1)
                            link(z, v.tensor_reduce(z.gs[:], z.ge[:], AX, ALU.add))
                            link(z, v.reciprocal(z.gr[:], z.gs[:]))
                            if f == 0:
                                link(z, v.scalar_tensor_tensor(z.ga[:], z.lm[:], 0.0, res["c_rank"][:], ALU.is_equal, ALU.mult))
                                link(z, v.tensor_reduce(z.gb[:], z.ga[:], AX, ALU.max))
                                link(z, v.tensor_tensor(z.ga[:], z.ga[:], per_tile(z.gb), ALU.is_equal))
                                v.tensor_tensor(z.gate[:], z.ga[:], per_tile(z.gr), ALU.mult).then_inc(s["gate_ready"], 1)
                            else:
                                v.tensor_tensor(z.gate[:], z.ge[:], per_tile(z.gr), ALU.mult).then_inc(s["gate_ready"], 1)

                        def stage(z):
                            s = z.s
                            base = (E + 1) * f
                            gates(z)
                            split(z, 0)
                            yield
                            for e in range(E):
                                if e + 1 < E:
                                    split(z, e + 1)
                                if e == 0:
                                    dve.wait_ge(s["b2_psum"], f + 1)
                                    v.tensor_tensor(z.h[:], tiles(bank[:, z.b + 3, 0:TP]), z.h[:], ALU.add)\
                                        .then_inc(s["acc_done"], 1)
                                dve.wait_ge(s["down_psum"], E * f + e + 1)
                                dve.wait_ge(s["acc_done"], base + e + 1)
                                for t in range(NT):
                                    i = v.scalar_tensor_tensor(z.h[:, t, :], bank[:, z.b + 3, tile(t)], z.gate[:, t, e:e + 1],
                                                               z.h[:, t, :], ALU.mult, ALU.add)
                                i.then_inc(s["acc_done"], 1)
                                yield
                            dve.wait_ge(s["acc_done"], base + E + 1)
                        return stage

                    def bproj(z):
                        s = z.s
                        rows = res["c_rows"]
                        for i in range(4):
                            dve.wait_ge(s["qk_hi"], FULL["qk_hi"] + i + 1)
                            x = bank[:, z.b + i, 0:TP]
                            if i < G1:
                                v.scalar_tensor_tensor(z.q1_st[:, i, :], z.q1_hi[:, i, :], rows[:, 0:1], x, ALU.mult,
                                                       ALU.add).then_inc(s["qk_lo"], 1)
                            else:
                                lower(z.k1_d[:, i - G1, :], x, z.k1_hi[:, i - G1, INNER]).then_inc(s["qk_lo"], 1)
                            yield
                        dve.wait_ge(s["qk_lo"], FULL["qk_lo"] + 4)
                        v.tensor_scalar(z.k1_lo[:, :, INNER], z.k1_d[:], rows[:, 1:2], rows[:, 2:3], ALU.mult, ALU.add)
                        for j in range(J1):
                            v.tensor_scalar(z.qz_st[:, :, j, :], z.q1_st[:], res["c_heads"][:, j:j + 1], None, ALU.mult)
                            i = v.tensor_scalar(z.qz_hi[:, :, j, :], z.q1_hi[:], res["c_heads"][:, j:j + 1], rows[:, 1:2],
                                                ALU.mult, ALU.mult)
                        i.then_inc(s["bqz_ready"], 1)
                        for i in range(2):
                            dve.wait_ge(s["v_hi"], FULL["v_hi"] + i + 1)
                            for u in range(NT):
                                n = lower(z.V1_lo[:, NT * i + u, :, 0:D1],
                                          bank[0:KC, z.b + i, tile(u)].rearrange("p (a d) -> p a d", a=H1),
                                          z.V1_hi[:, NT * i + u, :, 0:D1])
                            n.then_inc(s["v_lo"], 1)
                            yield

                    def bmax(z):
                        s = z.s
                        dve.wait_ge(s["margins_set"], 1)
                        for t in range(NT):
                            for pair in range(4):
                                u = 4 * t + pair
                                dve.wait_ge(s["smax_psum"], FULL["smax_psum"] + u + 1)
                                g, j = divmod(2 * pair, J1)
                                v.tensor_reduce(z.Mexp[:, t, g, 32 * j + M_ROW:32 * j + M_ROW + 33:32],
                                                bank[:, z.b + (u + 2) % 4, 0:2 * WIN].rearrange("p (a n) -> p a n", a=2),
                                                AX, ALU.max).then_inc(s["max_done"], 1)
                            yield
                        dve.wait_ge(s["maxT_psum"], FULL["maxT_psum"] + 1)
                        link(z, v.scalar_tensor_tensor(z.q1_m[:], z.q1_hi[:], res["c_rows"][:, 1:2],
                                                       bank[:, z.b:z.b + G1, 0:TP], ALU.mult, ALU.subtract))
                        for j in range(J1):
                            i = v.tensor_scalar(z.qz_m[:, :, j, :], z.q1_m[:], res["c_heads"][:, j:j + 1], None, ALU.mult)
                        i.then_inc(s["bq2_ready"], 1)
                        yield

                    def bheads(z):
                        s = z.s
                        for t in range(NT + 1):
                            if t < NT:
                                for u in range(4 * t, 4 * t + 4):
                                    dve.wait_ge(s["exp_done"], FULL["exp_done"] + u + 1)
                                    if u >= RING:
                                        dve.wait_ge(s["pv_psum"], FULL["pv_psum"] + (u - RING) // 4 + 1)
                                    v.tensor_copy(z.P1_hi[:, u % RING, :], z.P1f[:, u % 2, :]).then_inc(s["p_hi"], 1)
                                    if u % 4 != 3:
                                        dve.wait_ge(s["p_hi"], FULL["p_hi"] + u + 1)
                                        lower(z.P1_lo[:, u % RING, :], z.P1f[:, u % 2, :], z.P1_hi[:, u % RING, :])\
                                            .then_inc(s["p_lo"], 1)
                            if t:
                                dve.wait_ge(s["pv_psum"], FULL["pv_psum"] + t)
                                if t > 1:
                                    dve.wait_ge(s["o_norm"], FULL["o_norm"] + t - 1)
                                normalise(z, z.O1[:, t - 1, :, :], z.b + 3, H1, D1, s["o_norm"])
                            yield

                    def bout(z):
                        dve.wait_ge(z.s["oT_hi"], FULL["oT_hi"] + 1)
                        lower(z.O1T_lo, bank[:, z.b, 0:TP], z.O1T_hi).then_inc(z.s["oT_lo"], 1)
                        yield
                        dve.wait_ge(z.s["attn_psum"], FULL["attn_psum"] + 1)
                        add_to_h(z, 1)
                        yield

                    def cproj(z):
                        s = z.s
                        for t in range(NT):
                            dve.wait_ge(s["v_hi"], SLID["v_hi"] + t + 1)
                            lower(z.V_lo[:, t, 0:H2, 0:D2], bank[:, z.b + t, 2 * C:3 * C].rearrange("p (a d) -> p a d", a=H2),
                                  z.V_hi[:, t, 0:H2, 0:D2]).then_inc(s["v_lo"], 1)
                        dve.wait_ge(s["csq"], NT)
                        link(z, v.tensor_reduce(z.ve[:], z.sq.rearrange("p t (a d) -> p (t a) d", a=4), AX, ALU.add))
                        link(z, v.tensor_scalar(z.ve[:], z.ve[:], 1e-12, None, ALU.add))
                        rsqrt(z, z.ve[:], 4 * NT)
                        for t in range(NT):
                            i = v.tensor_tensor(z.qk[:, t, :, :], bank[:, z.b + t, 0:2 * C].rearrange("p (a d) -> p a d", a=4),
                                                z.rstd[:, 4 * t:4 * t + 4].unsqueeze(2).to_broadcast([P, 4, D2]), ALU.mult)
                        link(z, i)
                        for t in range(NT):
                            i = v.tensor_tensor(z.qk[:, t, :, :], z.qk[:, t, :, :], res["qkg"][:], ALU.mult)
                        i.then_inc(s["cqk_ready"], 1)
                        yield
                        for which in range(2):
                            for a in range(H2):
                                dve.wait_ge(s["qk_hi"], SLID["qk_hi"] + 2 * which + a + 1)
                                to = z.KB[0:D2, a, :] if which else z.QS[D2:, a, :]
                                lower(to, bank[D2 * a:D2 * a + D2, z.b + (0 if which else 3), 0:TP],
                                      (z.KS if which else z.QS)[0:D2, a, :]).then_inc(s["qk_lo"], 1)
                        yield

                    def cmax(z):
                        for u in range(H2 * NT):
                            dve.wait_ge(z.s["smax_psum"], SLID["smax_psum"] + u + 1)
                            v.tensor_reduce(z.Mx[:, u:u + 1], bank[:, z.b + (u + 1) % 4, 0:P * (u % NT + 1)], AX, ALU.max)\
                                .then_inc(z.s["max_done"], 1)
                        yield
                        yield

                    def cheads(z):
                        s = z.s
                        yield
                        for hd in range(H2):
                            for k in range(NT):
                                dve.wait_ge(s["exp_done"], SLID["exp_done"] + NT * hd + k + 1)
                                link(z, v.tensor_copy(z.P_hi[:, hd, k, P * k:TP], z.Pf[:, k, P * k:TP]))
                                lower(z.P_lo[:, hd, k, P * k:TP], z.Pf[:, k, P * k:TP], z.P_hi[:, hd, k, P * k:TP])\
                                    .then_inc(s["p_lo"], 1)
                            dve.wait_ge(s["pv_psum"], SLID["pv_psum"] + hd + 1)
                            if hd:
                                dve.wait_ge(s["o_norm"], SLID["o_norm"] + hd)
                            normalise(z, z.O[:, :, hd, :], z.b + 3, NT, D2, s["o_norm"])
                            yield

                    def cout(z):
                        dve.wait_ge(z.s["oT_hi"], SLID["oT_hi"] + 1)
                        lower(z.OT_lo[:, 0, :], bank[:, z.b, 0:TP], z.OT_hi[:, 0, :]).then_inc(z.s["oT_lo"], 1)
                        yield
                        dve.wait_ge(z.s["y_hi"], 1)
                        lower(z.hT_lo[:, INNER], bank[:, z.b + 1, 0:TP], z.hT_hi[:, INNER]).then_inc(z.s["y_lo"], 1)
                        yield

                    side_by_side({"tdnn": tdnn, "norm0": norm(0), "norm1": norm(1), "norm2": norm(2), "norm3": norm(3),
                                  "qkv": qkv, "maxima": maxima, "heads": heads, "out0": out0, "experts0": experts(0),
                                  "bproj": bproj, "bmax": bmax, "bheads": bheads, "bout": bout, "cproj": cproj,
                                  "cmax": cmax, "cheads": cheads, "cout": cout, "experts1": experts(1)}, slots)

                @block.gpsimd
                def _(pool):
                    g = nc.gpsimd

                    def nothing(n):
                        def stage(z):
                            for _ in range(n):
                                yield
                        return stage

                    def qkv(z):
                        for i in range(H0):
                            if i % 2 == 0:
                                pool.wait_ge(z.s["qk_hi"], 2 * i + 2)
                                g.tensor_copy(z.QB[0:D0, i:i + 2, :], z.QS[0:D0, i:i + 2, :]).then_inc(z.s["q_copied"], 2)
                            yield
                        for t in range(NT):
                            yield

                    def heads(z):
                        yield
                        for hd in range(H0):
                            pool.wait_ge(z.s["p_hi"], hd + 1)
                            if hd >= 2:
                                pool.wait_ge(z.s["pv_psum"], hd - 1)
                            g.tensor_tensor(z.P_lo[:, hd % 2, 2, :], z.Pf[:, 2, :], z.P_hi[:, hd % 2, 2, :], ALU.subtract)\
                                .then_inc(z.s["p_lo_pool"], 1)
                            yield

                    def experts(f):
                        def split(z, e):
                            n, c = E * f + e, FC - 1
                            pool.wait_ge(z.s["hid_hi"], FC * (n + 1))
                            g.tensor_tensor(z.H_lo[:, e % 2, c, :], z.Hf[:, c, :], z.H_hi[:, e % 2, c, :], ALU.subtract)\
                                .then_inc(z.s["hid_lo_pool"], 1)

                        def stage(z):
                            for e in range(E):
                                split(z, e)
                                yield
                            yield
                        return stage

                    def bproj(z):
                        pool.wait_ge(z.s["hn_ready"], 3)
                        for x in (z.k1_hi, z.k1_lo):
                            g.memset(x[:, :, 0:HALF], 0.0)
                            g.memset(x[:, :, HALF + TP:], 0.0)
                        g.memset(z.V1_lo[:, :, :, D1:], 0.0)
                        g.memset(z.V1_hi[:, :, :, D1:], 1.0)
                        g.memset(z.Mexp[:], 0.0).then_inc(z.s["margins_set"], 1)
                        for _ in range(PIECES["bproj"]):
                            yield

                    def bheads(z):
                        for t in range(NT):
                            u = 4 * t + 3
                            pool.wait_ge(z.s["p_hi"], FULL["p_hi"] + u + 1)
                            g.tensor_tensor(z.P1_lo[:, u % RING, :], z.P1f[:, u % 2, :], z.P1_hi[:, u % RING, :], ALU.subtract)\
                                .then_inc(z.s["p_lo_pool"], 1)
                            yield
                        yield

                    def cproj(z):
                        yield
                        pool.wait_ge(z.s["qk_hi"], SLID["qk_hi"] + H2)
                        g.tensor_copy(z.QB[0:D2, 0:H2, :], z.QS[0:D2, 0:H2, :]).then_inc(z.s["q_copied"], H2)
                        yield

                    stages = {n: nothing(k) for n, k in PIECES.items()}
                    stages.update({"qkv": qkv, "heads": heads, "experts0": experts(0), "experts1": experts(1),
                                   "bproj": bproj, "bheads": bheads, "cproj": cproj})
                    side_by_side(stages, slots)

            nc.all_engine_barrier()
            for one in sems:
                nc.gpsimd.sem_clear(one)
            nc.all_engine_barrier()


def layout(i):
    f = {k: np.asarray(v) for k, v in i.items()}
    a = np.ascontiguousarray

    def twice(b):
        return a(np.broadcast_to(b.reshape(1, -1), (2, b.size)))

    def chunks(m, n):
        return a(m.reshape(n, P, m.shape[-1]).transpose(1, 0, 2))

    w = {"x": a(f["x"].transpose(0, 2, 1)),
         "tokW": chunks(f["L0_tok_W"].T, TAPS), "tokb": twice(f["L0_tok_b"]),
         "Wq": a(f["L0_attn_Wq"].T), "Wk": a(f["L0_attn_Wk"].T), "Wv": a(f["L0_attn_Wv"].T),
         "Wo": chunks(f["L0_attn_Wo"].T, 4)}
    for pre, src, wg, bg in (("m0_", "L0_ffn_", "Ws", "bs"), ("m1_", "L1_ffn_", "gate_W", "gate_b")):
        w[pre + "Wg"] = a(f[src + wg])
        w[pre + "bg"] = twice(f[src + bg])
        w[pre + "W1"] = a(f[src + "W1"].transpose(1, 0, 2))
        w[pre + "b1"] = a(f[src + "b1"].reshape(E, FC, P).transpose(2, 0, 1))
        w[pre + "W2"] = a(f[src + "W2"].reshape(E, FC, P, C).transpose(2, 0, 1, 3))
        w[pre + "b2"] = a(f[src + "b2"])
    wqkv, bqkv = f["L1_attn_W_qkv"], f["L1_attn_b_qkv"]
    bias = np.zeros((2, G1 * P), np.float32)
    for k, name in enumerate(("Wq1", "Wk1")):
        m = wqkv[:, C * k:C * k + C].reshape(P, G1, J1, 1, D1)
        w[name] = a(np.broadcast_to(m, (P, G1, J1, 2, D1)).reshape(P, G1, P))
        b = bqkv[C * k:C * k + C].reshape(G1, J1, 1, D1)
        bias[k] = np.broadcast_to(b, (G1, J1, 2, D1)).reshape(G1 * P)
    w["bqk1"] = twice(bias)
    w["Wv1"] = a(wqkv[:, 2 * C:])
    w["bv1"] = twice(bqkv[2 * C:])
    w["Wp1"] = a(f["L1_attn_W_proj"])
    w["bp1"] = twice(f["L1_attn_b_proj"])
    w["lng"] = a(np.broadcast_to(f["L1_ffn_ln_g"], (P, C)))
    w["lnb"] = a(np.broadcast_to(f["L1_ffn_ln_b"], (P, C)))
    w["Wqkv2"] = a(np.concatenate([f["L1_ffn_Wq"], f["L1_ffn_Wk"], f["L1_ffn_Wv"]], 1))
    w["Wo2"] = a(f["L1_ffn_Wo"])
    g = np.stack([f["L1_ffn_qn_g"]] * H2 + [f["L1_ffn_kn_g"]] * H2)
    w["qkg"] = a(np.broadcast_to(g, (P, 2 * H2, D2)))
    return w


def kernel(**inputs):
    import concourse.bacc as _bacc
    from concourse.bass_utils import run_bass_kernel_spmd as _run

    nc = _bacc.Bacc("TRN2", target_bir_lowering=False, num_devices=1)
    arrays = {**layout(inputs), **constants()}
    aps = {n: nc.dram_tensor(f"in_{n}", a.shape, mybir.dt.from_np(a.dtype), kind="ExternalInput").ap()
           for n, a in arrays.items()}
    out = nc.dram_tensor("out_0", (B, T, C), F32, kind="ExternalOutput").ap()
    tower(nc, aps, out)
    r = _run(nc, [{f"in_{n}": a for n, a in arrays.items()}], core_ids=[0])
    return r.results[0]["out_0"]
```

```python
from contextlib import ExitStack

import numpy as np

import concourse.bass as bass
from concourse import mybir

F32 = mybir.dt.float32
BF16 = mybir.dt.bfloat16
F16 = mybir.dt.float16
I32 = mybir.dt.int32
ALU = mybir.AluOpType
ACT = mybir.ActivationFunctionType
AX = mybir.AxisListType.X

P = 128
B, T_IN, C = 16, 375, 128
TAPS = 5
T = T_IN - TAPS + 1
NT = -(-T // P)
TP = NT * P
LAST = T - (NT - 1) * P
H0, D0 = 8, 64
H1, D1, HALF = 8, 16, 32
H2, D2 = 2, 64
E, FF = 8, 512
FC = FF // P
WIN = P + 2 * HALF
KC = WIN // 2
G1 = 2
J1 = H1 // G1
MASKED = -1e30


def constants():
    q = np.arange(P)
    ident = np.eye(P, dtype=np.float32)
    band_q = np.full((P, NT, WIN), MASKED, np.float32)
    band_k = np.full((KC, NT, 2, P), MASKED, np.float32)
    for t in range(NT):
        key = P * t - HALF + np.arange(WIN)
        seen = (abs(key[None, :] - (P * t + q)[:, None]) <= HALF) & (key >= 0) & (key < T)
        band_q[:, t][seen] = 0
        for c in range(2):
            band_k[:, t, c][seen.T[KC * c:KC * (c + 1)]] = 0
    later_q = np.where(q[None, :] > q[:, None], MASKED, 0).astype(np.float32)
    sel0 = np.zeros((H0 + 1, 2 * H0), np.float32)
    sel0[:H0] = np.tile(np.eye(H0), 2)
    sel0[H0, H0:] = -30000
    part = np.array([[0], [-1]], np.float32)
    rank = np.tile(np.arange(E, 0, -1, dtype=np.float32), (P, NT)).reshape(P, NT, E)
    row = np.arange(P)
    rows = np.stack([-((row % 32 >= D1).astype(np.float32)), row % 32 < D1, row % 32 == D1], 1).astype(np.float32)
    heads = (row[:, None] // 32 == np.arange(J1)).astype(np.float32)
    return {"c_rows": rows, "c_heads": heads, "c_ident": ident, "c_band_q": band_q, "c_band_k": band_k, "c_later_q": later_q,
            "c_later_k": np.ascontiguousarray(later_q.T), "c_sel0": sel0, "c_part": part, "c_rank": rank}


FULL = dict(qk_psum=H0, qk_hi=2 * H0, qk_lo=2 * H0, q_copied=16 * H0 // 2, k_copied=16 * H0 // 2, v_psum=NT, v_hi=NT, v_lo=NT,
            smax_psum=H0 * NT // 2, max_done=H0 * NT // 2, maxT_psum=1, negmax_ready=1, st_psum=NT * H0, exp_done=NT * H0,
            p_hi=NT * H0, p_lo=H0, p_lo_pool=2 * H0, pv_psum=H0, o_norm=H0, oT_psum=4, oT_hi=4, oT_lo=4, attn_psum=1)
SLID = {n: FULL[n] + k for n, k in dict(
    qk_psum=4, qk_hi=4, qk_lo=4, q_copied=0, k_copied=0, v_psum=2, v_hi=2, v_lo=2, smax_psum=4 * NT, max_done=4 * NT,
    maxT_psum=1, negmax_ready=0, st_psum=4 * NT, exp_done=4 * NT, p_hi=4 * NT, p_lo=3 * NT, p_lo_pool=NT,
    pv_psum=NT, o_norm=NT, oT_psum=1, oT_hi=1, oT_lo=1, attn_psum=1).items()}


CUT0, CUT1 = "experts0", "bheads"
TURNS = ["""1 1 3 1 1 1 5 1 4 1 5 1 1 1 3 1 2 1 3 1 2 1 1 1 1 1 1 1 1 1 1 1 1 2 1 1 1 1 1 2 1 1 2 1 1 1 2 1
    1 1 1 1""",
         """0 1 1 3 1 4 1 3 1 2 1 3 1 2 1 2 1 2 1 6 1 1 2 1 2 2 1 1 1 1 1 1 2 1 1 2 1 2 1 2 1 1 1 2 1 1 1 1
    1 1 1 1 1 1 2 1 1 1 1 1 1 1 1 1 2 1 1 1 1 1 2 3 1 1 1 1 1 1 1 1 1 1 1 1 1 1 1"""]

PIECES = {"tdnn": 3, "norm0": 2, "qkv": 11, "maxima": 13, "heads": 10, "out0": 6, "norm1": 2, "experts0": 9,
          "norm2": 2, "bproj": 6, "bmax": 4, "bheads": 4, "bout": 2, "norm3": 2, "cproj": 3, "cmax": 2,
          "cheads": 4, "cout": 2, "experts1": 9}
STAGES = list(PIECES)


def side_by_side(stages, runs, turns):
    def through(run):
        for name in run.names:
            going = stages[name](run.slot)
            for k in range(PIECES[name]):
                next(going)
                yield
            assert next(going, "done") == "done", name

    going = [through(run) for run in runs]
    if len(runs) == 1:
        turns = [sum(PIECES[name] for name in runs[0].names)]
    for i, n in enumerate(turns):
        for _ in range(n):
            next(going[i % len(runs)])
    for g in going:
        assert next(g, "done") == "done"


class Run:

    def __init__(self, slot, names, now, before=None, after=None):
        self.slot, self.names, self.now, self.before, self.after = slot, names, now, before, after


def tower(nc, w, out):
    with ExitStack() as ctx:
        def sb(name, shape, dt=F32):
            return ctx.enter_context(nc.sbuf_tensor("s_" + name, shape, dt))

        load = ctx.enter_context(nc.semaphore("constants_loaded"))
        hi_made = ctx.enter_context(nc.semaphore("hi_made"))
        round_split = ctx.enter_context(nc.semaphore("round_split"))
        bank = ctx.enter_context(nc.psum_tensor("bank", [P, 8, 512], F32))
        SLOTS = range(2)

        PLAIN = ["c_rows", "c_heads", "c_sel0", "c_part", "c_ident", "c_rank", "lng", "lnb", "qkg",
                 "m0_b1", "m1_b1", "m0_b2", "m1_b2"]
        MASKS = {"c_band_q": "bandq", "c_band_k": "bandk", "c_later_q": "laterq", "c_later_k": "laterk"}
        res = {n: sb(n, list(w[n].shape)) for n in PLAIN}
        mask = {n: sb(MASKS[n], list(w[n].shape), BF16) for n in MASKS}
        SPLIT = ["tokW", "Wq", "Wk", "Wv", "Wo", "m0_Wg", "m1_Wg", "Wq1", "Wk1", "Wv1", "Wp1", "Wqkv2", "Wo2",
                 "m0_W1", "m0_W2", "m1_W1", "m1_W2"]
        hi = {n: sb(n + "_hi", list(w[n].shape), F16) for n in SPLIT}
        lo = {n: sb(n + "_lo", list(w[n].shape), F16) for n in SPLIT}
        BIAS = ["tokb", "m0_bg", "m1_bg", "bqk1", "bv1", "bp1"]
        bias = {n: sb(n, [2, w[n].shape[1]], F16) for n in BIAS}
        bias_hi = {n: sb(n + "_hi", [2, w[n].shape[1]], F16) for n in BIAS}
        ident = res["c_ident"]
        identb = sb("identb", [P, P], BF16)
        ones = sb("ones", [2, TP], F16)

        class Slot:
            pass

        slots = []
        RING = 6
        ARENA = 9776
        names = """margins_set x_loaded h_stored x_hi x_lo tdnn_psum h_ready hn_ready hnT_psum hnT_hi hnT_lo qk_psum
            qk_hi qk_lo q_copied k_copied v_psum v_hi v_lo smax_psum max_done maxT_psum negmax_ready st_psum
            exp_done p_hi p_lo p_lo_pool pv_psum o_norm oT_psum oT_hi oT_lo attn_psum logits_psum logits_shift
            gate_exp gate_ready gateT_psum gateT_ready b2_psum hid_psum gelu_done hid_hi hid_lo hid_lo_pool
            down_psum acc_done bqz_ready bq2_ready csq cqk_ready cqkT_psum y_psum y_hi y_lo vector_step""".split()
        for q in SLOTS:
            z = Slot()
            slots.append(z)

            def own(name, shape, dt=F32):
                return sb(f"{name}{q}", shape, dt)

            z.q, z.b = q, 4 * q
            z.steps, z.stored = 0, False
            z.s = {}
            for n in names:
                z.s[n] = ctx.enter_context(nc.semaphore(f"{n}{q}"))
            numbers = [x.num for x in z.s.values()]
            z.sem_range = range(numbers[0], numbers[-1] + 1)
            assert numbers == list(z.sem_range)
            z.xT_hi, z.xT_lo = own("xT_hi", [P, TP + TAPS - 1], F16), own("xT_lo", [P, TP + TAPS - 1], F16)
            z.h, z.hn = own("h", [P, NT, C]), own("hn", [P, NT, C])
            z.hT_hi, z.hT_lo = (own("hT_hi", [P, HALF + TP + HALF], F16), own("hT_lo", [P, HALF + TP + HALF], F16))
            z.xf = z.hn[:].rearrange("p t c -> p (t c)")[:, 0:T_IN]
            z.stats, z.mv = own("stats", [P, NT, 6]), own("mv", [P, NT, 2])
            z.ve, z.guess, z.n1, z.n2, z.rstd = (own(n, [P, 12]) for n in ("ve", "guess", "n1", "n2", "rstd"))
            z.KB = own("KB", [D0 + H0 + 1, H0, TP], F16)
            z.V_hi, z.V_lo = (own("V_hi", [P, NT, H0, D0 + 1], F16), own("V_lo", [P, NT, H0, D0 + 1], F16))
            z.Mx, z.rec = own("Mx", [P, (H0 + 1) * NT]), own("rec", [P, 8])
            z.lm, z.ge, z.ga, z.gate = (own(n, [P, NT, E]) for n in ("lm", "ge", "ga", "gate"))
            z.gm, z.gs, z.gr, z.gb = (own(n, [P, NT]) for n in ("gm", "gs", "gr", "gb"))
            arena = own("arena", [P, ARENA])
            z.arena = arena

            class Carver:
                at = 0

            def carve(words, dt, pattern, parts=P, **sizes):
                v = arena[0:parts, Carver.at:Carver.at + words]
                Carver.at += words
                assert Carver.at <= ARENA, Carver.at
                return (v if dt == F32 else v.bitcast(dt)).rearrange(pattern, **sizes)

            hw = H0 * TP // 2
            z.QS = carve(hw, F16, "p (a n) -> p a n", a=H0)
            z.QB = carve(hw, F16, "p (a n) -> p a n", a=H0)
            z.KS = carve(hw, F16, "p (a n) -> p a n", a=H0)
            z.Pf = carve(NT * TP, F32, "p (t n) -> p t n", t=NT)
            z.P_hi = carve(NT * TP, F16, "p (b t n) -> p b t n", b=2, t=NT)
            z.P_lo = carve(NT * TP, F16, "p (b t n) -> p b t n", b=2, t=NT)
            z.O = carve(NT * C * 4, F32, "p (t a d) -> p t a d", t=NT, a=H0)
            z.OT_hi = z.P_hi.rearrange("p b t n -> p (b t n)")[:, 0:4 * TP].rearrange("p (c n) -> p c n", c=4)
            z.OT_lo = z.P_lo.rearrange("p b t n -> p (b t n)")[:, 0:4 * TP].rearrange("p (c n) -> p c n", c=4)
            Carver.at = 0
            z.Hf = carve(FC * TP, F32, "p (c n) -> p c n", c=FC)
            z.H_hi = carve(FC * TP, F16, "p (b c n) -> p b c n", b=2, c=FC)
            z.H_lo = carve(FC * TP, F16, "p (b c n) -> p b c n", b=2, c=FC)
            z.gT = carve(TP, F32, "p n -> p n", parts=E)
            Carver.at = 0
            z.q1_hi = carve(TP * G1 // 2, F16, "p (g n) -> p g n", g=G1)
            z.q1_st = carve(TP * G1 // 2, F16, "p (g n) -> p g n", g=G1)
            z.q1_m = z.q1_st
            z.qz_hi = carve(TP * G1 * J1 // 2, F16, "p (g j n) -> p g j n", g=G1, j=J1)
            z.qz_st = carve(TP * G1 * J1 // 2, F16, "p (g j n) -> p g j n", g=G1, j=J1)
            z.qz_m = z.qz_hi
            z.P1f_whole = carve(2 * 512, F32, "p n -> p n")
            z.P1f = z.P1f_whole[0:KC, :].rearrange("p (b n) -> p b n", b=2)
            mexp_at = Carver.at
            z.P1_hi, z.P1_lo = (carve(RING * 256, F16, "p (u n) -> p u n", parts=KC, u=RING) for _ in range(2))
            z.k1_d = z.P1f_whole[:, 0:G1 * TP].rearrange("p (g n) -> p g n", g=G1)
            z.V1_hi, z.V1_lo = (carve(NT * H1 * (D1 + 1), F16, "p (t a d) -> p t a d", parts=KC, t=2 * NT, a=H1)
                                for _ in range(2))
            z.k1_hi, z.k1_lo = (carve(G1 * (HALF + TP + HALF) // 2, F16, "p (g n) -> p g n", g=G1) for _ in range(2))
            z.Mexp = arena[:, mexp_at:mexp_at + NT * G1 * P].rearrange("p (t g n) -> p t g n", t=NT, g=G1)
            z.O1 = z.hn[:].rearrange("p t (a d) -> p t a d", a=H1)
            z.O1T_hi, z.O1T_lo = z.q1_hi[:, 0, :], z.q1_hi[:, 1, :]
            Carver.at = 3 * hw
            z.sq = carve(NT * 2 * C, F32, "p (t c) -> p t c", t=NT)
            z.qk = carve(NT * 2 * C, F32, "p (t a d) -> p t a d", t=NT, a=4)

        def flat(x):
            k = len(x.shape)
            return x if k == 2 else x.rearrange({3: "p a b -> p (a b)", 4: "p a b c -> p (a b c)"}[k])

        AREA = ARENA // 2
        rounds, room = [[]], AREA
        for n in list(MASKS) + BIAS + SPLIT:
            words = int(np.prod(w[n].shape[1:]))
            if words > room:
                rounds.append([])
                room = AREA
            r = len(rounds) - 1
            at = AREA * (r // 2 % 2) + AREA - room
            rounds[-1].append((n, slots[r % 2].arena[0:w[n].shape[0], at:at + words]))
            room -= words
        landed = [ctx.enter_context(nc.semaphore(f"round{r}_landed")) for r in range(len(rounds))]
        with nc.Block() as block:
            @block.sync
            def _(sp):
                for r, what in enumerate(rounds):
                    if r >= 4:
                        sp.wait_ge(round_split, r - 3)
                    for n, land in what:
                        sp.dma_start(land, flat(w[n])).then_inc(landed[r], 16)
                    if r == 0:
                        for n in PLAIN:
                            sp.dma_start(res[n][:], w[n]).then_inc(load, 16)
                        for z in slots:
                            sp.dma_start(z.xf, w["x"][z.q]).then_inc(load, 16)

            @block.scalar
            def _(act):
                for r, what in enumerate(rounds):
                    act.wait_ge(landed[r], 16 * len(what))
                    for n, land in what:
                        to = hi[n][:] if n in SPLIT else bias_hi[n][:] if n in BIAS else mask[n][:]
                        nc.scalar.activation(flat(to), land, ACT.Copy).then_inc(hi_made, 1)

            @block.vector
            def _(dve):
                v = nc.vector
                v.memset(ones[:], 1.0)
                for z in slots:
                    for x in (z.xT_hi[:, T_IN:], z.xT_lo[:, T_IN:], z.hT_hi[:, 0:HALF], z.hT_hi[:, HALF + TP:],
                              z.hT_lo[:, 0:HALF], z.hT_lo[:, HALF + TP:], z.V_lo[:, :, :, D0:]):
                        v.memset(x, 0.0)
                    v.memset(z.V_hi[:, :, :, D0:], 1.0)
                    v.memset(z.Mx[:, H0 * NT:], -1.0)
                dve.wait_ge(load, 16 * (len(PLAIN) + 2))
                v.tensor_copy(identb[:], ident[:])
                for z in slots:
                    for at, n, rows in ((0, T, res["c_sel0"][:, 0:H0]), (T, TP - T, res["c_sel0"][:, H0:])):
                        v.tensor_copy(z.KB[D0:, :, at:at + n], rows.unsqueeze(2).to_broadcast([H0 + 1, H0, n]))
                made = 0
                for r, what in enumerate(rounds):
                    for n, land in what:
                        made += 1
                        dve.wait_ge(hi_made, made)
                        if n in SPLIT:
                            i = v.tensor_tensor(flat(lo[n][:]), land, flat(hi[n][:]), ALU.subtract)
                        elif n in BIAS:
                            i = v.scalar_tensor_tensor(bias[n][:], bias_hi[n][:], res["c_part"][:, 0:1], land,
                                                       ALU.mult, ALU.add)
                    i.then_inc(round_split, 1)
        nc.all_engine_barrier()

        def tile(t):
            return slice(P * t, P * (t + 1))

        def tiles(x):
            return x.rearrange("p (t c) -> p t c", t=NT)

        INNER = slice(HALF, HALF + TP)
        ROOT = D0 ** -0.5
        M_ROW = 16

        def nothing(n):
            def stage(z):
                for _ in range(n):
                    yield
            return stage

        EARLY0, LATE0 = STAGES[:STAGES.index(CUT0)], STAGES[STAGES.index(CUT0):]
        EARLY1, LATE1 = STAGES[:STAGES.index(CUT1)], STAGES[STAGES.index(CUT1):]

        def segment(*runs, leaving=None):
            turns = [int(n) for n in TURNS[0 if runs[0].names is EARLY0 else 1].split()]
            for run in runs:
                if run.names[0] == STAGES[0]:
                    run.slot.stored = run.before is not None
            with nc.Block() as block:
                @block.sync
                def _(sp):
                    def store(z, seq):
                        for t in range(NT):
                            n = P if t < NT - 1 else LAST
                            sp.dma_start(out[seq, P * t:P * t + n, :], z.h[0:n, t, :]).then_inc(z.s["h_stored"], 16)

                    run_of = {run.slot.q: run for run in runs}

                    def tdnn(z):
                        if run_of[z.q].before is not None:
                            store(z, run_of[z.q].before)
                        yield
                        yield
                        yield

                    def qkv(z):
                        for i in range(PIECES["qkv"]):
                            if i < H0 and i % 2:
                                sp.wait_ge(z.s["qk_hi"], 2 * i + 2)
                                sp.dma_start(z.KS[D0:, i - 1:i + 1, :], z.KS[0:D0, i - 1:i + 1, :])\
                                    .then_inc(z.s["k_copied"], 16)
                            elif i < H0:
                                sp.wait_ge(z.s["qk_hi"], 2 * i + 2)
                                sp.dma_start(z.QB[0:D0, i:i + 2, :], z.QS[0:D0, i:i + 2, :]).then_inc(z.s["q_copied"], 16)
                            yield

                    def cproj(z):
                        yield
                        yield
                        if run_of[z.q].after is not None:
                            sp.wait_ge(z.s["hnT_psum"], 4)
                            sp.dma_start(z.xf, w["x"][run_of[z.q].after]).then_inc(z.s["x_loaded"], 16)
                        sp.wait_ge(z.s["qk_hi"], SLID["qk_hi"] + H2)
                        sp.dma_start(z.QB[0:D2, 0:H2, :], z.QS[0:D2, 0:H2, :]).then_inc(z.s["q_copied"], 16)
                        sp.wait_ge(z.s["qk_hi"], SLID["qk_hi"] + 2 * H2)
                        sp.dma_start(z.KS[D2:, 0:H2, :], z.KS[0:D2, 0:H2, :]).then_inc(z.s["k_copied"], 16)
                        yield

                    stages = {n: nothing(k) for n, k in PIECES.items()}
                    stages.update({"tdnn": tdnn, "qkv": qkv, "cproj": cproj})
                    if leaving:
                        store(*leaving)
                        sp.wait_ge(leaving[0].s["h_stored"], 16 * NT)
                    side_by_side(stages, runs, turns)
                    for run in runs:
                        z = run.slot
                        if "cproj" in run.names and run.after is not None:
                            sp.wait_ge(z.s["x_loaded"], 16)
                        if "experts1" in run.names and run.after is None:
                            sp.wait_ge(z.s["acc_done"], 2 * (E + 1))
                            store(z, run.now)
                            sp.wait_ge(z.s["h_stored"], 16 * NT * (2 if z.stored else 1))

                @block.tensor
                def _(pe):
                    mm, tr = nc.tensor.matmul, nc.tensor.transpose

                    def mm3(to, a, b, start=True, stop=True):
                        mm(to, a[0], b[0], start=start, stop=False)
                        mm(to, a[0], b[1], start=False, stop=False)
                        return mm(to, a[1], b[0], start=False, stop=stop)

                    def weights(n, at):
                        return hi[n][at], lo[n][at]

                    def tdnn(z):
                        s = z.s
                        yield
                        pe.wait_ge(s["x_hi"], 1)
                        pe.wait_ge(s["x_lo"], 1)
                        for t in range(NT):
                            to = bank[:, z.b, tile(t)]
                            mm(to, ones[:, 0:P], bias["tokb"][:], start=True, stop=False)
                            for k in range(TAPS):
                                at = slice(P * t + k, P * t + k + P)
                                i = mm3(to, (z.xT_hi[:, at], z.xT_lo[:, at]), weights("tokW", np.s_[:, k, :]),
                                        start=False, stop=k == TAPS - 1)
                        i.then_inc(s["tdnn_psum"], 1)
                        yield
                        yield

                    def norm(k):
                        def stage(z):
                            yield
                            pe.wait_ge(z.s["hn_ready"], k + 1)
                            for t in range(NT):
                                i = tr(bank[:, z.b + 1, tile(t)], z.hn[:, t, :], ident[:])
                            i.then_inc(z.s["hnT_psum"], 1)
                            yield
                        return stage

                    def await_hnT(z, k):
                        pe.wait_ge(z.s["hnT_hi"], k + 1)
                        pe.wait_ge(z.s["hnT_lo"], k + 1)
                        return z.hT_hi[:, INNER], z.hT_lo[:, INNER]

                    def qkv(z):
                        s = z.s
                        x = await_hnT(z, 0)
                        for i in range(H0):
                            if i >= 4:
                                pe.wait_ge(s["qk_hi"], 2 * (i - 3))
                                pe.wait_ge(s["qk_lo"], 2 * (i - 3))
                            mm3(bank[:, z.b + i % 4, 0:TP], weights("Wk" if i % 2 else "Wq", np.s_[:, tile(i // 2)]), x)\
                                .then_inc(s["qk_psum"], 1)
                            yield
                        for t in range(NT):
                            pe.wait_ge(s["qk_hi"], 2 * t + 10)
                            pe.wait_ge(s["qk_lo"], 2 * t + 10)
                            mm3(bank[:, z.b + t, :], (x[0][:, tile(t)], x[1][:, tile(t)]), weights("Wv", np.s_[:, :]))\
                                .then_inc(s["v_psum"], 1)
                            yield

                    def maxima(z):
                        s = z.s
                        pe.wait_ge(s["qk_hi"], 2 * H0)
                        pe.wait_ge(s["qk_lo"], 2 * H0)
                        pe.wait_ge(s["v_hi"], NT)
                        pe.wait_ge(s["v_lo"], NT)
                        for i in range(H0 * NT // 2):
                            if i >= 2:
                                pe.wait_ge(s["max_done"], i - 1)
                            for a in range(2):
                                hd, t = divmod(2 * i + a, NT)
                                n = mm(bank[:, z.b + 2 * (i % 2) + a, 0:T], z.QS[0:D0, hd, tile(t)], z.KS[0:D0, hd, 0:T],
                                       start=True, stop=True)
                            n.then_inc(s["smax_psum"], 1)
                            yield
                        pe.wait_ge(s["max_done"], H0 * NT // 2)
                        for t in range(NT):
                            i = tr(bank[0:H0 + 1, z.b, tile(t)], z.Mx[:, t::NT], ident[:])
                        i.then_inc(s["maxT_psum"], 1)
                        yield

                    def heads(z):
                        s = z.s
                        for i in range(H0 + 2):
                            if i < H0:
                                if i == 0:
                                    pe.wait_ge(s["negmax_ready"], 1)
                                    pe.wait_ge(s["q_copied"], 16 * H0 // 2)
                                    pe.wait_ge(s["k_copied"], 16 * H0 // 2)
                                for t in range(NT):
                                    if i:
                                        pe.wait_ge(s["exp_done"], NT * (i - 1) + t + 1)
                                    mm(bank[:, z.b + t, 0:TP], z.KS[:, i, tile(t)], z.QS[:, i, :], start=True, stop=False)
                                    n = mm(bank[:, z.b + t, 0:TP], z.KB[:, i, tile(t)], z.QB[0:D0 + H0 + 1, i, :],
                                           start=False, stop=True)
                                    n.then_inc(s["st_psum"], 1)
                            if i >= 2:
                                hd = i - 2
                                pe.wait_ge(s["p_hi"], NT * (hd + 1))
                                pe.wait_ge(s["p_lo"], hd + 1)
                                pe.wait_ge(s["p_lo_pool"], 2 * (hd + 1))
                                if hd:
                                    pe.wait_ge(s["o_norm"], hd)
                                for t in range(NT):
                                    to = bank[:, z.b + 3, (D0 + 1) * t:(D0 + 1) * (t + 1)]
                                    for k in range(NT):
                                        m = P if k < NT - 1 else LAST
                                        n = mm3(to, (z.P_hi[0:m, hd % 2, k, tile(t)], z.P_lo[0:m, hd % 2, k, tile(t)]),
                                                (z.V_hi[0:m, k, hd, :], z.V_lo[0:m, k, hd, :]), start=k == 0, stop=k == NT - 1)
                                n.then_inc(s["pv_psum"], 1)
                            yield

                    def out0(z):
                        s = z.s
                        pe.wait_ge(s["o_norm"], H0)
                        for c in range(4):
                            for t in range(NT):
                                i = tr(bank[:, z.b + c, tile(t)],
                                       z.O[:, t, 2 * c:2 * c + 2, :].rearrange("p a d -> p (a d)"), ident[:])
                            i.then_inc(s["oT_psum"], 1)
                            yield
                        pe.wait_ge(s["oT_hi"], 4)
                        pe.wait_ge(s["oT_lo"], 4)
                        for t in range(NT):
                            for c in range(4):
                                i = mm3(bank[:, z.b, tile(t)], (z.OT_hi[:, c, tile(t)], z.OT_lo[:, c, tile(t)]),
                                        weights("Wo", np.s_[:, c, :]), start=c == 0, stop=c == 3)
                        i.then_inc(s["attn_psum"], 1)
                        yield
                        yield

                    def experts(f):
                        def up(z, e, x):
                            for c in range(FC):
                                n = (E * f + e) * FC + c
                                if n - E * f * FC >= 3:
                                    pe.wait_ge(z.s["gelu_done"], n - 2)
                                mm3(bank[:, z.b + (e * FC + c) % 3, 0:TP], weights(f"m{f}_W1", np.s_[:, e, tile(c)]), x)\
                                    .then_inc(z.s["hid_psum"], 1)

                        def down(z, e):
                            n = E * f + e
                            pe.wait_ge(z.s["hid_hi"], FC * (n + 1))
                            pe.wait_ge(z.s["hid_lo"], n + 1)
                            pe.wait_ge(z.s["hid_lo_pool"], (FC - 1) * (n + 1))
                            pe.wait_ge(z.s["acc_done"], (E + 1) * f + e + 1)
                            for t in range(NT):
                                for c in range(FC):
                                    i = mm3(bank[:, z.b + 3, tile(t)],
                                            (z.H_hi[:, e % 2, c, tile(t)], z.H_lo[:, e % 2, c, tile(t)]),
                                            weights(f"m{f}_W2", np.s_[:, e, c, :]), start=c == 0, stop=c == FC - 1)
                            i.then_inc(z.s["down_psum"], 1)

                        def stage(z):
                            s = z.s
                            if f == 0:
                                x = await_hnT(z, 1)
                            else:
                                pe.wait_ge(s["y_hi"], 1)
                                pe.wait_ge(s["y_lo"], 1)
                                x = z.hT_hi[:, INNER], z.hT_lo[:, INNER]
                            for t in range(NT):
                                to = bank[:, z.b + 3, E * t:E * t + E]
                                mm(to, ones[:, 0:P], bias[f"m{f}_bg"][:], start=True, stop=False)
                                i = mm3(to, (x[0][:, tile(t)], x[1][:, tile(t)]), weights(f"m{f}_Wg", np.s_[:, :]), start=False)
                            i.then_inc(s["logits_psum"], 1)
                            up(z, 0, x)
                            yield
                            for e in range(E):
                                if e == 0:
                                    pe.wait_ge(s["gate_ready"], f + 1)
                                    for t in range(NT):
                                        i = tr(bank[0:E, z.b + 3, tile(t)], z.gate[:, t, :], ident[:])
                                    i.then_inc(s["gateT_psum"], 1)
                                if e + 1 < E:
                                    up(z, e + 1, x)
                                if e == 0:
                                    pe.wait_ge(s["gateT_ready"], f + 1)
                                    for t in range(NT):
                                        i = mm(bank[:, z.b + 3, tile(t)], z.gT[:, tile(t)], res[f"m{f}_b2"][:],
                                               start=True, stop=True)
                                    i.then_inc(s["b2_psum"], 1)
                                down(z, e)
                                yield
                        return stage

                    def bproj(z):
                        s = z.s
                        x = await_hnT(z, 2)
                        for i in range(4):
                            g = i % G1
                            mm(bank[:, z.b + i, 0:TP], bias["bqk1"][:, P * i:P * i + P], ones[:], start=True, stop=False)
                            mm3(bank[:, z.b + i, 0:TP], weights("Wq1" if i < G1 else "Wk1", np.s_[:, g, :]), x, start=False)\
                                .then_inc(s["qk_psum"], 1)
                            yield
                        for i in range(2):
                            pe.wait_ge(s["qk_hi"], FULL["qk_hi"] + i + 1)
                            pe.wait_ge(s["qk_lo"], FULL["qk_lo"] + i + 1)
                            for u in range(NT):
                                t, c = divmod(NT * i + u, 2)
                                at = slice(P * t + KC * c, P * t + KC * c + KC)
                                to = bank[0:KC, z.b + i, tile(u)]
                                mm(to, ones[:, 0:KC], bias["bv1"][:], start=True, stop=False)
                                n = mm3(to, (z.hT_hi[:, at], z.hT_lo[:, at]), weights("Wv1", np.s_[:, :]), start=False)
                            n.then_inc(s["v_psum"], 1)
                            yield

                    def bmax(z):
                        s = z.s
                        pe.wait_ge(s["qk_hi"], FULL["qk_hi"] + 4)
                        pe.wait_ge(s["qk_lo"], FULL["qk_lo"] + 4)
                        pe.wait_ge(s["bqz_ready"], 1)
                        pe.wait_ge(s["margins_set"], 1)
                        for t in range(NT):
                            for pair in range(4):
                                u = 4 * t + pair
                                if u == 2:
                                    pe.wait_ge(s["v_hi"], FULL["v_hi"] + 2)
                                    pe.wait_ge(s["v_lo"], FULL["v_lo"] + 2)
                                if u >= 4:
                                    pe.wait_ge(s["max_done"], FULL["max_done"] + u - 3)
                                to = bank[:, z.b + (u + 2) % 4, 0:2 * WIN]
                                mm(to, identb[:], mask["c_band_q"][:, t, :].unsqueeze(1).to_broadcast([P, 2, WIN]),
                                   start=True, stop=True)
                                for a in range(2):
                                    g, j = divmod(2 * pair + a, J1)
                                    n = mm(bank[:, z.b + (u + 2) % 4, WIN * a:WIN * a + WIN], z.qz_hi[:, g, j, tile(t)],
                                           z.k1_hi[:, g, P * t:P * t + WIN], start=False, stop=True, skip_group_check=True)
                                n.then_inc(s["smax_psum"], 1)
                            yield
                        pe.wait_ge(s["max_done"], FULL["max_done"] + 4 * NT)
                        for g in range(G1):
                            for t in range(NT):
                                i = tr(bank[:, z.b + g, tile(t)], z.Mexp[:, t, g, :], ident[:])
                        i.then_inc(s["maxT_psum"], 1)
                        yield

                    def bheads(z):
                        s = z.s
                        pe.wait_ge(s["bq2_ready"], 1)
                        for t in range(NT + 1):
                            if t < NT:
                                for c in range(2):
                                    for g in range(G1):
                                        u = 4 * t + 2 * c + g
                                        if u >= 3:
                                            pe.wait_ge(s["exp_done"], FULL["exp_done"] + u - 2)
                                        to = bank[0:KC, z.b + u % 3, :]
                                        keys = slice(P * t + KC * c, P * t + KC * c + KC)
                                        mm(to, identb[0:KC, 0:KC],
                                           mask["c_band_k"][:, t, c, :].unsqueeze(1).to_broadcast([KC, J1, P]),
                                           start=True, stop=False)
                                        mm(to, z.k1_hi[:, g, keys], z.qz_st[:, g, :, tile(t)], start=False, stop=False)
                                        mm(to, z.k1_lo[:, g, keys], z.qz_m[:, g, :, tile(t)], start=False, stop=True)\
                                            .then_inc(s["st_psum"], 1)
                            if t:
                                pe.wait_ge(s["p_hi"], FULL["p_hi"] + 4 * t)
                                pe.wait_ge(s["p_lo"], FULL["p_lo"] + 3 * t)
                                pe.wait_ge(s["p_lo_pool"], FULL["p_lo_pool"] + t)
                                if t > 1:
                                    pe.wait_ge(s["o_norm"], FULL["o_norm"] + t - 1)
                                for hd in range(H1):
                                    g, j = divmod(hd, J1)
                                    for c in range(2):
                                        u = 4 * (t - 1) + 2 * c + g
                                        i = mm3(bank[:, z.b + 3, (D1 + 1) * hd:(D1 + 1) * (hd + 1)],
                                                (z.P1_hi[:, u % RING, tile(j)], z.P1_lo[:, u % RING, tile(j)]),
                                                (z.V1_hi[:, 2 * (t - 1) + c, hd, :], z.V1_lo[:, 2 * (t - 1) + c, hd, :]),
                                                start=c == 0, stop=c == 1)
                                i.then_inc(s["pv_psum"], 1)
                            yield

                    def bout(z):
                        s = z.s
                        pe.wait_ge(s["o_norm"], FULL["o_norm"] + NT)
                        for t in range(NT):
                            i = tr(bank[:, z.b, tile(t)], z.O1[:, t, :, :].rearrange("p a d -> p (a d)"), ident[:])
                        i.then_inc(s["oT_psum"], 1)
                        yield
                        pe.wait_ge(s["oT_hi"], FULL["oT_hi"] + 1)
                        pe.wait_ge(s["oT_lo"], FULL["oT_lo"] + 1)
                        for t in range(NT):
                            mm(bank[:, z.b + 1, tile(t)], ones[:, 0:P], bias["bp1"][:], start=True, stop=False)
                            i = mm3(bank[:, z.b + 1, tile(t)], (z.O1T_hi[:, tile(t)], z.O1T_lo[:, tile(t)]),
                                    weights("Wp1", np.s_[:, :]), start=False)
                        i.then_inc(s["attn_psum"], 1)
                        yield

                    def cproj(z):
                        s = z.s
                        x = await_hnT(z, 3)
                        for t in range(NT):
                            mm3(bank[:, z.b + t, 0:3 * C], (x[0][:, tile(t)], x[1][:, tile(t)]),
                                weights("Wqkv2", np.s_[:, :])).then_inc(s["v_psum"], 1)
                        yield
                        yield
                        pe.wait_ge(s["cqk_ready"], 1)
                        pe.wait_ge(s["v_hi"], SLID["v_hi"] + NT)
                        for which in range(2):
                            for t in range(NT):
                                i = tr(bank[:, z.b + (0 if which else 3), tile(t)],
                                       z.qk[:, t, 2 * which:2 * which + 2, :].rearrange("p a d -> p (a d)"), ident[:])
                            i.then_inc(s["cqkT_psum"], 1)
                        yield

                    def cmax(z):
                        s = z.s
                        pe.wait_ge(s["qk_hi"], SLID["qk_hi"] + 4)
                        pe.wait_ge(s["qk_lo"], SLID["qk_lo"] + 4)
                        for u in range(H2 * NT):
                            hd, t = divmod(u, NT)
                            if u >= 4:
                                pe.wait_ge(s["max_done"], SLID["max_done"] + u - 3)
                            L, b = P * (t + 1), z.b + (u + 1) % 4
                            mm(bank[:, b, 0:L], z.QS[0:D2, hd, tile(t)], z.KS[0:D2, hd, 0:L], start=True, stop=True)
                            mm(bank[:, b, tile(t)], identb[:], mask["c_later_q"][:], start=False, stop=True,
                               skip_group_check=True).then_inc(s["smax_psum"], 1)
                        yield
                        pe.wait_ge(s["max_done"], SLID["max_done"] + H2 * NT)
                        for t in range(NT):
                            i = tr(bank[0:H2, z.b, tile(t)], z.Mx[:, t:H2 * NT:NT], ident[:])
                        i.then_inc(s["maxT_psum"], 1)
                        yield

                    def cheads(z):
                        s = z.s
                        for i in range(2 * H2):
                            if i < H2:
                                if i == 0:
                                    pe.wait_ge(s["negmax_ready"], SLID["negmax_ready"] + 1)
                                    pe.wait_ge(s["q_copied"], SLID["q_copied"] + 16)
                                    pe.wait_ge(s["k_copied"], SLID["k_copied"] + 16)
                                else:
                                    pe.wait_ge(s["exp_done"], SLID["exp_done"] + NT)
                                for k in range(NT):
                                    to = bank[:, z.b + k, P * k:TP]
                                    mm(to, z.KS[:, i, tile(k)], z.QS[:, i, P * k:TP], start=True, stop=True)
                                    mm(to, z.KB[0:D2 + H2, i, tile(k)], z.QB[0:D2 + H2, i, P * k:TP], start=False,
                                       stop=True, skip_group_check=True)
                                    mm(bank[:, z.b + k, tile(k)], identb[:], mask["c_later_k"][:], start=False, stop=True,
                                       skip_group_check=True).then_inc(s["st_psum"], 1)
                            if i >= H2:
                                hd = i - H2
                                pe.wait_ge(s["p_lo"], SLID["p_lo"] + NT * (hd + 1))
                                if hd:
                                    pe.wait_ge(s["o_norm"], SLID["o_norm"] + hd)
                                for t in range(NT):
                                    for k in range(t + 1):
                                        n = mm3(bank[:, z.b + 3, (D2 + 1) * t:(D2 + 1) * (t + 1)],
                                                (z.P_hi[:, hd, k, tile(t)], z.P_lo[:, hd, k, tile(t)]),
                                                (z.V_hi[:, k, hd, :], z.V_lo[:, k, hd, :]), start=k == 0, stop=k == t)
                                n.then_inc(s["pv_psum"], 1)
                            yield

                    def cout(z):
                        s = z.s
                        pe.wait_ge(s["o_norm"], SLID["o_norm"] + H2)
                        for t in range(NT):
                            i = tr(bank[:, z.b, tile(t)], z.O[:, t, 0:H2, :].rearrange("p a d -> p (a d)"), ident[:])
                        i.then_inc(s["oT_psum"], 1)
                        yield
                        pe.wait_ge(s["oT_hi"], SLID["oT_hi"] + 1)
                        pe.wait_ge(s["oT_lo"], SLID["oT_lo"] + 1)
                        mm3(bank[:, z.b + 1, 0:TP], weights("Wo2", np.s_[:, :]), (z.OT_hi[:, 0, :], z.OT_lo[:, 0, :]))\
                            .then_inc(s["y_psum"], 1)
                        yield

                    side_by_side({"tdnn": tdnn, "norm0": norm(0), "norm1": norm(1), "norm2": norm(2), "norm3": norm(3),
                                  "qkv": qkv, "maxima": maxima, "heads": heads, "out0": out0, "experts0": experts(0),
                                  "bproj": bproj, "bmax": bmax, "bheads": bheads, "bout": bout, "cproj": cproj,
                                  "cmax": cmax, "cheads": cheads, "cout": cout, "experts1": experts(1)}, runs, turns)

                @block.scalar
                def _(act):
                    fn = nc.scalar.activation

                    def tdnn(z):
                        fn(z.xT_hi[:, 0:T_IN], z.xf[:, 0:T_IN], ACT.Copy).then_inc(z.s["x_hi"], 1)
                        yield
                        yield
                        act.wait_ge(z.s["tdnn_psum"], 1)
                        if z.stored:
                            act.wait_ge(z.s["h_stored"], 16 * NT)
                        fn(z.h[:], tiles(bank[:, z.b, 0:TP]), ACT.Relu).then_inc(z.s["h_ready"], 1)
                        yield

                    def norm(k):
                        def stage(z):
                            yield
                            act.wait_ge(z.s["hnT_psum"], k + 1)
                            fn(z.hT_hi[:, INNER], bank[:, z.b + 1, 0:TP], ACT.Copy).then_inc(z.s["hnT_hi"], 1)
                            yield
                        return stage

                    def qkv(z):
                        for i in range(H0):
                            act.wait_ge(z.s["qk_psum"], i + 1)
                            for a in range(2):
                                fn((z.KS if i % 2 else z.QS)[0:D0, 2 * (i // 2) + a, :],
                                   bank[D0 * a:D0 * a + D0, z.b + i % 4, 0:TP], ACT.Copy).then_inc(z.s["qk_hi"], 1)
                            yield
                        for t in range(NT):
                            act.wait_ge(z.s["v_psum"], t + 1)
                            fn(z.V_hi[:, t, :, 0:D0], bank[:, z.b + t, :].rearrange("p (a d) -> p a d", a=H0), ACT.Copy)\
                                .then_inc(z.s["v_hi"], 1)
                            yield

                    def maxima(z):
                        for i in range(H0 * NT // 2):
                            yield
                        act.wait_ge(z.s["maxT_psum"], 1)
                        fn(z.QB[D0:D0 + H0 + 1, :, :],
                           bank[0:H0 + 1, z.b, 0:TP].unsqueeze(1).to_broadcast([H0 + 1, H0, TP]),
                           ACT.Copy, scale=-1.0).then_inc(z.s["negmax_ready"], 1)
                        yield

                    def heads(z):
                        for i in range(H0):
                            for t in range(NT):
                                act.wait_ge(z.s["st_psum"], NT * i + t + 1)
                                if i and t == 0:
                                    act.wait_ge(z.s["p_lo"], i)
                                elif i:
                                    act.wait_ge(z.s["p_lo_pool"], 2 * (i - 1) + t)
                                fn(z.Pf[:, t, :], bank[:, z.b + t, 0:TP], ACT.Exp, scale=ROOT).then_inc(z.s["exp_done"], 1)
                            yield
                        yield
                        yield

                    def out0(z):
                        for c in range(4):
                            act.wait_ge(z.s["oT_psum"], c + 1)
                            fn(z.OT_hi[:, c, :], bank[:, z.b + c, 0:TP], ACT.Copy).then_inc(z.s["oT_hi"], 1)
                            yield
                        yield
                        yield

                    def experts(f):
                        def gelus(z, e):
                            n = E * f + e
                            for c in range(FC):
                                act.wait_ge(z.s["hid_psum"], FC * n + c + 1)
                                if n:
                                    if c == 0:
                                        act.wait_ge(z.s["hid_lo"], n)
                                    else:
                                        act.wait_ge(z.s["hid_lo_pool"], (FC - 1) * (n - 1) + c)
                                fn(z.Hf[:, c, :], bank[:, z.b + (FC * e + c) % 3, 0:TP],
                                   ACT.Gelu_apprx_tanh if f else ACT.Gelu, bias=res[f"m{f}_b1"][:, e, c:c + 1])\
                                    .then_inc(z.s["gelu_done"], 1)

                        def stage(z):
                            s = z.s
                            act.wait_ge(s["logits_shift"], f + 1)
                            fn(z.ge[:], z.lm[:], ACT.Exp).then_inc(s["gate_exp"], 1)
                            gelus(z, 0)
                            yield
                            act.wait_ge(s["gateT_psum"], f + 1)
                            fn(z.gT, bank[0:E, z.b + 3, 0:TP], ACT.Copy).then_inc(s["gateT_ready"], 1)
                            for e in range(1, E):
                                gelus(z, e)
                                yield
                            yield
                        return stage

                    def bproj(z):
                        for i in range(4):
                            act.wait_ge(z.s["qk_psum"], FULL["qk_psum"] + i + 1)
                            to = z.q1_hi[:, i, :] if i < G1 else z.k1_hi[:, i - G1, INNER]
                            fn(to, bank[:, z.b + i, 0:TP], ACT.Copy).then_inc(z.s["qk_hi"], 1)
                            yield
                        for i in range(2):
                            act.wait_ge(z.s["v_psum"], FULL["v_psum"] + i + 1)
                            for u in range(NT):
                                n = fn(z.V1_hi[:, NT * i + u, :, 0:D1],
                                       bank[0:KC, z.b + i, tile(u)].rearrange("p (a d) -> p a d", a=H1), ACT.Copy)
                            n.then_inc(z.s["v_hi"], 1)
                            yield

                    def bmax(z):
                        for t in range(NT + 1):
                            yield

                    def bheads(z):
                        for t in range(NT):
                            for u in range(4 * t, 4 * t + 4):
                                act.wait_ge(z.s["st_psum"], FULL["st_psum"] + u + 1)
                                if u >= 2:
                                    act.wait_ge(z.s["p_lo"], FULL["p_lo"] + sum(x % 4 != 3 for x in range(u - 1)))
                                    if u >= 5:
                                        act.wait_ge(z.s["p_lo_pool"], FULL["p_lo_pool"] + sum(x % 4 == 3 for x in range(u - 1)))
                                fn(z.P1f[:, u % 2, :], bank[0:KC, z.b + u % 3, :], ACT.Exp, scale=D1 ** -0.5)\
                                    .then_inc(z.s["exp_done"], 1)
                            yield
                        yield

                    def bout(z):
                        act.wait_ge(z.s["oT_psum"], FULL["oT_psum"] + 1)
                        fn(z.O1T_hi, bank[:, z.b, 0:TP], ACT.Copy).then_inc(z.s["oT_hi"], 1)
                        yield
                        yield

                    def cproj(z):
                        for t in range(NT):
                            act.wait_ge(z.s["v_psum"], SLID["v_psum"] + t + 1)
                            fn(z.sq[:, t, :], bank[:, z.b + t, 0:2 * C], ACT.Square).then_inc(z.s["csq"], 1)
                            fn(z.V_hi[:, t, 0:H2, 0:D2], bank[:, z.b + t, 2 * C:3 * C].rearrange("p (a d) -> p a d", a=H2),
                               ACT.Copy).then_inc(z.s["v_hi"], 1)
                        yield
                        yield
                        for which in range(2):
                            act.wait_ge(z.s["cqkT_psum"], which + 1)
                            for a in range(H2):
                                fn((z.KS if which else z.QS)[0:D2, a, :],
                                   bank[D2 * a:D2 * a + D2, z.b + (0 if which else 3), 0:TP], ACT.Copy)\
                                    .then_inc(z.s["qk_hi"], 1)
                        yield

                    def cmax(z):
                        yield
                        act.wait_ge(z.s["maxT_psum"], SLID["maxT_psum"] + 1)
                        fn(z.QB[D2:D2 + H2, 0:H2, :], bank[0:H2, z.b, 0:TP].unsqueeze(1).to_broadcast([H2, H2, TP]),
                           ACT.Copy, scale=-1.0).then_inc(z.s["negmax_ready"], 1)
                        yield

                    def cheads(z):
                        for i in range(H2):
                            for k in range(NT):
                                act.wait_ge(z.s["st_psum"], SLID["st_psum"] + NT * i + k + 1)
                                if i:
                                    act.wait_ge(z.s["p_lo"], SLID["p_lo"] + k + 1)
                                fn(z.Pf[:, k, P * k:TP], bank[:, z.b + k, P * k:TP], ACT.Exp, scale=float(D2) ** 0.5)\
                                    .then_inc(z.s["exp_done"], 1)
                            yield
                        yield
                        yield

                    def cout(z):
                        act.wait_ge(z.s["oT_psum"], SLID["oT_psum"] + 1)
                        fn(z.OT_hi[:, 0, :], bank[:, z.b, 0:TP], ACT.Copy).then_inc(z.s["oT_hi"], 1)
                        yield
                        act.wait_ge(z.s["y_psum"], 1)
                        fn(z.hT_hi[:, INNER], bank[:, z.b + 1, 0:TP], ACT.Copy).then_inc(z.s["y_hi"], 1)
                        yield

                    side_by_side({"tdnn": tdnn, "norm0": norm(0), "norm1": norm(1), "norm2": norm(2), "norm3": norm(3),
                                  "qkv": qkv, "maxima": maxima, "heads": heads, "out0": out0, "experts0": experts(0),
                                  "bproj": bproj, "bmax": bmax, "bheads": bheads, "bout": bout, "cproj": cproj,
                                  "cmax": cmax, "cheads": cheads, "cout": cout, "experts1": experts(1)}, runs, turns)

                @block.vector
                def _(dve):
                    v = nc.vector
                    def link(z, i):
                        z.steps += 1
                        i.then_inc(z.s["vector_step"], 1)
                        dve.wait_ge(z.s["vector_step"], z.steps)

                    def lower(to, x, high):
                        return v.tensor_tensor(to, x, high, ALU.subtract)

                    def rsqrt(z, x, n):
                        y, other = z.guess[:, 0:n], z.rstd[:, 0:n]
                        link(z, v.tensor_scalar(y.bitcast(I32), x.bitcast(I32), -0.5, 1597463007.0, ALU.mult, ALU.add))
                        for _ in range(3):
                            link(z, v.scalar_tensor_tensor(z.n1[:, 0:n], y, -0.5, y, ALU.mult, ALU.mult))
                            link(z, v.tensor_tensor(z.n2[:, 0:n], z.n1[:, 0:n], x, ALU.mult))
                            link(z, v.scalar_tensor_tensor(other, z.n2[:, 0:n], 1.5, y, ALU.add, ALU.mult))
                            y, other = other, y

                    def tdnn(z):
                        dve.wait_ge(z.s["x_hi"], 1)
                        lower(z.xT_lo[:, 0:T_IN], z.xf[:, 0:T_IN], z.xT_hi[:, 0:T_IN]).then_inc(z.s["x_lo"], 1)
                        yield
                        yield
                        yield

                    def norm(k):
                        def stage(z):
                            if k == 0:
                                dve.wait_ge(z.s["h_ready"], 1)
                            for t in range(NT):
                                i = v.bn_stats(z.stats[:, t, :], z.h[:, t, :])
                            link(z, i)
                            for t in range(NT):
                                i = v.bn_aggr(z.mv[:, t, :], z.stats[:, t, :])
                            link(z, i)
                            link(z, v.tensor_scalar(z.ve[:, 0:NT], z.mv[:, :, 1], 1e-5, None, ALU.add))
                            rsqrt(z, z.ve[:, 0:NT], NT)
                            for t in range(NT):
                                if k < 3:
                                    i = v.tensor_scalar(z.hn[:, t, :], z.h[:, t, :], z.mv[:, t, 0:1], z.rstd[:, t:t + 1],
                                                        ALU.subtract, ALU.mult)
                                else:
                                    i = v.scalar_tensor_tensor(z.hn[:, t, :], z.h[:, t, :], z.mv[:, t, 0:1], res["lng"][:],
                                                               ALU.subtract, ALU.mult)
                            if k == 3:
                                link(z, i)
                                for t in range(NT):
                                    i = v.scalar_tensor_tensor(z.hn[:, t, :], z.hn[:, t, :], z.rstd[:, t:t + 1],
                                                               res["lnb"][:], ALU.mult, ALU.add)
                            i.then_inc(z.s["hn_ready"], 1)
                            if k == 0:
                                dve.wait_ge(z.s["hn_ready"], 1)
                                link(z, v.tensor_tensor(z.h[:], z.h[:], z.hn[:], ALU.add))
                            yield
                            dve.wait_ge(z.s["hnT_psum"], k + 1)
                            dve.wait_ge(z.s["hnT_hi"], k + 1)
                            lower(z.hT_lo[:, INNER], bank[:, z.b + 1, 0:TP], z.hT_hi[:, INNER]).then_inc(z.s["hnT_lo"], 1)
                            yield
                        return stage

                    def add_to_h(z, b):
                        link(z, v.tensor_tensor(z.h[:], tiles(bank[:, z.b + b, 0:TP]), z.h[:], ALU.add))

                    def qkv(z):
                        s = z.s
                        for i in range(H0):
                            for a in range(2):
                                hd = 2 * (i // 2) + a
                                dve.wait_ge(s["qk_hi"], 2 * i + a + 1)
                                to = z.KB[0:D0, hd, :] if i % 2 else z.QS[D0:, hd, :]
                                lower(to, bank[D0 * a:D0 * a + D0, z.b + i % 4, 0:TP], (z.KS if i % 2 else z.QS)[0:D0, hd, :])\
                                    .then_inc(s["qk_lo"], 1)
                            yield
                        for t in range(NT):
                            dve.wait_ge(s["v_hi"], t + 1)
                            lower(z.V_lo[:, t, :, 0:D0], bank[:, z.b + t, :].rearrange("p (a d) -> p a d", a=H0),
                                  z.V_hi[:, t, :, 0:D0]).then_inc(s["v_lo"], 1)
                            yield

                    def maxima(z):
                        for i in range(H0 * NT // 2):
                            dve.wait_ge(z.s["smax_psum"], i + 1)
                            b = z.b + 2 * (i % 2)
                            v.tensor_reduce(z.Mx[:, 2 * i:2 * i + 2], bank[:, b:b + 2, 0:T], AX, ALU.max)\
                                .then_inc(z.s["max_done"], 1)
                            yield
                        yield

                    def normalise(z, to, b, n, d, sem):
                        x = bank[:, b, 0:n * (d + 1)].rearrange("p (a d) -> p a d", a=n)
                        link(z, v.reciprocal(z.rec[:, 0:n], x[:, :, d]))
                        v.tensor_tensor(to, x[:, :, 0:d], z.rec[:, 0:n].unsqueeze(2).to_broadcast([P, n, d]), ALU.mult)\
                            .then_inc(sem, 1)

                    def heads(z):
                        s = z.s
                        for i in range(H0 + 2):
                            if i < H0:
                                if i >= 2:
                                    dve.wait_ge(s["pv_psum"], i - 1)
                                for t in range(NT):
                                    dve.wait_ge(s["exp_done"], NT * i + t + 1)
                                    v.tensor_copy(z.P_hi[:, i % 2, t, :], z.Pf[:, t, :]).then_inc(s["p_hi"], 1)
                                    if t == 1:
                                        dve.wait_ge(s["p_hi"], NT * i + t)
                                        lower(z.P_lo[:, i % 2, t - 1, :], z.Pf[:, t - 1, :], z.P_hi[:, i % 2, t - 1, :])\
                                            .then_inc(s["p_lo"], 1)
                            if i >= 2:
                                hd = i - 2
                                dve.wait_ge(s["pv_psum"], hd + 1)
                                if hd:
                                    dve.wait_ge(s["o_norm"], hd)
                                normalise(z, z.O[:, :, hd, :], z.b + 3, NT, D0, s["o_norm"])
                            yield

                    def out0(z):
                        s = z.s
                        for c in range(4):
                            dve.wait_ge(s["oT_hi"], c + 1)
                            lower(z.OT_lo[:, c, :], bank[:, z.b + c, 0:TP], z.OT_hi[:, c, :]).then_inc(s["oT_lo"], 1)
                            yield
                        yield
                        dve.wait_ge(s["attn_psum"], 1)
                        add_to_h(z, 0)
                        yield

                    def experts(f):
                        def per_tile(x):
                            return x[:].unsqueeze(2).to_broadcast([P, NT, E])

                        def split(z, e):
                            n = E * f + e
                            if e >= 2:
                                dve.wait_ge(z.s["down_psum"], n - 1)
                            for c in range(FC):
                                dve.wait_ge(z.s["gelu_done"], FC * n + c + 1)
                                v.tensor_copy(z.H_hi[:, e % 2, c, :], z.Hf[:, c, :]).then_inc(z.s["hid_hi"], 1)
                                if c == 1:
                                    dve.wait_ge(z.s["hid_hi"], FC * n + c)
                                    lower(z.H_lo[:, e % 2, c - 1, :], z.Hf[:, c - 1, :], z.H_hi[:, e % 2, c - 1, :])\
                                        .then_inc(z.s["hid_lo"], 1)

                        def gates(z):
                            s = z.s
                            dve.wait_ge(s["logits_psum"], f + 1)
                            lg = bank[:, z.b + 3, 0:NT * E].rearrange("p (t e) -> p t e", t=NT)
                            link(z, v.tensor_reduce(z.gm[:], lg, AX, ALU.max))
                            v.tensor_tensor(z.lm[:], lg, per_tile(z.gm), ALU.subtract).then_inc(s["logits_shift"], 1)
                            dve.wait_ge(s["gate_exp"], f + 1)
                            link(z, v.tensor_reduce(z.gs[:], z.ge[:], AX, ALU.add))
                            link(z, v.reciprocal(z.gr[:], z.gs[:]))
                            if f == 0:
                                link(z, v.scalar_tensor_tensor(z.ga[:], z.lm[:], 0.0, res["c_rank"][:], ALU.is_equal, ALU.mult))
                                link(z, v.tensor_reduce(z.gb[:], z.ga[:], AX, ALU.max))
                                link(z, v.tensor_tensor(z.ga[:], z.ga[:], per_tile(z.gb), ALU.is_equal))
                                v.tensor_tensor(z.gate[:], z.ga[:], per_tile(z.gr), ALU.mult).then_inc(s["gate_ready"], 1)
                            else:
                                v.tensor_tensor(z.gate[:], z.ge[:], per_tile(z.gr), ALU.mult).then_inc(s["gate_ready"], 1)

                        def stage(z):
                            s = z.s
                            base = (E + 1) * f
                            gates(z)
                            split(z, 0)
                            yield
                            for e in range(E):
                                if e + 1 < E:
                                    split(z, e + 1)
                                if e == 0:
                                    dve.wait_ge(s["b2_psum"], f + 1)
                                    v.tensor_tensor(z.h[:], tiles(bank[:, z.b + 3, 0:TP]), z.h[:], ALU.add)\
                                        .then_inc(s["acc_done"], 1)
                                dve.wait_ge(s["down_psum"], E * f + e + 1)
                                dve.wait_ge(s["acc_done"], base + e + 1)
                                for t in range(NT):
                                    i = v.scalar_tensor_tensor(z.h[:, t, :], bank[:, z.b + 3, tile(t)], z.gate[:, t, e:e + 1],
                                                               z.h[:, t, :], ALU.mult, ALU.add)
                                i.then_inc(s["acc_done"], 1)
                                yield
                            dve.wait_ge(s["acc_done"], base + E + 1)
                        return stage

                    def bproj(z):
                        s = z.s
                        rows = res["c_rows"]
                        for i in range(4):
                            dve.wait_ge(s["qk_hi"], FULL["qk_hi"] + i + 1)
                            x = bank[:, z.b + i, 0:TP]
                            if i < G1:
                                v.scalar_tensor_tensor(z.q1_st[:, i, :], z.q1_hi[:, i, :], rows[:, 0:1], x, ALU.mult,
                                                       ALU.add).then_inc(s["qk_lo"], 1)
                            else:
                                lower(z.k1_d[:, i - G1, :], x, z.k1_hi[:, i - G1, INNER]).then_inc(s["qk_lo"], 1)
                            yield
                        dve.wait_ge(s["qk_lo"], FULL["qk_lo"] + 4)
                        v.tensor_scalar(z.k1_lo[:, :, INNER], z.k1_d[:], rows[:, 1:2], rows[:, 2:3], ALU.mult, ALU.add)
                        for j in range(J1):
                            v.tensor_scalar(z.qz_st[:, :, j, :], z.q1_st[:], res["c_heads"][:, j:j + 1], None, ALU.mult)
                            i = v.tensor_scalar(z.qz_hi[:, :, j, :], z.q1_hi[:], res["c_heads"][:, j:j + 1], rows[:, 1:2],
                                                ALU.mult, ALU.mult)
                        i.then_inc(s["bqz_ready"], 1)
                        for i in range(2):
                            dve.wait_ge(s["v_hi"], FULL["v_hi"] + i + 1)
                            for u in range(NT):
                                n = lower(z.V1_lo[:, NT * i + u, :, 0:D1],
                                          bank[0:KC, z.b + i, tile(u)].rearrange("p (a d) -> p a d", a=H1),
                                          z.V1_hi[:, NT * i + u, :, 0:D1])
                            n.then_inc(s["v_lo"], 1)
                            yield

                    def bmax(z):
                        s = z.s
                        dve.wait_ge(s["margins_set"], 1)
                        for t in range(NT):
                            for pair in range(4):
                                u = 4 * t + pair
                                dve.wait_ge(s["smax_psum"], FULL["smax_psum"] + u + 1)
                                g, j = divmod(2 * pair, J1)
                                v.tensor_reduce(z.Mexp[:, t, g, 32 * j + M_ROW:32 * j + M_ROW + 33:32],
                                                bank[:, z.b + (u + 2) % 4, 0:2 * WIN].rearrange("p (a n) -> p a n", a=2),
                                                AX, ALU.max).then_inc(s["max_done"], 1)
                            yield
                        dve.wait_ge(s["maxT_psum"], FULL["maxT_psum"] + 1)
                        link(z, v.scalar_tensor_tensor(z.q1_m[:], z.q1_hi[:], res["c_rows"][:, 1:2],
                                                       bank[:, z.b:z.b + G1, 0:TP], ALU.mult, ALU.subtract))
                        for j in range(J1):
                            i = v.tensor_scalar(z.qz_m[:, :, j, :], z.q1_m[:], res["c_heads"][:, j:j + 1], None, ALU.mult)
                        i.then_inc(s["bq2_ready"], 1)
                        yield

                    def bheads(z):
                        s = z.s
                        for t in range(NT + 1):
                            if t < NT:
                                for u in range(4 * t, 4 * t + 4):
                                    dve.wait_ge(s["exp_done"], FULL["exp_done"] + u + 1)
                                    if u >= RING:
                                        dve.wait_ge(s["pv_psum"], FULL["pv_psum"] + (u - RING) // 4 + 1)
                                    v.tensor_copy(z.P1_hi[:, u % RING, :], z.P1f[:, u % 2, :]).then_inc(s["p_hi"], 1)
                                    if u % 4 != 3:
                                        dve.wait_ge(s["p_hi"], FULL["p_hi"] + u + 1)
                                        lower(z.P1_lo[:, u % RING, :], z.P1f[:, u % 2, :], z.P1_hi[:, u % RING, :])\
                                            .then_inc(s["p_lo"], 1)
                            if t:
                                dve.wait_ge(s["pv_psum"], FULL["pv_psum"] + t)
                                if t > 1:
                                    dve.wait_ge(s["o_norm"], FULL["o_norm"] + t - 1)
                                normalise(z, z.O1[:, t - 1, :, :], z.b + 3, H1, D1, s["o_norm"])
                            yield

                    def bout(z):
                        dve.wait_ge(z.s["oT_hi"], FULL["oT_hi"] + 1)
                        lower(z.O1T_lo, bank[:, z.b, 0:TP], z.O1T_hi).then_inc(z.s["oT_lo"], 1)
                        yield
                        dve.wait_ge(z.s["attn_psum"], FULL["attn_psum"] + 1)
                        add_to_h(z, 1)
                        yield

                    def cproj(z):
                        s = z.s
                        yield
                        for t in range(NT):
                            dve.wait_ge(s["v_hi"], SLID["v_hi"] + t + 1)
                            lower(z.V_lo[:, t, 0:H2, 0:D2], bank[:, z.b + t, 2 * C:3 * C].rearrange("p (a d) -> p a d", a=H2),
                                  z.V_hi[:, t, 0:H2, 0:D2]).then_inc(s["v_lo"], 1)
                        dve.wait_ge(s["csq"], NT)
                        link(z, v.tensor_reduce(z.ve[:], z.sq.rearrange("p t (a d) -> p (t a) d", a=4), AX, ALU.add))
                        link(z, v.tensor_scalar(z.ve[:], z.ve[:], 1e-12, None, ALU.add))
                        rsqrt(z, z.ve[:], 4 * NT)
                        for t in range(NT):
                            for a in range(4):
                                i = v.scalar_tensor_tensor(z.qk[:, t, a, :], bank[:, z.b + t, D2 * a:D2 * a + D2],
                                                           z.rstd[:, 4 * t + a:4 * t + a + 1], res["qkg"][:, a, :],
                                                           ALU.mult, ALU.mult)
                        i.then_inc(s["cqk_ready"], 1)
                        yield
                        for which in range(2):
                            for a in range(H2):
                                dve.wait_ge(s["qk_hi"], SLID["qk_hi"] + 2 * which + a + 1)
                                to = z.KB[0:D2, a, :] if which else z.QS[D2:, a, :]
                                lower(to, bank[D2 * a:D2 * a + D2, z.b + (0 if which else 3), 0:TP],
                                      (z.KS if which else z.QS)[0:D2, a, :]).then_inc(s["qk_lo"], 1)
                        yield

                    def cmax(z):
                        for u in range(H2 * NT):
                            dve.wait_ge(z.s["smax_psum"], SLID["smax_psum"] + u + 1)
                            v.tensor_reduce(z.Mx[:, u:u + 1], bank[:, z.b + (u + 1) % 4, 0:P * (u % NT + 1)], AX, ALU.max)\
                                .then_inc(z.s["max_done"], 1)
                        yield
                        yield

                    def cheads(z):
                        s = z.s
                        for hd in range(H2):
                            for k in range(NT):
                                dve.wait_ge(s["exp_done"], SLID["exp_done"] + NT * hd + k + 1)
                                link(z, v.tensor_copy(z.P_hi[:, hd, k, P * k:TP], z.Pf[:, k, P * k:TP]))
                                lower(z.P_lo[:, hd, k, P * k:TP], z.Pf[:, k, P * k:TP], z.P_hi[:, hd, k, P * k:TP])\
                                    .then_inc(s["p_lo"], 1)
                            yield
                        for hd in range(H2):
                            dve.wait_ge(s["pv_psum"], SLID["pv_psum"] + hd + 1)
                            if hd:
                                dve.wait_ge(s["o_norm"], SLID["o_norm"] + hd)
                            normalise(z, z.O[:, :, hd, :], z.b + 3, NT, D2, s["o_norm"])
                            yield

                    def cout(z):
                        dve.wait_ge(z.s["oT_hi"], SLID["oT_hi"] + 1)
                        lower(z.OT_lo[:, 0, :], bank[:, z.b, 0:TP], z.OT_hi[:, 0, :]).then_inc(z.s["oT_lo"], 1)
                        yield
                        dve.wait_ge(z.s["y_hi"], 1)
                        lower(z.hT_lo[:, INNER], bank[:, z.b + 1, 0:TP], z.hT_hi[:, INNER]).then_inc(z.s["y_lo"], 1)
                        yield

                    side_by_side({"tdnn": tdnn, "norm0": norm(0), "norm1": norm(1), "norm2": norm(2), "norm3": norm(3),
                                  "qkv": qkv, "maxima": maxima, "heads": heads, "out0": out0, "experts0": experts(0),
                                  "bproj": bproj, "bmax": bmax, "bheads": bheads, "bout": bout, "cproj": cproj,
                                  "cmax": cmax, "cheads": cheads, "cout": cout, "experts1": experts(1)}, runs, turns)

                @block.gpsimd
                def _(pool):
                    g = nc.gpsimd

                    def heads(z):
                        for hd in range(H0):
                            for t in (1, 2):
                                pool.wait_ge(z.s["p_hi"], NT * hd + t + 1)
                                if hd >= 2:
                                    pool.wait_ge(z.s["pv_psum"], hd - 1)
                                g.tensor_tensor(z.P_lo[:, hd % 2, t, :], z.Pf[:, t, :], z.P_hi[:, hd % 2, t, :],
                                                ALU.subtract).then_inc(z.s["p_lo_pool"], 1)
                            yield
                        yield
                        yield

                    def experts(f):
                        def split(z, e):
                            n = E * f + e
                            for c in range(1, FC):
                                pool.wait_ge(z.s["hid_hi"], FC * n + c + 1)
                                g.tensor_tensor(z.H_lo[:, e % 2, c, :], z.Hf[:, c, :], z.H_hi[:, e % 2, c, :], ALU.subtract)\
                                    .then_inc(z.s["hid_lo_pool"], 1)

                        def stage(z):
                            for e in range(E):
                                split(z, e)
                                yield
                            yield
                        return stage

                    def bproj(z):
                        pool.wait_ge(z.s["hn_ready"], 3)
                        for x in (z.k1_hi, z.k1_lo):
                            g.memset(x[:, :, 0:HALF], 0.0)
                            g.memset(x[:, :, HALF + TP:], 0.0)
                        g.memset(z.V1_lo[:, :, :, D1:], 0.0)
                        g.memset(z.V1_hi[:, :, :, D1:], 1.0)
                        g.memset(z.Mexp[:], 0.0).then_inc(z.s["margins_set"], 1)
                        for _ in range(PIECES["bproj"]):
                            yield

                    def bheads(z):
                        for t in range(NT):
                            u = 4 * t + 3
                            pool.wait_ge(z.s["p_hi"], FULL["p_hi"] + u + 1)
                            g.tensor_tensor(z.P1_lo[:, u % RING, :], z.P1f[:, u % 2, :], z.P1_hi[:, u % RING, :], ALU.subtract)\
                                .then_inc(z.s["p_lo_pool"], 1)
                            yield
                        yield

                    stages = {n: nothing(k) for n, k in PIECES.items()}
                    stages.update({"heads": heads, "experts0": experts(0), "experts1": experts(1),
                                   "bproj": bproj, "bheads": bheads})
                    side_by_side(stages, runs, turns)

            nc.all_engine_barrier()
            done = [run.slot for run in runs if run.names[-1] == STAGES[-1]]
            for z in done:
                z.steps = 0
                nc.gpsimd.sem_clear(z.sem_range)
            if done:
                nc.all_engine_barrier()

        z0, z1 = slots
        segment(Run(z0, EARLY0, 0, after=2))
        segment(Run(z0, LATE0, 0, after=2), Run(z1, EARLY1, 1, after=3))
        with nc.Fori(0, B - 3, 2) as seq:
            segment(Run(z0, EARLY0, seq + 2, before=seq, after=(seq + 4) % B), Run(z1, LATE1, seq + 1, after=seq + 3))
            segment(Run(z0, LATE0, seq + 2, after=(seq + 4) % B), Run(z1, EARLY1, seq + 3, before=seq + 1, after=(seq + 5) % B))
        segment(Run(z1, LATE1, B - 1), leaving=(z0, B - 2))


def layout(i):
    f = {k: np.asarray(v) for k, v in i.items()}
    a = np.ascontiguousarray

    def twice(b):
        return a(np.broadcast_to(b.reshape(1, -1), (2, b.size)))

    def chunks(m, n):
        return a(m.reshape(n, P, m.shape[-1]).transpose(1, 0, 2))

    w = {"x": a(f["x"].transpose(0, 2, 1)),
         "tokW": chunks(f["L0_tok_W"].T, TAPS), "tokb": twice(f["L0_tok_b"]),
         "Wq": a(f["L0_attn_Wq"].T), "Wk": a(f["L0_attn_Wk"].T), "Wv": a(f["L0_attn_Wv"].T),
         "Wo": chunks(f["L0_attn_Wo"].T, 4)}
    for pre, src, wg, bg in (("m0_", "L0_ffn_", "Ws", "bs"), ("m1_", "L1_ffn_", "gate_W", "gate_b")):
        w[pre + "Wg"] = a(f[src + wg])
        w[pre + "bg"] = twice(f[src + bg])
        w[pre + "W1"] = a(f[src + "W1"].transpose(1, 0, 2))
        w[pre + "b1"] = a(f[src + "b1"].reshape(E, FC, P).transpose(2, 0, 1))
        w[pre + "W2"] = a(f[src + "W2"].reshape(E, FC, P, C).transpose(2, 0, 1, 3))
        w[pre + "b2"] = a(f[src + "b2"])
    wqkv, bqkv = f["L1_attn_W_qkv"], f["L1_attn_b_qkv"]
    bias = np.zeros((2, G1 * P), np.float32)
    for k, name in enumerate(("Wq1", "Wk1")):
        m = wqkv[:, C * k:C * k + C].reshape(P, G1, J1, 1, D1)
        w[name] = a(np.broadcast_to(m, (P, G1, J1, 2, D1)).reshape(P, G1, P))
        b = bqkv[C * k:C * k + C].reshape(G1, J1, 1, D1)
        bias[k] = np.broadcast_to(b, (G1, J1, 2, D1)).reshape(G1 * P)
    w["bqk1"] = twice(bias)
    w["Wv1"] = a(wqkv[:, 2 * C:])
    w["bv1"] = twice(bqkv[2 * C:])
    w["Wp1"] = a(f["L1_attn_W_proj"])
    w["bp1"] = twice(f["L1_attn_b_proj"])
    w["lng"] = a(np.broadcast_to(f["L1_ffn_ln_g"], (P, C)))
    w["lnb"] = a(np.broadcast_to(f["L1_ffn_ln_b"], (P, C)))
    w["Wqkv2"] = a(np.concatenate([f["L1_ffn_Wq"], f["L1_ffn_Wk"], f["L1_ffn_Wv"]], 1))
    w["Wo2"] = a(f["L1_ffn_Wo"])
    g = np.stack([f["L1_ffn_qn_g"]] * H2 + [f["L1_ffn_kn_g"]] * H2)
    w["qkg"] = a(np.broadcast_to(g, (P, 2 * H2, D2)))
    return w


def kernel(**inputs):
    import concourse.bacc as _bacc
    from concourse.bass_utils import run_bass_kernel_spmd as _run

    nc = _bacc.Bacc("TRN2", target_bir_lowering=False, num_devices=1)
    arrays = {**layout(inputs), **constants()}
    aps = {n: nc.dram_tensor(f"in_{n}", a.shape, mybir.dt.from_np(a.dtype), kind="ExternalInput").ap()
           for n, a in arrays.items()}
    out = nc.dram_tensor("out_0", (B, T, C), F32, kind="ExternalOutput").ap()
    tower(nc, aps, out)
    r = _run(nc, [{f"in_{n}": a for n, a in arrays.items()}], core_ids=[0])
    return r.results[0]["out_0"]
```
